# Optimizing a Trainium2 kernel written in Bass

```python
import numpy as np
import jax
import jax.numpy as jnp

def _softmax(x, axis=-1):
    return jax.nn.softmax(x, axis=axis)

def _gelu(x):
    return jax.nn.gelu(x, approximate=True)

def _silu(x):
    return jax.nn.silu(x)

def _sigmoid(x):
    return jax.nn.sigmoid(x)

def _layernorm(x, axis=-1, eps=1e-05):
    m = jnp.mean(x, axis=axis, keepdims=True)
    v = jnp.var(x, axis=axis, keepdims=True)
    return (x - m) / jnp.sqrt(v + eps)

def _scatter_add(tgt, idx, src, axis=0):
    return tgt.at[idx].add(src)

def _segment_sum(src, seg, n):
    return jax.ops.segment_sum(src, seg, n)
kernel_name = 'mk_flamingo_gated_d2_seqx_r8_e2e314'

def setup_inputs(seed: int=0):
    np.random.seed(seed)
    _w = jnp.asarray

    def _rec_inputs():
        import jax
        import jax.numpy as jnp
        _rk = jax.random.key(seed)
        x = -0.0003929 + 0.9999 * jax.random.normal(jax.random.fold_in(_rk, 1), (32, 100, 128), jnp.float32)
        _lenS = 100 - jax.random.randint(jax.random.fold_in(_rk, 7), (32,), 0, max(1, 100 // 4) + 1, jnp.int32)
        _lenS2 = 1444 - jax.random.randint(jax.random.fold_in(_rk, 8), (32,), 0, max(1, 1444 // 4) + 1, jnp.int32)
        _ctx_768P = jax.random.normal(jax.random.fold_in(_rk, 11), (32, 16, 96), jnp.float32)
        _ctx_768c = jax.random.dirichlet(jax.random.fold_in(_rk, 511), 0.3 * jnp.ones((16,), jnp.float32), (32, 1444))
        _ctx_768t = jnp.einsum('bsk,bkd->bsd', _ctx_768c, _ctx_768P)
        _ctx_768t = _ctx_768t * jax.lax.rsqrt(jnp.mean(jnp.square(_ctx_768t)) + 1e-12) * 0.953939
        ctx_768 = 2.09791e-05 + 1.00001 * (_ctx_768t + 0.3 * jax.random.normal(jax.random.fold_in(_rk, 611), (32, 1444, 96), jnp.float32))
        _g = jax.random.normal(jax.random.fold_in(_rk, 9001), (2, 2), jnp.float32)
        _g = jnp.sign(_g) * jnp.maximum(jnp.abs(_g), 1.0) + (_g == 0) * 1.0
        g_xattn = _g[0]
        g_ffn = _g[1]
        return (x, ctx_768, g_xattn, g_ffn)
    x, ctx_768, g_xattn, g_ffn = _rec_inputs()

    def _L0_xattn_setup():
        import jax, jax.numpy as jnp
        import numpy as np
        QUERY_DIM = 128
        KEY_DIM = 96
        NUM_HEADS = 16
        HEAD_DIM = QUERY_DIM // NUM_HEADS
        SCALE = HEAD_DIM ** (-0.5)
        key = jax.random.key(seed)
        ks = jax.random.split(key, 11)
        B, Nq, Nk = (4, 512, 128)
        s_q = QUERY_DIM ** (-0.5)
        s_k = KEY_DIM ** (-0.5)
        return {'query': jax.random.normal(ks[0], (B, Nq, QUERY_DIM), jnp.float32), 'key': jax.random.normal(ks[1], (B, Nk, KEY_DIM), jnp.float32), 'value': jax.random.normal(ks[2], (B, Nk, KEY_DIM), jnp.float32), 'Wq': jax.random.normal(ks[3], (QUERY_DIM, QUERY_DIM), jnp.float32) * s_q, 'bq': jnp.zeros((QUERY_DIM,), jnp.float32), 'Wk': jax.random.normal(ks[4], (KEY_DIM, QUERY_DIM), jnp.float32) * s_k, 'bk': jnp.zeros((QUERY_DIM,), jnp.float32), 'Wv': jax.random.normal(ks[5], (KEY_DIM, QUERY_DIM), jnp.float32) * s_k, 'bv': jnp.zeros((QUERY_DIM,), jnp.float32), 'Wo': jax.random.normal(ks[6], (QUERY_DIM, QUERY_DIM), jnp.float32) * s_q, 'bo': jnp.zeros((QUERY_DIM,), jnp.float32)}
    _L0_xattn_all = _L0_xattn_setup()
    _L0_xattn_in = {k: v for k, v in _L0_xattn_all.items() if k in ('Wq', 'bq', 'Wk', 'bk', 'Wv', 'bv', 'Wo', 'bo')}
    del _L0_xattn_all

    def _L0_ffn_setup():
        import jax, jax.numpy as jnp
        import numpy as np
        HIDDEN = 128
        HEAD_DIM = 64
        N_EXPERTS = 16
        MIN_EXPERTS = 2
        B, T = (4, 256)

        def _normalize(x, axis):
            n = jnp.sqrt(jnp.sum(x * x, axis=axis, keepdims=True))
            return x / jnp.maximum(n, 1e-12)

        def _ste(x):
            hard = jax.lax.stop_gradient((x > 0).astype(x.dtype))
            return hard + x - jax.lax.stop_gradient(x)

        def _gating(hidden_states, sim_matrix, gates):
            b, t, c = hidden_states.shape
            flat = hidden_states.reshape(b * t, c)
            logits = _normalize(flat, -1) @ _normalize(sim_matrix, 0) - jax.nn.sigmoid(gates)
            gated = jax.nn.relu(logits)
            mask = _ste(gated)
            inactive = jnp.sum(mask, axis=1) == 0
            _, fb_idx = jax.lax.top_k(logits, MIN_EXPERTS)
            fb = jnp.zeros_like(mask).at[jnp.arange(b * t)[:, None], fb_idx].set(1.0)
            fb_applied = inactive[:, None] & (fb > 0)
            mask = jnp.where(fb_applied, 1.0, mask)
            masked_logits = jnp.where(mask > 0, gated, -jnp.inf)
            return jax.nn.softmax(masked_logits, axis=-1).reshape(b, t, -1)
        key = jax.random.key(seed)
        ks = jax.random.split(key, 6)
        xav_qkv = float(np.sqrt(6.0 / (HIDDEN + HEAD_DIM)))
        return {'hidden_states': jax.random.normal(ks[0], (B, T, HIDDEN), dtype=jnp.float32), 'sim_matrix': jax.random.normal(ks[1], (HIDDEN, N_EXPERTS), dtype=jnp.float32), 'gates': jnp.zeros((N_EXPERTS,), dtype=jnp.float32), 'q_proj': jax.random.uniform(ks[2], (N_EXPERTS, HIDDEN, HEAD_DIM), jnp.float32, -xav_qkv, xav_qkv), 'k_proj': jax.random.uniform(ks[3], (N_EXPERTS, HIDDEN, HEAD_DIM), jnp.float32, -xav_qkv, xav_qkv), 'v_proj': jax.random.uniform(ks[4], (N_EXPERTS, HIDDEN, HEAD_DIM), jnp.float32, -xav_qkv, xav_qkv), 'o_proj': jax.random.uniform(ks[5], (N_EXPERTS, HEAD_DIM, HIDDEN), jnp.float32, -xav_qkv, xav_qkv)}
    _L0_ffn_all = _L0_ffn_setup()
    _L0_ffn_in = {k: v for k, v in _L0_ffn_all.items() if k in ('sim_matrix', 'gates', 'q_proj', 'k_proj', 'v_proj', 'o_proj')}
    del _L0_ffn_all

    def _L1_xattn_setup():
        import jax, jax.numpy as jnp
        import numpy as np
        NUM_HEADS = 16
        key = jax.random.key(seed)
        ks = jax.random.split(key, 8)
        dim, cond_dim = (128, 96)
        B, N, condN = (4, 256, 128)
        s = lambda k, shp, fan: jax.random.normal(k, shp, dtype=jnp.float32) * fan ** (-0.5)
        return {'x': jax.random.normal(ks[0], (B, N, dim), dtype=jnp.float32), 'cond': jax.random.normal(ks[1], (B, condN, cond_dim), dtype=jnp.float32), 'q_w': s(ks[2], (dim, dim), dim), 'q_b': jnp.zeros((dim,), jnp.float32), 'kv_w': s(ks[3], (cond_dim, 2 * dim), cond_dim), 'kv_b': jnp.zeros((2 * dim,), jnp.float32), 'proj_w': s(ks[4], (dim, dim), dim), 'proj_b': jnp.zeros((dim,), jnp.float32)}
    _L1_xattn_all = _L1_xattn_setup()
    _L1_xattn_in = {k: v for k, v in _L1_xattn_all.items() if k in ('q_w', 'q_b', 'kv_w', 'kv_b', 'proj_w', 'proj_b')}
    del _L1_xattn_all

    def _L1_ffn_setup():
        import jax, jax.numpy as jnp
        import numpy as np
        B, S, D, F, E, K = (4, 256, 128, 512, 8, 2)
        FS = 128
        LN_EPS = 1e-05

        def _swiglu(x, gu_w, dn_w):
            gate, up = jnp.split(x @ gu_w, 2, axis=-1)
            gate = jnp.clip(gate, -10.0, 10.0)
            return jax.nn.silu(gate) * up @ dn_w
        key = jax.random.key(seed)
        ks = jax.random.split(key, 6)
        s = 0.02
        return {'x': jax.random.normal(ks[0], (B, S, D), jnp.float32), 'ln_gamma': jnp.ones((D,), jnp.float32), 'ln_beta': jnp.zeros((D,), jnp.float32), 'router_w': jax.random.normal(ks[1], (D, E), jnp.float32) * s, 'gate_up_w': jax.random.normal(ks[2], (E, D, 2 * F), jnp.float32) * s, 'down_w': jax.random.normal(ks[3], (E, F, D), jnp.float32) * s, 'shared_gate_up_w': jax.random.normal(ks[4], (D, 2 * FS), jnp.float32) * s, 'shared_down_w': jax.random.normal(ks[5], (FS, D), jnp.float32) * s}
    _L1_ffn_all = _L1_ffn_setup()
    _L1_ffn_in = {k: v for k, v in _L1_ffn_all.items() if k in ('ln_gamma', 'ln_beta', 'router_w', 'gate_up_w', 'down_w', 'shared_gate_up_w', 'shared_down_w')}
    del _L1_ffn_all
    return {'x': x, 'ctx_768': ctx_768, 'g_xattn': g_xattn, 'g_ffn': g_ffn, 'L0_xattn_Wq': _L0_xattn_in['Wq'], 'L0_xattn_bq': _L0_xattn_in['bq'], 'L0_xattn_Wk': _L0_xattn_in['Wk'], 'L0_xattn_bk': _L0_xattn_in['bk'], 'L0_xattn_Wv': _L0_xattn_in['Wv'], 'L0_xattn_bv': _L0_xattn_in['bv'], 'L0_xattn_Wo': _L0_xattn_in['Wo'], 'L0_xattn_bo': _L0_xattn_in['bo'], 'L0_ffn_sim_matrix': _L0_ffn_in['sim_matrix'], 'L0_ffn_gates': _L0_ffn_in['gates'], 'L0_ffn_q_proj': _L0_ffn_in['q_proj'], 'L0_ffn_k_proj': _L0_ffn_in['k_proj'], 'L0_ffn_v_proj': _L0_ffn_in['v_proj'], 'L0_ffn_o_proj': _L0_ffn_in['o_proj'], 'L1_xattn_q_w': _L1_xattn_in['q_w'], 'L1_xattn_q_b': _L1_xattn_in['q_b'], 'L1_xattn_kv_w': _L1_xattn_in['kv_w'], 'L1_xattn_kv_b': _L1_xattn_in['kv_b'], 'L1_xattn_proj_w': _L1_xattn_in['proj_w'], 'L1_xattn_proj_b': _L1_xattn_in['proj_b'], 'L1_ffn_ln_gamma': _L1_ffn_in['ln_gamma'], 'L1_ffn_ln_beta': _L1_ffn_in['ln_beta'], 'L1_ffn_router_w': _L1_ffn_in['router_w'], 'L1_ffn_gate_up_w': _L1_ffn_in['gate_up_w'], 'L1_ffn_down_w': _L1_ffn_in['down_w'], 'L1_ffn_shared_gate_up_w': _L1_ffn_in['shared_gate_up_w'], 'L1_ffn_shared_down_w': _L1_ffn_in['shared_down_w']}

def reference(x, ctx_768, g_xattn, g_ffn, L0_xattn_Wq, L0_xattn_bq, L0_xattn_Wk, L0_xattn_bk, L0_xattn_Wv, L0_xattn_bv, L0_xattn_Wo, L0_xattn_bo, L0_ffn_sim_matrix, L0_ffn_gates, L0_ffn_q_proj, L0_ffn_k_proj, L0_ffn_v_proj, L0_ffn_o_proj, L1_xattn_q_w, L1_xattn_q_b, L1_xattn_kv_w, L1_xattn_kv_b, L1_xattn_proj_w, L1_xattn_proj_b, L1_ffn_ln_gamma, L1_ffn_ln_beta, L1_ffn_router_w, L1_ffn_gate_up_w, L1_ffn_down_w, L1_ffn_shared_gate_up_w, L1_ffn_shared_down_w):
    import jax
    import jax.numpy as jnp

    def _L0_xattn_ref(query, key, value, Wq, bq, Wk, bk, Wv, bv, Wo, bo):
        import jax, jax.numpy as jnp
        import numpy as np
        QUERY_DIM = 128
        KEY_DIM = 96
        NUM_HEADS = 16
        HEAD_DIM = QUERY_DIM // NUM_HEADS
        SCALE = HEAD_DIM ** (-0.5)
        B, Nq, _ = query.shape
        Nk = key.shape[1]
        q = (query @ Wq + bq).reshape(B, Nq, NUM_HEADS, HEAD_DIM).transpose(0, 2, 1, 3)
        k = (key @ Wk + bk).reshape(B, Nk, NUM_HEADS, HEAD_DIM).transpose(0, 2, 1, 3)
        v = (value @ Wv + bv).reshape(B, Nk, NUM_HEADS, HEAD_DIM).transpose(0, 2, 1, 3)
        attn = jnp.einsum('bhqd,bhkd->bhqk', q, k) * SCALE
        attn = jax.nn.softmax(attn, axis=-1)
        out = jnp.einsum('bhqk,bhkd->bhqd', attn, v)
        out = out.transpose(0, 2, 1, 3).reshape(B, Nq, QUERY_DIM)
        return out @ Wo + bo

    def _L0_ffn_ref(hidden_states, sim_matrix, gates, q_proj, k_proj, v_proj, o_proj):
        import jax, jax.numpy as jnp
        import numpy as np
        HIDDEN = 128
        HEAD_DIM = 64
        N_EXPERTS = 16
        MIN_EXPERTS = 2
        B, T = (4, 256)

        def _normalize(x, axis):
            n = jnp.sqrt(jnp.sum(x * x, axis=axis, keepdims=True))
            return x / jnp.maximum(n, 1e-12)

        def _ste(x):
            hard = jax.lax.stop_gradient((x > 0).astype(x.dtype))
            return hard + x - jax.lax.stop_gradient(x)

        def _gating(hidden_states, sim_matrix, gates):
            b, t, c = hidden_states.shape
            flat = hidden_states.reshape(b * t, c)
            logits = _normalize(flat, -1) @ _normalize(sim_matrix, 0) - jax.nn.sigmoid(gates)
            gated = jax.nn.relu(logits)
            mask = _ste(gated)
            inactive = jnp.sum(mask, axis=1) == 0
            _, fb_idx = jax.lax.top_k(logits, MIN_EXPERTS)
            fb = jnp.zeros_like(mask).at[jnp.arange(b * t)[:, None], fb_idx].set(1.0)
            fb_applied = inactive[:, None] & (fb > 0)
            mask = jnp.where(fb_applied, 1.0, mask)
            masked_logits = jnp.where(mask > 0, gated, -jnp.inf)
            return jax.nn.softmax(masked_logits, axis=-1).reshape(b, t, -1)
        b, t, c = hidden_states.shape
        rw = _gating(hidden_states, sim_matrix, gates)
        q = jnp.einsum('bte,bted->btd', rw, jnp.einsum('btc,ecd->bted', hidden_states, q_proj))
        k = jnp.einsum('bte,bted->btd', rw, jnp.einsum('btc,ecd->bted', hidden_states, k_proj))
        v = jnp.einsum('bte,bted->btd', rw, jnp.einsum('btc,ecd->bted', hidden_states, v_proj))
        scale = 1.0 / jnp.sqrt(jnp.asarray(HEAD_DIM, dtype=q.dtype))
        scores = jnp.einsum('bqd,bkd->bqk', q, k) * scale
        causal = jnp.tril(jnp.ones((t, t), dtype=bool))
        scores = jnp.where(causal, scores, -jnp.inf)
        attn = jnp.einsum('bqk,bkd->bqd', jax.nn.softmax(scores, axis=-1), v)
        mixed = attn[:, :, None, :] * rw[..., None]
        return jnp.einsum('bted,edc->btc', mixed, o_proj)

    def _L1_xattn_ref(x, cond, q_w, q_b, kv_w, kv_b, proj_w, proj_b):
        import jax, jax.numpy as jnp
        import numpy as np
        NUM_HEADS = 16
        B, N, C = x.shape
        condN = cond.shape[1]
        H = NUM_HEADS
        hd = C // H
        scale = hd ** (-0.5)
        q = (x @ q_w + q_b).reshape(B, N, H, hd).transpose(0, 2, 1, 3)
        kv = (cond @ kv_w + kv_b).reshape(B, condN, 2, H, hd)
        k = kv[:, :, 0].transpose(0, 2, 1, 3)
        v = kv[:, :, 1].transpose(0, 2, 1, 3)
        attn = jnp.einsum('bhnd,bhmd->bhnm', q * scale, k)
        attn = jax.nn.softmax(attn, axis=-1)
        out = jnp.einsum('bhnm,bhmd->bhnd', attn, v)
        out = out.transpose(0, 2, 1, 3).reshape(B, N, C)
        return out @ proj_w + proj_b

    def _L1_ffn_ref(x, ln_gamma, ln_beta, router_w, gate_up_w, down_w, shared_gate_up_w, shared_down_w):
        import jax, jax.numpy as jnp
        import numpy as np
        B, S, D, F, E, K = (4, 256, 128, 512, 8, 2)
        FS = 128
        LN_EPS = 1e-05

        def _swiglu(x, gu_w, dn_w):
            gate, up = jnp.split(x @ gu_w, 2, axis=-1)
            gate = jnp.clip(gate, -10.0, 10.0)
            return jax.nn.silu(gate) * up @ dn_w
        b, s, d = x.shape
        xf = x.reshape(-1, d)
        mu = jnp.mean(xf, axis=-1, keepdims=True)
        var = jnp.var(xf, axis=-1, keepdims=True)
        xn = (xf - mu) * jax.lax.rsqrt(var + LN_EPS) * ln_gamma + ln_beta
        logits = xn @ router_w
        probs = jax.nn.softmax(logits, axis=-1)
        topv, topi = jax.lax.top_k(probs, K)
        topv = topv / jnp.sum(topv, axis=-1, keepdims=True)
        comb = jnp.sum(jax.nn.one_hot(topi, E, dtype=xn.dtype) * topv[..., None], axis=1)
        out = jnp.zeros_like(xf)
        for e in range(E):
            out = out + comb[:, e:e + 1] * _swiglu(xn, gate_up_w[e], down_w[e])
        out = out + _swiglu(xn, shared_gate_up_w, shared_down_w)
        return out.reshape(b, s, d)
    x = x + jnp.tanh(g_xattn[0]) * _L0_xattn_ref(_layernorm(x, axis=-1), ctx_768, ctx_768, L0_xattn_Wq, L0_xattn_bq, L0_xattn_Wk, L0_xattn_bk, L0_xattn_Wv, L0_xattn_bv, L0_xattn_Wo, L0_xattn_bo)
    x = x + jnp.tanh(g_ffn[0]) * _L0_ffn_ref(_layernorm(x, axis=-1), L0_ffn_sim_matrix, L0_ffn_gates, L0_ffn_q_proj, L0_ffn_k_proj, L0_ffn_v_proj, L0_ffn_o_proj)
    x = x + jnp.tanh(g_xattn[1]) * _L1_xattn_ref(_layernorm(x, axis=-1), ctx_768, L1_xattn_q_w, L1_xattn_q_b, L1_xattn_kv_w, L1_xattn_kv_b, L1_xattn_proj_w, L1_xattn_proj_b)
    x = x + jnp.tanh(g_ffn[1]) * _L1_ffn_ref(_layernorm(x, axis=-1), L1_ffn_ln_gamma, L1_ffn_ln_beta, L1_ffn_router_w, L1_ffn_gate_up_w, L1_ffn_down_w, L1_ffn_shared_gate_up_w, L1_ffn_shared_down_w)
    return x

_drawn_inputs = setup_inputs


def setup_inputs(seed=0):
    import zlib

    import numpy as np

    out = dict(_drawn_inputs(seed))
    spreads = {'g_ffn': (-1.0, 0.6),
     'L0_xattn_bq': (0.0, 0.3),
     'L0_xattn_bk': (0.0, 0.8),
     'L0_xattn_bv': (0.0, 0.1),
     'L0_xattn_bo': (0.0, 0.1),
     'L0_ffn_gates': (0.0, 0.1),
     'L1_xattn_q_b': (0.0, 0.421),
     'L1_xattn_kv_b': (0.0, 0.1),
     'L1_xattn_proj_b': (0.0, 0.1),
     'L1_ffn_ln_gamma': (1.0, 0.6),
     'L1_ffn_ln_beta': (0.0, 0.8)}
    factors = {'L1_ffn_router_w': 8.0,
     'L1_ffn_gate_up_w': 8.0,
     'L1_ffn_down_w': 8.0,
     'L1_ffn_shared_gate_up_w': 8.0,
     'L1_ffn_shared_down_w': 8.0}
    for name, (base, spread) in spreads.items():
        noise = np.random.default_rng([zlib.crc32(name.encode()), seed]).standard_normal(out[name].shape)
        drawn = base * np.exp(spread * noise) if base else spread * noise
        out[name] = jnp.asarray(drawn.astype(out[name].dtype))
    for name, factor in factors.items():
        out[name] = (out[name] * factor).astype(out[name].dtype)
    return out
```

```python
from contextlib import ExitStack

import numpy as np

import concourse.bass as bass
from concourse import mybir

F32, BF16 = mybir.dt.float32, mybir.dt.bfloat16
ALU, ACT, AX = mybir.AluOpType, mybir.ActivationFunctionType, mybir.AxisListType

B, NQ, D = 32, 100, 128
NK, DC = 1444, 96
H = 16
HD = D // H
TOK = B * NQ
G = 4
NG, GT = B // G, G * NQ
P = 128
EPS = 1e-5

KT = -(-NK // P)
KFULL = KT - 2
KW = [P] * KFULL + [(NK - P * KFULL) // 2] * 2
KS = [sum(KW[:t]) for t in range(KT)]
assert sum(KW) == NK
PAIRS = H // 2
TERMS = [0, 0, 0, 1, 1, 2]
QTERMS = [0, 1, 2, 0, 1, 0]
ROWS = len(TERMS) * 2 * HD
SH = 3
QUADS = H // 4
QW = 4 * NQ
UNITS = KT * QUADS
QTR = NK // 4
LAG = 3
NE, NP_ = 3, 6


class Semaphores:

    def __init__(self, nc, suffix):
        self.nc, self.suffix, self.held = nc, suffix, []

    def __call__(self, name):
        self.held.append(self.nc.alloc_semaphore(name=f"{name}_{self.suffix}"))
        return self.held[-1]

    def clear(self):
        self.nc.clear_and_free_semaphores(self.held)
        self.nc.all_engine_barrier()


class Step:

    def __init__(self, place, reg=None):
        self.place, self.reg = place, reg

    def lin(self, mult, off=0):
        if self.reg is None:
            return mult * self.place + off
        return self.reg * (3 * mult) + (mult * (1 + self.place) + off)

    def mod3(self, off=0):
        return (self.place + off + (0 if self.reg is None else 1)) % 3

    def has_prep(self):
        return self.reg is not None or -2 <= self.place <= B - 3

    def has_max(self):
        return self.reg is not None or -1 <= self.place <= B - 2

    def has_main(self):
        return self.reg is not None or 0 <= self.place <= B - 1

    def has_final(self):
        return self.reg is not None or 1 <= self.place <= B


LOOPS = 9
HEAD_STEPS = [Step(b) for b in (-2, -1, 0)]
TAIL_STEPS = [Step(b) for b in range(3 * LOOPS + 1, B + 1)]

def _slot_users():
    order = [("K", 0), ("K", 1)] + [("M", i) for i in range(32)]
    for at, user in ((4, ("O", 0)), (8, ("A", 0)), (12, ("W", 0)), (16, ("V", 0)), (20, ("V", 1))):
        order.insert(at, user)
    at = [1 + i * 40 // len(order) for i in range(len(order))]
    return [(k, i, s) for (k, i), s in zip(order, at)] + [("T", 0, 45)]


USERS = _slot_users()
SLOT = {(k, i): n % 2 for n, (k, i, _) in enumerate(USERS)}
PER_STEP = len(USERS) // 2
assert len(USERS) % 2 == 0


def _present(step, kind):
    return {"K": step.has_prep, "V": step.has_prep, "M": step.has_max, "T": step.has_max,
            "O": step.has_final, "A": step.has_final, "W": step.has_final}[kind]()


def _uses(place, slot):
    step = Step(place)
    return sum(_present(step, k) and SLOT[k, i] == slot for k, i, _ in USERS)


def slot_count(step, kind, idx):
    slot = SLOT[kind, idx]
    rank = 0
    for k, i, _ in USERS:
        if SLOT[k, i] == slot and _present(step, k):
            rank += 1
        if (k, i) == (kind, idx):
            break
    if step.reg is None:
        return sum(_uses(p, slot) for p in range(-2, step.place)) + rank
    return step.lin(PER_STEP, sum(_uses(p, slot) for p in range(-2, 1)) - PER_STEP + rank)


def attention(nc, env, lay, W, scr, x_sb):
    (ctxT, wq, bq, wk, bk, wv, bv, wo, bo) = W
    kscr, qscr, mscr = scr
    ident, tg = env["ident"], env["tg"]

    sem = Semaphores(nc, f"a{lay}")
    st = ExitStack()
    with st:
        sb = lambda name, shape, dt=F32: st.enter_context(nc.sbuf_tensor(f"{name}{lay}", shape, dt))

        wq_sb, bq_sb = sb("wq", [D, D]), sb("bq", [D, 1])
        wk_sb, bk_sb, wv_sb = sb("wk", [DC, D]), sb("bk", [D, 1]), sb("wv", [DC, D])
        bv_sb, wo_sb, bo_sb = sb("bv", [NQ, D]), sb("wo", [D, D]), sb("bo", [NQ, D])

        with ExitStack() as ps1:
            pb = lambda name, shape: ps1.enter_context(nc.psum_tensor(f"{name}{lay}", shape, F32))
            sp1 = lambda name, shape, dt=F32: ps1.enter_context(nc.sbuf_tensor(f"{name}{lay}", shape, dt))
            stat, mv = sp1("stat", [NQ, B, 6]), sp1("mv", [NQ, B, 2])
            rstd, nmr = sp1("rstd", [NQ, B]), sp1("nmr", [NQ, B])
            xn = sp1("xn", [NQ, 2, G, D])
            xnT = sp1("xnT", [D, 2, GT])
            q32, qr = sp1("q32", [D, GT]), sp1("qr", [D, GT])
            qs = sp1("qs", [D, 3, TOK], BF16)
            xnT_ps, q_ps = pb("xnT_ps", [P, 2, 512]), pb("q_ps", [P, 2, 512])

            w_in, stats, var_ok, std_ok, rstd_ok = (sem(n) for n in ("w_in", "stats", "var_ok", "std_ok", "rstd_ok"))
            ln_ok, ln_T, ln_T_out, q_mm = (sem(n) for n in ("ln_ok", "ln_T", "ln_T_out", "q_mm"))
            q_full, q_hi, q_res, q_mid, q_split = (sem(n) for n in ("q_full", "q_hi", "q_res", "q_mid", "q_split"))
            q_out = sem("q_out")

            with nc.Block() as block:
                @block.sync
                def _(sp):
                    for dst, src in ((wq_sb, wq), (bq_sb, bq), (wk_sb, wk), (bk_sb, bk), (wv_sb, wv),
                                     (wo_sb, wo)):
                        sp.dma_start(dst[:], src).then_inc(w_in, 16)
                    sp.dma_start(bv_sb[:], bv.partition_broadcast(NQ)).then_inc(w_in, 16)
                    sp.dma_start(bo_sb[:], bo.partition_broadcast(NQ)).then_inc(w_in, 16)
                    with sp.Fori(0, NG) as n:
                        sp.wait_ge(q_split, n + 1)
                        sp.dma_start(qscr[:, :, bass.ds(n * GT, GT)].rearrange("t p c -> p t c"),
                                     qs[:, :, bass.ds(n * GT, GT)]).then_inc(q_out, 16)
                    sp.wait_ge(q_out, 16 * NG)

                @block.scalar
                def _(act):
                    act.wait_ge(var_ok, 1)
                    nc.scalar.activation(rstd[:], rstd[:], ACT.Sqrt).then_inc(std_ok, 1)
                    act.wait_ge(rstd_ok, 2)
                    with act.Fori(0, NG // 2) as i:
                        for u in range(2):
                            act.wait_ge(ln_T, 2 * i + (u + 1))
                            for j in range(G):
                                off = i * (2 * G) + (u * G + j)
                                nc.scalar.activation(
                                    xn[:, u, j, :], x_sb[:, bass.ds(i * (2 * G * D) + (u * G + j) * D, D)],
                                    ACT.Identity, bias=nmr[:, bass.ds(off, 1)],
                                    scale=rstd[:, bass.ds(off, 1)]).then_inc(ln_ok, 1)

                @block.tensor
                def _(pe):
                    pe.sem_inc(ln_T, 2)
                    pe.wait_ge(env["ident_ok"], 2)
                    pe.wait_ge(w_in, 16 * 8)
                    with pe.Fori(0, NG // 2) as i:
                        for u in range(2):
                            pe.wait_ge(ln_ok, i * (2 * G) + G * (u + 1))
                            for j in range(G):
                                last = nc.tensor.transpose(xnT_ps[:, u, j * NQ:(j + 1) * NQ], xn[:, u, j, :],
                                                           ident[0:NQ, 0:NQ])
                            last.then_inc(ln_T, 1)
                            pe.wait_ge(ln_T_out, 2 * i + (u + 1))
                            nc.tensor.matmul(q_ps[:, u, 0:GT], wq_sb[:], xnT[:, u, :], start=True,
                                             stop=True).then_inc(q_mm, 1)

                @block.vector
                def _(dve):
                    with dve.Fori(0, B // 4) as i:
                        for j in range(4):
                            nc.vector.bn_stats(stat[:, bass.ds(i * 4 + j, 1), :].rearrange("p o s -> p (o s)"),
                                               x_sb[:, bass.ds(i * (4 * D) + j * D, D)]).then_inc(stats, 1)
                    dve.wait_ge(stats, B)
                    for b in range(B):
                        nc.vector.bn_aggr(mv[:, b, :], stat[:, b, :]).then_inc(stats, 1)
                    dve.wait_ge(stats, 2 * B)
                    nc.vector.tensor_scalar_add(rstd[:], mv[:, :, 1], EPS).then_inc(var_ok, 1)
                    dve.wait_ge(std_ok, 1)
                    nc.vector.reciprocal(rstd[:], rstd[:]).then_inc(rstd_ok, 1)
                    dve.wait_ge(rstd_ok, 1)
                    nc.vector.scalar_tensor_tensor(nmr[:], mv[:, :, 0], -1.0, rstd[:], ALU.mult,
                                                   ALU.mult).then_inc(rstd_ok, 1)
                    dve.wait_ge(w_in, 16 * 8)
                    with dve.Fori(0, NG // 2) as i:
                        for u in range(2):
                            n = 2 * i + u
                            dve.wait_ge(ln_T, n + 3)
                            nc.vector.tensor_copy(xnT[:, u, :], xnT_ps[:, u, 0:GT]).then_inc(ln_T_out, 1)
                            dve.wait_ge(q_mm, n + 1)
                            nc.vector.tensor_scalar(q32[:], q_ps[:, u, 0:GT], bq_sb[:, 0:1], HD ** -0.5,
                                                    ALU.add, ALU.mult).then_inc(q_full, 1)
                            dve.wait_ge(q_full, n + 1)
                            part = [qs[:, t, bass.ds(n * GT, GT)] for t in range(3)]
                            nc.vector.tensor_copy(part[0], q32[:]).then_inc(q_hi, 1)
                            dve.wait_ge(q_hi, n + 1)
                            nc.vector.tensor_tensor(qr[:], q32[:], part[0], ALU.subtract).then_inc(q_res, 1)
                            dve.wait_ge(q_res, n + 1)
                            nc.vector.tensor_copy(part[1], qr[:]).then_inc(q_mid, 1)
                            dve.wait_ge(q_mid, n + 1)
                            nc.vector.tensor_tensor(part[2], qr[:], part[1], ALU.subtract).then_inc(q_split, 1)

        ctx_sb = sb("ctx", [DC, 3, NK])
        k32, kr = sb("k32", [D, NK]), sb("kr", [D, NK])
        ks = sb("ks", [D, 3, NK], BF16)
        Kp, Qp, V = env["Kp"], env["Qp"], env["V"]
        probs = sb("probs", [P, NP_, QW])
        mx, mmax = sb("mx", [NQ, 2, H]), sb("mmax", [NQ, H])
        mr = sb("mr", [H, NQ])
        mT = sb("mT", [H, 3, NQ], BF16)
        oT = sb("oT", [P, QW])
        rden, heads = sb("rden", [NQ, H]), sb("heads", [NQ, D])
        headsT, gated = sb("headsT", [D, NQ]), sb("gated", [NQ, D])

        pb = lambda name, shape: st.enter_context(nc.psum_tensor(f"{name}{lay}", shape, F32))
        slots = [pb("slot_a", [P, 2, 512]), pb("slot_b", [P, 2, 512])]
        scores, o_ps = pb("scores", [P, NE, 512]), pb("o_ps", [P, 512])

        slot_full = [sem("slot_a_full"), sem("slot_b_full")]
        slot_read = [sem("slot_a_read"), sem("slot_b_read")]
        ctx_in = [sem(f"ctx_in{i}_") for i in range(3)]
        pack_in = [sem(f"pack_in{i}_") for i in range(3)]
        shift_in = [sem(f"shift_in{i}_") for i in range(3)]
        init, k_evac, k_diff, k_split, k_out = (sem(n) for n in ("init", "k_evac", "k_diff", "k_split", "k_out"))
        scored, exped, pv_done, o_evac = (sem(n) for n in ("scored", "exped", "pv_done", "o_evac"))
        m_ready, m_hi, m_res, m_mid, m_split, m_out = (
            sem(n) for n in ("m_ready", "m_hi", "m_res", "m_mid", "m_split", "m_out"))
        den_ok, heads_mul, heads_ok, headsT_ok, wo_bias, x_ok = (
            sem(n) for n in ("den_ok", "heads_mul", "heads_ok", "headsT_ok", "wo_bias", "x_ok"))

        def user_wait(eng, sems, step, kind, idx):
            eng.wait_ge(sems[SLOT[kind, idx]], slot_count(step, kind, idx))

        def users_at(step, s):
            return [(k, i) for k, i, at in USERS if at == s and _present(step, k)]

        def run(eng, body):
            for step in HEAD_STEPS:
                body(step)
            with eng.Fori(0, LOOPS) as i:
                for u in range(3):
                    body(Step(u, i))
            for step in TAIL_STEPS:
                body(step)

        def at_batch(step, off):
            return step.lin(1, off)

        with nc.Block() as block:
            @block.sync
            def _(sp):
                def body(step):
                    if step.reg is not None or -2 <= step.place <= B - 4:
                        nb = step.mod3(3)
                        if step.reg is not None or step.place >= 1:
                            sp.wait_ge(scored, step.lin(UNITS))
                        elif step.place == 0:
                            user_wait(sp, slot_full, Step(-2), "V", 1)
                        sp.dma_start(ctx_sb[:, nb, :], ctxT[bass.ds(step.lin(DC, 3 * DC), DC), :])\
                          .then_inc(ctx_in[nb], 16)
                    if step.has_prep():
                        nb = step.mod3(2)
                        sp.wait_ge(k_split, step.lin(1, 3))
                        if step.reg is not None or step.place >= 1:
                            sp.wait_ge(scored, step.lin(UNITS))
                        sp.dma_start(kscr[nb].rearrange("t p n -> p t n"), ks[:]).then_inc(k_out, 16)
                        for t, part in enumerate(QTERMS):
                            for hh in range(2):
                                r = (2 * t + hh) * HD
                                src = qscr[part, hh * 64:(hh + 1) * 64, bass.ds(step.lin(NQ, 2 * NQ), NQ)]
                                dst = Qp[r:r + HD, nb, :].rearrange("d (g a c) -> d g a c", g=PAIRS, a=2)
                                sp.dma_start(dst[:, :, hh, :], src.rearrange("(d g) c -> d g c", g=PAIRS))\
                                  .then_inc(pack_in[nb], 16)
                        sp.wait_ge(k_out, step.lin(16, 3 * 16))
                        for t, part in enumerate(TERMS):
                            r = 2 * t * HD
                            sp.dma_start(Kp[r:r + 2 * HD, nb, :, :],
                                         kscr[nb, part].rearrange("(r g) n -> r g n", g=PAIRS))\
                              .then_inc(pack_in[nb], 16)
                    if step.has_max():
                        nb = step.mod3(1)
                        sp.wait_ge(m_split, step.lin(1, 2))
                        sp.dma_start(mscr[nb].rearrange("t h c -> h t c"), mT[:]).then_inc(m_out, 16)
                        sp.wait_ge(m_out, step.lin(16, 2 * 16))
                        sp.dma_start(Qp[ROWS:ROWS + SH, nb, :], mscr[nb].rearrange("t h c -> t (h c)"))\
                          .then_inc(shift_in[nb], 16)

                sp.dma_start(ctx_sb[:, 0, :], ctxT[0:DC, :]).then_inc(ctx_in[0], 16)
                run(sp, body)

            @block.gpsimd
            def _(pool):
                def body(step):
                    if step.has_prep():
                        pool.wait_ge(k_evac, step.lin(2, 3 * 2))
                        nc.gpsimd.tensor_tensor(kr[:], k32[:], ks[:, 0, :], ALU.subtract).then_inc(k_diff, 1)
                        nc.gpsimd.tensor_tensor(ks[:, 1, :], k32[:], ks[:, 0, :], ALU.subtract).then_inc(k_diff, 1)
                        pool.wait_ge(k_diff, step.lin(2, 3 * 2))
                        nc.gpsimd.tensor_tensor(ks[:, 2, :], kr[:], ks[:, 1, :], ALU.subtract).then_inc(k_split, 1)

                run(pool, body)

            @block.scalar
            def _(act):
                def evac_k(step, i):
                    cols = slice(2 * i * QTR, 2 * (i + 1) * QTR)
                    src = slots[SLOT["K", i]][:, :, 0:QTR]
                    if i == 0 and (step.reg is not None or step.place >= -1):
                        act.wait_ge(k_split, step.lin(1, 2))
                        act.wait_ge(k_out, step.lin(16, 2 * 16))
                    user_wait(act, slot_full, step, "K", i)
                    nc.scalar.activation(k32[:, cols].rearrange("p (a n) -> p a n", a=2), src, ACT.Identity,
                                         bias=bk_sb[:, 0:1]).then_inc(slot_read[SLOT["K", i]], 1)
                    user_wait(act, slot_read, step, "K", i)
                    nc.scalar.activation(ks[:, 0, cols], k32[:, cols], ACT.Copy).then_inc(k_evac, 1)

                def evac_v(step, i):
                    nb, slot = step.mod3(2), SLOT["V", i]
                    if i == 0 and (step.reg is not None or step.place >= 1):
                        act.wait_ge(pv_done, step.lin(UNITS))
                    user_wait(act, slot_full, step, "V", i)
                    if i == 0:
                        src = slots[slot][:].rearrange("p a n -> p (a n)")
                        nc.scalar.activation(V[:, nb, 0:8, :, 0:HD],
                                             src.rearrange("p (t h d) -> p t h d", t=8, h=H), ACT.Copy)\
                          .then_inc(slot_read[slot], 1)
                    else:
                        src = slots[slot][:, 0, :].rearrange("p (t h d) -> p t h d", t=4, h=H)
                        nc.scalar.activation(V[:, nb, 8:KFULL, :, 0:HD], src[:, 0:KFULL - 8], ACT.Copy)
                        nc.scalar.activation(V[0:KW[-1], nb, KFULL:KT, :, 0:HD], src[0:KW[-1], KFULL - 8:KT - 8],
                                             ACT.Copy)\
                          .then_inc(slot_read[slot], 1)

                def body(step):
                    for s in range(UNITS):
                        if step.has_main():
                            w = KW[s // QUADS]
                            act.wait_ge(scored, step.lin(UNITS, s + 1))
                            if step.reg is not None or UNITS * step.place + s >= NP_:
                                act.wait_ge(pv_done, step.lin(UNITS, s - NP_ + 1))
                            nc.scalar.activation(probs[0:w, s % NP_, :], scores[0:w, s % NE, 0:QW], ACT.Exp)\
                              .then_inc(exped, 1)
                        if s == LAG - 1 and step.has_final():
                            act.wait_ge(pv_done, step.lin(UNITS))
                            nc.scalar.activation(oT[:], o_ps[:, 0:QW], ACT.Copy).then_inc(o_evac, 1)
                        for kind, i in users_at(step, s):
                            if kind == "K":
                                evac_k(step, i)
                            elif kind == "V":
                                evac_v(step, i)

                run(act, body)

            @block.vector
            def _(dve):
                nc.vector.memset(o_ps[:], 0.0).then_inc(init, 1)

                def body(step):
                    for kind, i, _ in USERS:
                        if kind in "KV" or not _present(step, kind):
                            continue
                        slot = slots[SLOT[kind, i]]
                        user_wait(dve, slot_full, step, kind, i)
                        freed = slot_read[SLOT[kind, i]]
                        if kind == "M":
                            nc.vector.tensor_reduce(mx[:, i % 2, i // 2:i // 2 + 1], slot[0:NQ, :, 0:QTR], AX.XY,
                                                    ALU.max).then_inc(freed, 1)
                            if i == 31:
                                for j in (30, 31):
                                    user_wait(dve, slot_read, step, "M", j)
                                nc.vector.tensor_tensor(mmax[:], mx[:, 0, :], mx[:, 1, :], ALU.max).then_inc(m_ready, 1)
                        elif kind == "T":
                            mps = slot[0:H, 0, 0:NQ]
                            if step.reg is not None or step.place >= 0:
                                dve.wait_ge(m_out, step.lin(16, 16))
                            nc.vector.tensor_scalar_mul(mT[:, 0, :], mps, -1.0).then_inc(m_hi, 1)
                            dve.wait_ge(m_hi, step.lin(1, 2))
                            nc.vector.scalar_tensor_tensor(mr[:], mps, -1.0, mT[:, 0, :], ALU.mult,
                                                           ALU.subtract).then_inc(freed, 1)
                            user_wait(dve, slot_read, step, "T", 0)
                            nc.vector.tensor_copy(mT[:, 1, :], mr[:]).then_inc(m_mid, 1)
                            dve.wait_ge(m_mid, step.lin(1, 2))
                            nc.vector.tensor_tensor(mT[:, 2, :], mr[:], mT[:, 1, :], ALU.subtract)\
                              .then_inc(m_split, 1)
                        elif kind == "O":
                            ov = slot[0:NQ, 0, :].rearrange("c (h e) -> c h e", h=H)
                            nc.vector.reciprocal(rden[:], ov[:, :, HD]).then_inc(den_ok, 1)
                            dve.wait_ge(den_ok, at_batch(step, 0))
                            hv = heads[:].rearrange("c (h d) -> c h d", h=H)
                            nc.vector.tensor_tensor(hv, ov[:, :, 0:HD],
                                                    rden[:].unsqueeze(2).to_broadcast([NQ, H, HD]), ALU.mult)\
                              .then_inc(freed, 1)
                            user_wait(dve, slot_read, step, "O", 0)
                            nc.vector.tensor_tensor(heads[:], heads[:], bv_sb[:], ALU.add).then_inc(heads_ok, 1)
                        elif kind == "A":
                            nc.vector.tensor_copy(headsT[:], slot[:, 0, 0:NQ]).then_inc(freed, 1)
                        elif kind == "W":
                            nc.vector.tensor_tensor(gated[:], slot[0:NQ, 0, 0:D], bo_sb[:], ALU.add)\
                              .then_inc(freed, 1)
                            user_wait(dve, slot_read, step, "W", 0)
                            xb = x_sb[:, bass.ds(step.lin(D, -D), D)]
                            nc.vector.scalar_tensor_tensor(xb, gated[:], tg[0:NQ, lay:lay + 1], xb, ALU.mult,
                                                           ALU.add).then_inc(x_ok, 1)

                run(dve, body)

            @block.tensor
            def _(pe):
                def project_k(step, i):
                    nb, slot = step.mod3(2), slots[SLOT["K", i]]
                    if i == 0:
                        pe.wait_ge(ctx_in[nb], third(step, 2, 16))
                    for a in range(2):
                        c = (2 * i + a) * QTR
                        last = nc.tensor.matmul(slot[:, a, 0:QTR], wk_sb[:], ctx_sb[:, nb, c:c + QTR], start=True,
                                                stop=True)
                    return last

                def project_v(step, i):
                    nb, slot = step.mod3(2), slots[SLOT["V", i]]
                    for n in range(8 * i, min(8 * i + 8, KT)):
                        a, c = (n - 8 * i) // 4, (n % 4) * D
                        last = nc.tensor.matmul(slot[0:KW[n], a, c:c + D], ctx_sb[:, nb, KS[n]:KS[n] + KW[n]],
                                                wv_sb[:], start=True, stop=True)
                    return last

                def third(step, off, mult):
                    if step.reg is None:
                        return mult * ((step.place + off) // 3 + 1)
                    return step.reg * mult + mult * ((1 + step.place + off) // 3 + 1)

                def max_unit(step, i):
                    nb, h = step.mod3(1), i // 2
                    if i == 0:
                        pe.wait_ge(pack_in[nb], third(step, 1, 16 * (2 * len(QTERMS) + len(TERMS))))
                    for a in range(2):
                        c = (2 * (i % 2) + a) * QTR
                        last = nc.tensor.matmul(slots[SLOT["M", i]][0:NQ, a, 0:QTR],
                                                Qp[0:ROWS, nb, h * NQ:(h + 1) * NQ],
                                                Kp[0:ROWS, nb, h // 2, c:c + QTR], start=True, stop=True)
                    return last

                def use_slot(step, kind, i):
                    count = slot_count(step, kind, i)
                    if step.reg is not None or count > 1:
                        pe.wait_ge(slot_read[SLOT[kind, i]], count - 1)
                    slot = slots[SLOT[kind, i]]
                    if kind == "K":
                        last = project_k(step, i)
                    elif kind == "V":
                        last = project_v(step, i)
                    elif kind == "M":
                        last = max_unit(step, i)
                    elif kind == "T":
                        pe.wait_ge(m_ready, at_batch(step, 2))
                        last = nc.tensor.transpose(slot[0:H, 0, 0:NQ], mmax[:], ident[0:NQ, 0:NQ])
                    elif kind == "O":
                        pe.wait_ge(o_evac, at_batch(step, 0))
                        for q in range(QUADS):
                            last = nc.tensor.transpose(slot[0:NQ, 0, q * P:(q + 1) * P], oT[:, q * NQ:(q + 1) * NQ],
                                                       ident[:])
                    elif kind == "A":
                        pe.wait_ge(heads_ok, at_batch(step, 0))
                        last = nc.tensor.transpose(slot[:, 0, 0:NQ], heads[:], ident[0:NQ, 0:NQ])
                    elif kind == "W":
                        user_wait(pe, slot_read, step, "A", 0)
                        last = nc.tensor.matmul(slot[0:NQ, 0, 0:D], headsT[:], wo_sb[:], start=True, stop=True)
                    last.then_inc(slot_full[SLOT[kind, i]], 1)

                def score_unit(step, s):
                    nb, n, q = step.mod3(), s // QUADS, s % QUADS
                    if s == 0:
                        pe.wait_ge(shift_in[nb], third(step, 0, 16))
                    if step.reg is not None or UNITS * step.place + s >= NE:
                        pe.wait_ge(exped, step.lin(UNITS, s - NE + 1))
                    for a in range(2):
                        g = 2 * q + a
                        last = nc.tensor.matmul(scores[0:KW[n], s % NE, a * 2 * NQ:(a + 1) * 2 * NQ],
                                                Kp[0:ROWS + SH, nb, g, KS[n]:KS[n] + KW[n]],
                                                Qp[0:ROWS + SH, nb, g * 2 * NQ:(g + 1) * 2 * NQ],
                                                start=True, stop=True)
                    last.then_inc(scored, 1)

                def pv_unit(step, s, back):
                    nb, n, q = step.mod3(-back), s // QUADS, s % QUADS
                    if s == 0:
                        if step.reg is not None or step.place >= 1:
                            pe.wait_ge(o_evac, at_batch(step, 0))
                    pe.wait_ge(exped, step.lin(UNITS, s + 1 - back * UNITS))
                    for j in range(4):
                        last = nc.tensor.matmul(o_ps[32 * j:32 * j + HD + 1, q * NQ:(q + 1) * NQ],
                                                V[0:KW[n], nb, n, 4 * q + j, :],
                                                probs[0:KW[n], s % NP_, j * NQ:(j + 1) * NQ],
                                                start=(n == 0 and q == 0), stop=(n == KT - 1),
                                                skip_group_check=True)
                    last.then_inc(pv_done, 1)

                def body(step):
                    for s in range(UNITS):
                        if step.has_main():
                            score_unit(step, s)
                        if s < LAG:
                            if step.has_final():
                                pv_unit(step, UNITS - LAG + s, 1)
                        elif step.has_main():
                            pv_unit(step, s - LAG, 0)
                        for kind, i in users_at(step, s):
                            use_slot(step, kind, i)

                pe.wait_ge(init, 1)
                run(pe, body)
    sem.clear()


def layer_norm_stats(nc, dve, act_io, x_of, stat, mv, rstd, nmr, sems):
    stats, var_ok, std_ok, rstd_ok = sems
    with dve.Fori(0, B // 4) as i:
        for j in range(4):
            nc.vector.bn_stats(stat[:, bass.ds(i * 4 + j, 1), :].rearrange("p o s -> p (o s)"),
                               x_of(i * (4 * D) + j * D)).then_inc(stats, 1)
    dve.wait_ge(stats, B)
    for b in range(B):
        nc.vector.bn_aggr(mv[:, b, :], stat[:, b, :]).then_inc(stats, 1)
    dve.wait_ge(stats, 2 * B)
    nc.vector.tensor_scalar_add(rstd[:], mv[:, :, 1], EPS).then_inc(var_ok, 1)
    dve.wait_ge(std_ok, 1)
    nc.vector.reciprocal(rstd[:], rstd[:]).then_inc(rstd_ok, 1)
    dve.wait_ge(rstd_ok, 1)
    nc.vector.scalar_tensor_tensor(nmr[:], mv[:, :, 0], -1.0, rstd[:], ALU.mult,
                                   ALU.mult).then_inc(rstd_ok, 1)


def bc(ap, n):
    return ap.unsqueeze(2).to_broadcast([ap.shape[0], ap.shape[1], n])


def bm(ap, n):
    return ap.unsqueeze(1).to_broadcast([ap.shape[0], n, ap.shape[1]])


def top_two(nc, link, L, L2, desc, cand, f1, f2, mx, E):
    for n, (src, f) in enumerate(((L, f1), (L2, f2))):
        link(nc.vector.tensor_tensor(cand, src, bc(mx, E), ALU.is_ge))
        link(nc.vector.tensor_tensor(cand, cand, desc, ALU.mult))
        link(nc.vector.tensor_reduce(mx, cand, AX.X, ALU.max))
        link(nc.vector.tensor_tensor(f, cand, bc(mx, E), ALU.is_equal))
        if n == 0:
            link(nc.vector.scalar_tensor_tensor(L2, f, -1e30, L, ALU.mult, ALU.add))
            link(nc.vector.tensor_reduce(mx, L2, AX.X, ALU.max))
    link(nc.vector.tensor_tensor(f1, f1, f2, ALU.add))


def expert_attention(nc, env, W, x_sb):
    sim, gates, wqk, wv, wo = W
    E, HE = 16, 64
    EP = E // 2
    ident, tg = env["ident"], env["tg"]
    sem = Semaphores(nc, "f")
    st = ExitStack()
    with st:
        sb = lambda name, shape, dt=F32: st.enter_context(nc.sbuf_tensor(f"{name}_f", shape, dt))
        wqk_sb, wv_sb, wo_sb = sb("wqk", [D, E, 2 * HE]), sb("wve", [D, E, HE]), sb("woe", [P, EP, D])
        causal = sb("causal", [NQ, NQ])
        rstd, nmr, rw = sb("rstd", [NQ, B]), sb("nmr", [NQ, B]), sb("rw", [NQ, B, E])

        with ExitStack() as s1:
            sg_ = lambda name, shape, dt=F32: s1.enter_context(nc.sbuf_tensor(f"{name}_g", shape, dt))
            sim_sb, ssq, snorm, ones = sg_("sim", [D, E]), sg_("ssq", [D, E]), sg_("snorm", [D, E]), sg_("ones", [D, D])
            gs = sg_("gs", [NQ, E])
            stat, mv = sg_("stat", [NQ, B, 6]), sg_("mv", [NQ, B, 2])
            xn, sq, xnT = sg_("xn", [NQ, 2, G, D]), sg_("sq", [NQ, 2, G, D]), sg_("xnT", [D, 2, GT])
            ss = sg_("ss", [NQ, B])
            L, L2, cand = sg_("L", [NQ, B, E]), sg_("L2", [NQ, B, E]), sg_("cand", [NQ, B, E])
            f1, f2, mask = sg_("f1", [NQ, B, E]), sg_("f2", [NQ, B, E]), sg_("mask", [NQ, B, E])
            gated = sg_("gated", [NQ, B, E])
            mx, top, idle = sg_("mx", [NQ, B]), sg_("top", [NQ, B]), sg_("idle", [NQ, B])
            desc_i, desc = sg_("desc_i", [NQ, E], mybir.dt.int32), sg_("desc", [NQ, E])
            xnT_ps = s1.enter_context(nc.psum_tensor("xnT_ps_g", [P, 2, 512], F32))
            log_ps = s1.enter_context(nc.psum_tensor("log_ps_g", [P, 2, 512], F32))
            sim_ps = s1.enter_context(nc.psum_tensor("sim_ps_g", [P, 512], F32))
            sim_in, w_in, stats, var_ok, std_ok, rstd_ok = (
                sem(n) for n in ("sim_in", "w_in", "stats", "var_ok", "std_ok", "rstd_ok"))
            sim_sq, sim_sum, sim_root, sim_n, sig_exp = (
                sem(n) for n in ("sim_sq", "sim_sum", "sim_root", "sim_n", "sig_exp"))
            ln_ok, sq_ok, ln_T, ln_T_out, logit_mm, logit_ok = (
                sem(n) for n in ("ln_ok", "sq_ok", "ln_T", "ln_T_out", "logit_mm", "logit_ok"))
            norm_root, pre_exp, gate_exp, chain, iota_ok = (
                sem(n) for n in ("norm_root", "pre_exp", "gate_exp", "chain", "iota_ok"))

            with nc.Block() as block:
                @block.sync
                def _(sp):
                    sp.dma_start(sim_sb[:], sim).then_inc(sim_in, 16)
                    sp.dma_start(gs[:], gates.partition_broadcast(NQ)).then_inc(sim_in, 16)
                    sp.dma_start(wqk_sb[:], wqk).then_inc(w_in, 16)
                    sp.dma_start(wv_sb[:], wv).then_inc(w_in, 16)
                    sp.dma_start(wo_sb[:], wo).then_inc(w_in, 16)
                    sp.wait_ge(w_in, 48)

                @block.gpsimd
                def _(pool):
                    nc.gpsimd.iota(desc_i[:], [[-1, E]], base=E, channel_multiplier=0).then_inc(iota_ok, 1)
                    nc.gpsimd.memset(causal[:], 0.0).then_inc(iota_ok, 1)
                    pool.wait_ge(iota_ok, 2)
                    nc.gpsimd.affine_select(out=causal[:], in_=causal[:], compare_op=ALU.is_ge, fill=-1e30, base=0,
                                            pattern=[[-1, NQ]], channel_multiplier=1).then_inc(iota_ok, 1)

                @block.scalar
                def _(act):
                    act.wait_ge(sim_in, 32)
                    nc.scalar.activation(gs[:], gs[:], ACT.Exp, scale=-1.0).then_inc(sig_exp, 1)
                    act.wait_ge(sim_sum, 1)
                    nc.scalar.activation(snorm[:], sim_ps[:, 0:E], ACT.Sqrt).then_inc(sim_root, 1)
                    act.wait_ge(var_ok, 1)
                    nc.scalar.activation(rstd[:], rstd[:], ACT.Sqrt).then_inc(std_ok, 1)
                    act.wait_ge(rstd_ok, 2)
                    with act.Fori(0, NG // 2) as i:
                        for u in range(2):
                            n = 2 * i + u
                            act.wait_ge(ln_T, n + 1)
                            act.wait_ge(logit_ok, n + 1)
                            for j in range(G):
                                off = i * (2 * G) + (u * G + j)
                                nc.scalar.activation(
                                    xn[:, u, j, :], x_sb[:, bass.ds(i * (2 * G * D) + (u * G + j) * D, D)],
                                    ACT.Identity, bias=nmr[:, bass.ds(off, 1)],
                                    scale=rstd[:, bass.ds(off, 1)]).then_inc(ln_ok, 1)
                            act.wait_ge(ln_ok, i * (2 * G) + (u + 1) * G)
                            nc.scalar.activation(sq[:, u], xn[:, u], ACT.Square).then_inc(sq_ok, 1)
                    act.wait_ge(logit_ok, NG + 2)
                    nc.scalar.activation(ss[:], ss[:], ACT.Sqrt).then_inc(norm_root, 1)
                    act.wait_ge(pre_exp, 1)
                    nc.scalar.activation(L[:], gated[:], ACT.Exp).then_inc(gate_exp, 1)

                @block.tensor
                def _(pe):
                    pe.sem_inc(ln_T, 2)
                    pe.wait_ge(sim_sq, 2)
                    nc.tensor.matmul(sim_ps[:, 0:E], ones[:], ssq[:], start=True, stop=True).then_inc(sim_sum, 1)
                    pe.wait_ge(sim_n, 3)
                    with pe.Fori(0, NG // 2) as i:
                        for u in range(2):
                            n = 2 * i + u
                            pe.wait_ge(ln_ok, i * (2 * G) + G * (u + 1))
                            for j in range(G):
                                last = nc.tensor.transpose(xnT_ps[:, u, j * NQ:(j + 1) * NQ], xn[:, u, j, :],
                                                           ident[0:NQ, 0:NQ])
                            last.then_inc(ln_T, 1)
                            pe.wait_ge(ln_T_out, n + 1)
                            for j in range(G):
                                last = nc.tensor.matmul(log_ps[0:NQ, u, j * E:(j + 1) * E],
                                                        xnT[:, u, j * NQ:(j + 1) * NQ], sim_sb[:],
                                                        start=True, stop=True)
                            last.then_inc(logit_mm, 1)

                @block.vector
                def _(dve):
                    done = [0]

                    def link(ins):
                        done[0] += 1
                        ins.then_inc(chain, 1)
                        dve.wait_ge(chain, done[0])

                    dve.sem_inc(logit_ok, 2)
                    nc.vector.memset(ones[:], 1.0).then_inc(sim_sq, 1)
                    dve.wait_ge(sim_in, 32)
                    nc.vector.tensor_tensor(ssq[:], sim_sb[:], sim_sb[:], ALU.mult).then_inc(sim_sq, 1)
                    dve.wait_ge(sig_exp, 1)
                    link(nc.vector.tensor_scalar_add(gs[:], gs[:], 1.0))
                    link(nc.vector.reciprocal(gs[:], gs[:]))
                    dve.wait_ge(iota_ok, 1)
                    link(nc.vector.tensor_copy(desc[:], desc_i[:]))
                    dve.wait_ge(sim_root, 1)
                    nc.vector.tensor_scalar_max(snorm[:], snorm[:], 1e-12).then_inc(sim_n, 1)
                    dve.wait_ge(sim_n, 1)
                    nc.vector.reciprocal(snorm[:], snorm[:]).then_inc(sim_n, 1)
                    dve.wait_ge(sim_n, 2)
                    nc.vector.tensor_tensor(sim_sb[:], sim_sb[:], snorm[:], ALU.mult).then_inc(sim_n, 1)
                    layer_norm_stats(nc, dve, None, lambda off: x_sb[:, bass.ds(off, D)], stat, mv, rstd, nmr,
                                     (stats, var_ok, std_ok, rstd_ok))
                    Lf = L[:].rearrange("p b e -> p (b e)")
                    with dve.Fori(0, NG // 2) as i:
                        for u in range(2):
                            n = 2 * i + u
                            dve.wait_ge(ln_T, n + 3)
                            nc.vector.tensor_copy(xnT[:, u, :], xnT_ps[:, u, 0:GT]).then_inc(ln_T_out, 1)
                            dve.wait_ge(sq_ok, n + 1)
                            nc.vector.tensor_reduce(ss[:, bass.ds(n * G, G)], sq[:, u], AX.X, ALU.add)
                            dve.wait_ge(logit_mm, n + 1)
                            nc.vector.tensor_copy(Lf[:, bass.ds(n * (G * E), G * E)],
                                                  log_ps[0:NQ, u, 0:G * E]).then_inc(logit_ok, 1)
                    dve.wait_ge(norm_root, 1)
                    link(nc.vector.tensor_scalar_max(ss[:], ss[:], 1e-12))
                    link(nc.vector.reciprocal(ss[:], ss[:]))
                    link(nc.vector.tensor_tensor(L[:], L[:], bc(ss[:], E), ALU.mult))
                    link(nc.vector.tensor_tensor(L[:], L[:], bm(gs[:], B), ALU.subtract))
                    link(nc.vector.tensor_reduce(top[:], L[:], AX.X, ALU.max))
                    nc.vector.tensor_scalar_max(gated[:], L[:], 0.0)
                    nc.vector.tensor_single_scalar(mask[:], L[:], 0.0, ALU.is_gt)
                    nc.vector.tensor_single_scalar(idle[:], top[:], 0.0, ALU.is_le)
                    link(nc.vector.tensor_copy(mx[:], top[:]))
                    top_two(nc, link, L[:], L2[:], bm(desc[:], B), cand[:], f1[:], f2[:], mx[:], E)
                    link(nc.vector.tensor_tensor(f1[:], f1[:], bc(idle[:], E), ALU.mult))
                    nc.vector.tensor_tensor(mask[:], mask[:], f1[:], ALU.add)
                    link(nc.vector.tensor_scalar_max(top[:], top[:], 0.0))
                    nc.vector.tensor_tensor(gated[:], gated[:], bc(top[:], E), ALU.subtract).then_inc(pre_exp, 1)
                    dve.wait_ge(gate_exp, 1)
                    link(nc.vector.tensor_tensor(L[:], L[:], mask[:], ALU.mult))
                    link(nc.vector.tensor_reduce(mx[:], L[:], AX.X, ALU.add))
                    link(nc.vector.reciprocal(mx[:], mx[:]))
                    link(nc.vector.tensor_tensor(rw[:], L[:], bc(mx[:], E), ALU.mult))

        xn, xs = sb("xnb", [NQ, D]), sb("xs", [NQ, E, D])
        xsT = sb("xsT", [D, E * NQ])
        qT, kT, v = sb("qT", [HE, NQ]), sb("kT", [HE, NQ]), sb("v", [NQ, HE])
        masked, nmax, den, rden = sb("masked", [NQ, NQ]), sb("nmax", [NQ, 1]), sb("den", [NQ, 1]), sb("rden", [NQ, 1])
        pr, prT, rwd = sb("pr", [NQ, NQ]), sb("prT", [NQ, NQ]), sb("rwd", [NQ, E])
        mixed, mixT = sb("mixed", [NQ, E, HE]), sb("mixT", [P, EP * NQ])
        pb = lambda name: st.enter_context(nc.psum_tensor(f"{name}_f", [P, 512], F32))
        T_ps = [pb("T_a"), pb("T_b")]
        qk_ps, v_ps, sc_ps, prT_ps, att_ps, out_ps = (
            pb(n) for n in ("qk_ps", "v_ps", "sc_ps", "prT_ps", "att_ps", "out_ps"))
        T_full, T_read, xn_ok, xs_ok, qk_mm, qk_out, v_mm, v_out = (
            sem(n) for n in ("T_full", "T_read", "xn_ok", "xs_ok", "qk_mm", "qk_out", "v_mm", "v_out"))
        sc_mm, masked_ok, nmax_ok, pr_ok, prT_full, prT_out, att_mm = (
            sem(n) for n in ("sc_mm", "masked_ok", "nmax_ok", "pr_ok", "prT_full", "prT_out", "att_mm"))
        rden_ok, rwd_ok, mixed_ok, out_mm, x_ok = (
            sem(n) for n in ("rden_ok", "rwd_ok", "mixed_ok", "out_mm", "x_ok"))

        class Two:

            def __init__(self, place, reg=None):
                self.place, self.reg = place, reg

            def lin(self, mult, off=0):
                if self.reg is None:
                    return mult * self.place + off
                return self.reg * (2 * mult) + (mult * (2 + self.place) + off)

            def on(self, lag):
                return self.reg is not None or 0 <= self.place - lag < B

        def T_use(step, k):
            if step.reg is not None:
                return step.lin(6, k - 4)
            first = sum(4 * Two(p).on(0) + 2 * Two(p).on(2) for p in range(step.place))
            return first + (k if step.on(0) else k - 4)

        def run(eng, body):
            for p in (-1, 0, 1):
                body(Two(p))
            with eng.Fori(0, (B - 4) // 2) as i:
                for u in range(2):
                    body(Two(u, i))
            for p in (B - 2, B - 1, B, B + 1):
                body(Two(p))

        with nc.Block() as block:
            @block.tensor
            def _(pe):
                def transposes(step, k, src, w):
                    n = T_use(step, k)
                    if step.reg is not None or n >= 2:
                        pe.wait_ge(T_read, n - 1)
                    for j in range(4):
                        last = nc.tensor.transpose(T_ps[k % 2][:, j * NQ:(j + 1) * NQ], src[:, 4 * (k % 4) + j, :],
                                                   ident[0:NQ, 0:NQ])
                    last.then_inc(T_full, 1)

                def body(step):
                    if step.on(0):
                        pe.wait_ge(xs_ok, step.lin(1, 1))
                        for k in range(4):
                            transposes(step, k, xs, D)
                    if step.on(1):
                        pe.wait_ge(qk_out, step.lin(1))
                        nc.tensor.matmul(sc_ps[0:NQ, 0:NQ], qT[:], kT[:], start=True, stop=True).then_inc(sc_mm, 1)
                    if step.on(2):
                        pe.wait_ge(mixed_ok, step.lin(1, -1))
                        mv_ = mixed[:].rearrange("p (j a) d -> p j (a d)", a=2)
                        for k in range(4, 6):
                            transposes(step, k, mv_, P)
                    if step.on(0):
                        pe.wait_ge(T_read, T_use(step, 3) + 1)
                        for e in range(E):
                            last = nc.tensor.matmul(qk_ps[:, 0:NQ], wqk_sb[:, e, :], xsT[:, e * NQ:(e + 1) * NQ],
                                                    start=(e == 0), stop=(e == E - 1))
                        last.then_inc(qk_mm, 1)
                    if step.on(2):
                        pe.wait_ge(T_read, T_use(step, 5) + 1)
                        for j in range(EP):
                            last = nc.tensor.matmul(out_ps[0:NQ, 0:D], mixT[:, j * NQ:(j + 1) * NQ], wo_sb[:, j, :],
                                                    start=(j == 0), stop=(j == EP - 1))
                        last.then_inc(out_mm, 1)
                    if step.on(1):
                        pe.wait_ge(pr_ok, step.lin(1))
                        nc.tensor.transpose(prT_ps[0:NQ, 0:NQ], pr[:], ident[0:NQ, 0:NQ]).then_inc(prT_full, 1)
                    if step.on(0):
                        if step.reg is not None or step.place >= 1:
                            pe.wait_ge(v_out, step.lin(1))
                        for e in range(E):
                            last = nc.tensor.matmul(v_ps[0:NQ, 0:HE], xsT[:, e * NQ:(e + 1) * NQ], wv_sb[:, e, :],
                                                    start=(e == 0), stop=(e == E - 1))
                        last.then_inc(v_mm, 1)
                    if step.on(1):
                        pe.wait_ge(prT_out, step.lin(1))
                        pe.wait_ge(v_out, step.lin(1))
                        nc.tensor.matmul(att_ps[0:NQ, 0:HE], prT[:], v[:], start=True, stop=True)\
                          .then_inc(att_mm, 1)

                run(pe, body)

            @block.scalar
            def _(act):
                def evac(step, k, dst):
                    act.wait_ge(T_full, T_use(step, k) + 1)
                    nc.scalar.activation(dst[:, (k % 4) * GT:(k % 4 + 1) * GT], T_ps[k % 2][:, 0:GT], ACT.Copy)\
                      .then_inc(T_read, 1)

                def body(step):
                    if step.on(0):
                        for k in range(4):
                            evac(step, k, xsT)
                    if step.on(-1):
                        if step.reg is not None or step.place >= 0:
                            act.wait_ge(xs_ok, step.lin(1, 1))
                        nc.scalar.activation(xn[:], x_sb[:, bass.ds(step.lin(D, D), D)], ACT.Identity,
                                             bias=nmr[:, bass.ds(step.lin(1, 1), 1)],
                                             scale=rstd[:, bass.ds(step.lin(1, 1), 1)]).then_inc(xn_ok, 1)
                    if step.on(2):
                        for k in range(4, 6):
                            evac(step, k, mixT)
                    if step.on(1):
                        act.wait_ge(nmax_ok, step.lin(1))
                        if step.reg is not None or step.place >= 2:
                            act.wait_ge(rden_ok, step.lin(1, -1))
                        nc.scalar.activation(pr[:], masked[:], ACT.Exp, bias=nmax[:, 0:1],
                                             accum_out=den[:, 0:1]).then_inc(pr_ok, 1)
                        act.wait_ge(prT_full, step.lin(1))
                        nc.scalar.activation(prT[:], prT_ps[0:NQ, 0:NQ], ACT.Copy).then_inc(prT_out, 1)
                    if step.on(0):
                        act.wait_ge(v_mm, step.lin(1, 1))
                        if step.reg is not None or step.place >= 1:
                            act.wait_ge(att_mm, step.lin(1))
                        nc.scalar.activation(v[:], v_ps[0:NQ, 0:HE], ACT.Copy).then_inc(v_out, 1)

                run(act, body)

            @block.vector
            def _(dve):
                def body(step):
                    if step.on(1):
                        dve.wait_ge(sc_mm, step.lin(1))
                        nc.vector.scalar_tensor_tensor(masked[:], sc_ps[0:NQ, 0:NQ], HE ** -0.5, causal[:],
                                                       ALU.mult, ALU.add).then_inc(masked_ok, 1)
                        dve.wait_ge(masked_ok, step.lin(1))
                        nc.vector.tensor_reduce(nmax[:], masked[:], AX.X, ALU.max, negate=True)\
                          .then_inc(nmax_ok, 1)
                    if step.on(-1):
                        dve.wait_ge(xn_ok, step.lin(1, 2))
                        if step.reg is not None or step.place >= 0:
                            dve.wait_ge(T_full, T_use(step, 3) + 1)
                        nc.vector.tensor_tensor(
                            xs[:], xn[:].unsqueeze(1).to_broadcast([NQ, E, D]),
                            bc(rw[:, bass.ds(step.lin(1, 1), 1), :].rearrange("p o e -> p (o e)"), D), ALU.mult)\
                          .then_inc(xs_ok, 1)
                    if step.on(0):
                        dve.wait_ge(qk_mm, step.lin(1, 1))
                        nc.vector.tensor_copy(qT[:], qk_ps[0:HE, 0:NQ])
                        nc.vector.tensor_copy(kT[:], qk_ps[HE:2 * HE, 0:NQ]).then_inc(qk_out, 1)
                    if step.on(1):
                        dve.wait_ge(pr_ok, step.lin(1))
                        nc.vector.reciprocal(rden[:], den[:]).then_inc(rden_ok, 1)
                        dve.wait_ge(rden_ok, step.lin(1))
                        nc.vector.tensor_scalar(
                            rwd[:], rw[:, bass.ds(step.lin(1, -1), 1), :].rearrange("p o e -> p (o e)"),
                            rden[:, 0:1], None, ALU.mult).then_inc(rwd_ok, 1)
                    if step.on(2):
                        dve.wait_ge(out_mm, step.lin(1, -1))
                        xb = x_sb[:, bass.ds(step.lin(D, -2 * D), D)]
                        nc.vector.scalar_tensor_tensor(xb, out_ps[0:NQ, 0:D], tg[0:NQ, 2:3], xb, ALU.mult,
                                                       ALU.add).then_inc(x_ok, 1)
                    if step.on(1):
                        dve.wait_ge(rwd_ok, step.lin(1))
                        dve.wait_ge(att_mm, step.lin(1))
                        nc.vector.tensor_tensor(mixed[:], att_ps[0:NQ, 0:HE].unsqueeze(1).to_broadcast([NQ, E, HE]),
                                                bc(rwd[:], HE), ALU.mult).then_inc(mixed_ok, 1)

                run(dve, body)
    sem.clear()


def mixture_of_experts(nc, env, W, x_sb):
    gamma, beta, router, wgu, wdn, sgu, sdn = W
    E, F = 8, 512
    FC = F // P
    CHUNKS = [(E, 0)] + [(e, c) for e in range(E) for c in range(FC)]
    NC = len(CHUNKS)
    NB = 3
    BACK = 2
    assert NC % NB == 0
    ident, tg = env["ident"], env["tg"]
    sem = Semaphores(nc, "m")
    st = ExitStack()
    with st:
        sb = lambda name, shape, dt=F32: st.enter_context(nc.sbuf_tensor(f"{name}_m", shape, dt))
        wgu_sb, wdn_sb = sb("wgu", [D, E, 2 * F]), sb("wdn", [P, E, FC, D])
        sgu_sb, sdn_sb = sb("sgu", [D, 2 * P]), sb("sdn", [P, D])
        xT, comb = sb("xT", [D, TOK]), sb("comb", [NQ, B, E])
        w_in = sem("w_in")

        with ExitStack() as s1:
            sg_ = lambda name, shape, dt=F32: s1.enter_context(nc.sbuf_tensor(f"{name}_r", shape, dt))
            gb, rt = sg_("gb", [D, 2]), sg_("rt", [D, E])
            h = sg_("h", [NQ, B * D])
            stat, mv, rstd, nmr = sg_("stat", [NQ, B, 6]), sg_("mv", [NQ, B, 2]), sg_("rstd", [NQ, B]), sg_("nmr", [NQ, B])
            stat2, mv2, rstd2, nmr2 = (sg_("stat2", [NQ, B, 6]), sg_("mv2", [NQ, B, 2]), sg_("rstd2", [NQ, B]),
                                       sg_("nmr2", [NQ, B]))
            xn, xg = sg_("xn", [NQ, 2, G, D]), sg_("xg", [D, 2, GT])
            L, L2, cand, f1, f2 = (sg_(n, [NQ, B, E]) for n in ("L", "L2", "cand", "f1", "f2"))
            mx = sg_("mx", [NQ, B])
            desc_i, desc = sg_("desc_i", [NQ, E], mybir.dt.int32), sg_("desc", [NQ, E])
            xnT_ps = s1.enter_context(nc.psum_tensor("xnT_ps_r", [P, 2, 512], F32))
            log_ps = s1.enter_context(nc.psum_tensor("log_ps_r", [P, 2, 512], F32))
            small_in, iota_ok = sem("small_in"), sem("iota_ok")
            ln1 = [sem(n) for n in ("stats", "var_ok", "std_ok", "rstd_ok")]
            ln2 = [sem(n) for n in ("stats2", "var_ok2", "std_ok2", "rstd_ok2")]
            h_ok, ln_ok, ln_T, ln_T_out, xT_ok, logit_mm, logit_ok, pre_exp, gate_exp, chain = (
                sem(n) for n in ("h_ok", "ln_ok", "ln_T", "ln_T_out", "xT_ok", "logit_mm", "logit_ok", "pre_exp",
                                 "gate_exp", "chain"))

            with nc.Block() as block:
                @block.sync
                def _(sp):
                    for dst, src in ((gb[:, 0:1], gamma), (gb[:, 1:2], beta), (rt[:], router)):
                        sp.dma_start(dst, src).then_inc(small_in, 16)
                    sp.dma_start(sgu_sb[:], sgu).then_inc(w_in, 16)
                    sp.dma_start(sdn_sb[:], sdn).then_inc(w_in, 16)
                    sp.dma_start(wgu_sb[:], wgu.rearrange("e c f -> c e f")).then_inc(w_in, 16)
                    sp.dma_start(wdn_sb[:], wdn.rearrange("e (a f) c -> f e a c", a=FC)).then_inc(w_in, 16)
                    sp.wait_ge(w_in, 64)

                @block.gpsimd
                def _(pool):
                    nc.gpsimd.iota(desc_i[:], [[-1, E]], base=E, channel_multiplier=0).then_inc(iota_ok, 1)

                @block.scalar
                def _(act):
                    act.wait_ge(ln1[1], 1)
                    nc.scalar.activation(rstd[:], rstd[:], ACT.Sqrt).then_inc(ln1[2], 1)
                    act.wait_ge(ln1[3], 2)
                    with act.Fori(0, B // 4) as i:
                        for j in range(4):
                            at = bass.ds(i * (4 * D) + j * D, D)
                            nc.scalar.activation(h[:, at], x_sb[:, at], ACT.Identity,
                                                 bias=nmr[:, bass.ds(i * 4 + j, 1)],
                                                 scale=rstd[:, bass.ds(i * 4 + j, 1)]).then_inc(h_ok, 1)
                    act.wait_ge(ln2[1], 1)
                    nc.scalar.activation(rstd2[:], rstd2[:], ACT.Sqrt).then_inc(ln2[2], 1)
                    act.wait_ge(ln2[3], 2)
                    with act.Fori(0, NG // 2) as i:
                        for u in range(2):
                            n = 2 * i + u
                            act.wait_ge(ln_T, n + 1)
                            for j in range(G):
                                off = i * (2 * G) + (u * G + j)
                                nc.scalar.activation(
                                    xn[:, u, j, :], h[:, bass.ds(i * (2 * G * D) + (u * G + j) * D, D)],
                                    ACT.Identity, bias=nmr2[:, bass.ds(off, 1)],
                                    scale=rstd2[:, bass.ds(off, 1)]).then_inc(ln_ok, 1)
                            act.wait_ge(ln_T_out, n + 1)
                            nc.scalar.activation(xT[:, bass.ds(n * GT, GT)], xg[:, u, :], ACT.Copy)\
                              .then_inc(xT_ok, 1)
                    act.wait_ge(pre_exp, 1)
                    nc.scalar.activation(L[:], L[:], ACT.Exp).then_inc(gate_exp, 1)

                @block.tensor
                def _(pe):
                    pe.sem_inc(ln_T, 2)
                    pe.wait_ge(small_in, 48)
                    with pe.Fori(0, NG // 2) as i:
                        for u in range(2):
                            n = 2 * i + u
                            pe.wait_ge(ln_ok, i * (2 * G) + G * (u + 1))
                            for j in range(G):
                                last = nc.tensor.transpose(xnT_ps[:, u, j * NQ:(j + 1) * NQ], xn[:, u, j, :],
                                                           ident[0:NQ, 0:NQ])
                            last.then_inc(ln_T, 1)
                            pe.wait_ge(ln_T_out, n + 1)
                            for j in range(G):
                                last = nc.tensor.matmul(log_ps[0:NQ, u, j * E:(j + 1) * E],
                                                        xg[:, u, j * NQ:(j + 1) * NQ], rt[:], start=True, stop=True)
                            last.then_inc(logit_mm, 1)

                @block.vector
                def _(dve):
                    done = [0]

                    def link(ins):
                        done[0] += 1
                        ins.then_inc(chain, 1)
                        dve.wait_ge(chain, done[0])

                    dve.sem_inc(xT_ok, 2)
                    dve.wait_ge(iota_ok, 1)
                    link(nc.vector.tensor_copy(desc[:], desc_i[:]))
                    layer_norm_stats(nc, dve, None, lambda off: x_sb[:, bass.ds(off, D)], stat, mv, rstd, nmr, ln1)
                    dve.wait_ge(h_ok, B)
                    layer_norm_stats(nc, dve, None, lambda off: h[:, bass.ds(off, D)], stat2, mv2, rstd2, nmr2, ln2)
                    dve.wait_ge(small_in, 48)
                    Lf = L[:].rearrange("p b e -> p (b e)")
                    with dve.Fori(0, NG // 2) as i:
                        for u in range(2):
                            n = 2 * i + u
                            dve.wait_ge(ln_T, n + 3)
                            dve.wait_ge(xT_ok, n + 1)
                            nc.vector.tensor_scalar(xg[:, u, :], xnT_ps[:, u, 0:GT], gb[:, 0:1], gb[:, 1:2],
                                                    ALU.mult, ALU.add).then_inc(ln_T_out, 1)
                            dve.wait_ge(logit_mm, n + 1)
                            nc.vector.tensor_copy(Lf[:, bass.ds(n * (G * E), G * E)],
                                                  log_ps[0:NQ, u, 0:G * E]).then_inc(logit_ok, 1)
                    dve.wait_ge(logit_ok, NG)
                    link(nc.vector.tensor_reduce(mx[:], L[:], AX.X, ALU.max))
                    nc.vector.tensor_tensor(L[:], L[:], bc(mx[:], E), ALU.subtract).then_inc(pre_exp, 1)
                    dve.wait_ge(gate_exp, 1)
                    link(nc.vector.tensor_reduce(mx[:], L[:], AX.X, ALU.add))
                    link(nc.vector.reciprocal(mx[:], mx[:]))
                    link(nc.vector.tensor_tensor(L[:], L[:], bc(mx[:], E), ALU.mult))
                    link(nc.vector.tensor_reduce(mx[:], L[:], AX.X, ALU.max))
                    top_two(nc, link, L[:], L2[:], bm(desc[:], B), cand[:], f1[:], f2[:], mx[:], E)
                    link(nc.vector.tensor_tensor(L[:], L[:], f1[:], ALU.mult))
                    link(nc.vector.tensor_reduce(mx[:], L[:], AX.X, ALU.add))
                    link(nc.vector.reciprocal(mx[:], mx[:]))
                    link(nc.vector.tensor_tensor(comb[:], L[:], bc(mx[:], E), ALU.mult))

        xg, clip, silu, hT = (sb("xgm", [D, 2, GT]), sb("clip", [P, NB, GT]), sb("silu", [P, NB, GT]),
                              sb("hT", [P, NB, GT]))
        acc = sb("acc", [NQ, 2, G, D])
        gate_ps = st.enter_context(nc.psum_tensor("gate_ps", [P, NB, 512], F32))
        up_ps = st.enter_context(nc.psum_tensor("up_ps", [P, NB, 512], F32))
        down_ps = st.enter_context(nc.psum_tensor("down_ps", [P, 2, 512], F32))
        xg_ok, gate_mm, clip_ok, silu_ok, h_ok2, down_mm, acc_ok, group_ok, x_ok = (
            sem(n) for n in ("xg_ok", "gate_mm", "clip_ok", "silu_ok", "h_ok2", "down_mm", "acc_ok", "group_ok",
                             "x_ok"))
        EX = E + 1
        with nc.Block() as block:
            @block.tensor
            def _(pe):
                pe.sem_inc(h_ok2, NB)
                pe.sem_inc(acc_ok, 2)
                with pe.Fori(0, NG // 2) as i:
                    def gate_up(k):
                        u, (e, c) = k // NC, CHUNKS[k % NC]
                        pe.wait_ge(h_ok2, i * (2 * NC) + (k + 1))
                        w = sgu_sb if e == E else wgu_sb[:, e, :]
                        f = P if e == E else F
                        nc.tensor.matmul(gate_ps[:, k % NB, 0:GT], w[:, c * P:(c + 1) * P], xg[:, u, :],
                                         start=True, stop=True).then_inc(gate_mm, 1)
                        nc.tensor.matmul(up_ps[:, k % NB, 0:GT], w[:, f + c * P:f + (c + 1) * P], xg[:, u, :],
                                         start=True, stop=True).then_inc(gate_mm, 1)

                    def down(k):
                        u, (e, c) = k // NC, CHUNKS[k % NC]
                        x = u * EX + (0 if e == E else e + 1)
                        last_c = 0 if e == E else FC - 1
                        if c == 0:
                            pe.wait_ge(acc_ok, i * (2 * EX) + (x + 1))
                        pe.wait_ge(h_ok2, i * (2 * NC) + (k + 1 + NB))
                        for j in range(G):
                            last = nc.tensor.matmul(down_ps[0:NQ, x % 2, j * D:(j + 1) * D],
                                                    hT[:, k % NB, j * NQ:(j + 1) * NQ],
                                                    sdn_sb[:] if e == E else wdn_sb[:, e, c, :],
                                                    start=(c == 0 and j == 0), stop=(c == last_c),
                                                    skip_group_check=True)
                        if c == last_c:
                            last.then_inc(down_mm, 1)

                    for k in range(2 * NC + BACK):
                        if k < 2 * NC:
                            if k % NC == 0:
                                pe.wait_ge(xg_ok, 2 * i + (k // NC + 1))
                            gate_up(k)
                        if k >= BACK:
                            down(k - BACK)

            @block.scalar
            def _(act):
                with act.Fori(0, NG // 2) as i:
                    for u in range(2):
                        nc.scalar.activation(xg[:, u, :], xT[:, bass.ds(i * (2 * GT) + u * GT, GT)], ACT.Copy)\
                          .then_inc(xg_ok, 1)
                    for k in range(2 * NC):
                        act.wait_ge(clip_ok, i * (2 * NC) + (k + 1))
                        nc.scalar.activation(silu[:, k % NB, :], clip[:, k % NB, :], ACT.Silu).then_inc(silu_ok, 1)
                    act.wait_ge(gate_mm, i * (4 * NC) + 4 * NC)

            @block.vector
            def _(dve):
                with dve.Fori(0, NG // 2) as i:
                    def clipped(k):
                        dve.wait_ge(gate_mm, i * (4 * NC) + (2 * k + 1))
                        nc.vector.tensor_scalar(clip[:, k % NB, :], gate_ps[:, k % NB, 0:GT], -10.0, 10.0, ALU.max,
                                                ALU.min).then_inc(clip_ok, 1)

                    def hidden(k):
                        dve.wait_ge(gate_mm, i * (4 * NC) + (2 * k + 2))
                        dve.wait_ge(silu_ok, i * (2 * NC) + (k + 1))
                        nc.vector.tensor_tensor(hT[:, k % NB, :], silu[:, k % NB, :], up_ps[:, k % NB, 0:GT],
                                                ALU.mult).then_inc(h_ok2, 1)

                    def accumulate(x):
                        u, e = x // EX, x % EX - 1
                        dve.wait_ge(down_mm, i * (2 * EX) + (x + 1))
                        if e < 0:
                            nc.vector.tensor_copy(acc[:, u].rearrange("p j d -> p (j d)"), down_ps[0:NQ, x % 2, :])\
                              .then_inc(acc_ok, 1)
                        else:
                            dve.wait_ge(acc_ok, i * (2 * EX) + (x + 2))
                            for j in range(G):
                                w = comb[:, bass.ds(i * (2 * G) + (u * G + j), 1), e]
                                last = nc.vector.scalar_tensor_tensor(
                                    acc[:, u, j, :], down_ps[0:NQ, x % 2, j * D:(j + 1) * D], w, acc[:, u, j, :],
                                    ALU.mult, ALU.add)
                            last.then_inc(acc_ok, 1)
                        if e == E - 1:
                            dve.wait_ge(acc_ok, i * (2 * EX) + (x + 3))
                            xb = x_sb[:, bass.ds(i * (2 * G * D) + u * (G * D), G * D)]
                            nc.vector.scalar_tensor_tensor(xb, acc[:, u].rearrange("p j d -> p (j d)"),
                                                           tg[0:NQ, 3:4], xb, ALU.mult, ALU.add).then_inc(x_ok, 1)

                    ends = {}
                    for x in range(2 * EX):
                        u, e = x // EX, x % EX - 1
                        ends[u * NC + (0 if e < 0 else 1 + e * FC + FC - 1)] = x
                    for k in range(2 * NC + BACK + 1):
                        if k < 2 * NC:
                            clipped(k)
                        if 1 <= k <= 2 * NC:
                            hidden(k - 1)
                        if k - BACK - 1 in ends:
                            accumulate(ends[k - BACK - 1])
    sem.clear()


def build(nc, x, ctxT, g_xattn, g_ffn, layers, out, ffn0=None, ffn1=None):
    ctx = ExitStack()
    with ctx:
        sb = lambda name, shape, dt=F32: ctx.enter_context(nc.sbuf_tensor(name, shape, dt))
        sem = lambda name: ctx.enter_context(nc.semaphore(name))
        env = {"ctx": ctx}
        x_sb = sb("x_sb", [NQ, B * D])
        ident = env["ident"] = sb("ident", [P, P])
        gates = sb("gates", [P, 4])
        tg = env["tg"] = sb("tg", [P, 4])
        x_in, g_in, ident_ok, tanh_ok, packs_ok = (
            sem(n) for n in ("x_in", "g_in", "ident_ok", "tanh_ok", "packs_ok"))
        env["ident_ok"] = ident_ok
        kscr = nc.dram_tensor("kscr", (3, 3, P, NK), BF16).ap()
        qscr = nc.dram_tensor("qscr", (3, P, TOK), BF16).ap()
        mscr = nc.dram_tensor("mscr", (3, SH, H, NQ), BF16).ap()

        with ExitStack() as packs:
            env["Kp"] = packs.enter_context(nc.sbuf_tensor("Kp", [P, 3, PAIRS, NK], BF16))
            env["Qp"] = packs.enter_context(nc.sbuf_tensor("Qp", [P, 3, H * NQ], BF16))
            env["V"] = packs.enter_context(nc.sbuf_tensor("V", [P, 3, KT, H, HD + 1], F32))

            with nc.Block() as block:
                @block.sync
                def _(sp):
                    sp.dma_start(x_sb[:].rearrange("q (b d) -> q b d", b=B), x.rearrange("b q d -> q b d"))\
                      .then_inc(x_in, 16)
                    for i, g in enumerate((g_xattn, g_ffn)):
                        sp.dma_start(gates[:, 2 * i:2 * i + 2], g.partition_broadcast(P)).then_inc(g_in, 16)
                    sp.wait_ge(x_in, 16)

                @block.scalar
                def _(act):
                    act.wait_ge(g_in, 32)
                    nc.scalar.activation(tg[:], gates[:], ACT.Tanh).then_inc(tanh_ok, 1)

                @block.gpsimd
                def _(pool):
                    nc.gpsimd.memset(ident[:], 0.0).then_inc(ident_ok, 1)
                    pool.wait_ge(ident_ok, 1)
                    nc.gpsimd.affine_select(out=ident[:], in_=ident[:], compare_op=ALU.not_equal, fill=1.0, base=0,
                                            pattern=[[-1, P]], channel_multiplier=1).then_inc(ident_ok, 1)
                    pool.wait_ge(ident_ok, 2)
                    nc.gpsimd.memset(env["Kp"][ROWS:P, :, :, :], 1.0).then_inc(packs_ok, 1)

                @block.vector
                def _(dve):
                    nc.vector.memset(env["Qp"][:], 0.0).then_inc(packs_ok, 1)
                    nc.vector.memset(env["V"][:], 1.0).then_inc(packs_ok, 1)

            scr = (kscr, qscr, mscr)
            attention(nc, env, 0, (ctxT, *layers[0]), scr, x_sb)
            if ffn0:
                expert_attention(nc, env, ffn0, x_sb)
            if len(layers) > 1:
                attention(nc, env, 1, (ctxT, *layers[1]), scr, x_sb)

        if ffn1:
            mixture_of_experts(nc, env, ffn1, x_sb)
        out_done = sem("out_done")
        with nc.Block() as block:
            @block.sync
            def _(sp):
                sp.dma_start(out.rearrange("b q d -> q b d"), x_sb[:].rearrange("q (b d) -> q b d", b=B))\
                  .then_inc(out_done, 16)
                sp.wait_ge(out_done, 16)


def kernel(**inputs):
    import concourse.bacc as bacc
    from concourse.bass_utils import run_bass_kernel_spmd

    def paired(w):
        w = w.reshape(-1, PAIRS, 2, HD)
        return w.transpose(0, 2, 3, 1).reshape(w.shape[0], D)

    a = {name: np.asarray(v) for name, v in inputs.items()}
    kv_w, kv_b = a["L1_xattn_kv_w"], a["L1_xattn_kv_b"]
    laid = {
        "x": a["x"],
        "ctxT": a["ctx_768"].transpose(0, 2, 1).reshape(B * DC, NK),
        "g_xattn": a["g_xattn"], "g_ffn": a["g_ffn"],
    }
    for lay, (wq, bq, wk, bk, wv, bv, wo, bo) in enumerate((
            tuple(a[f"L0_xattn_{n}"] for n in ("Wq", "bq", "Wk", "bk", "Wv", "bv", "Wo", "bo")),
            (a["L1_xattn_q_w"], a["L1_xattn_q_b"], kv_w[:, :D], kv_b[:D], kv_w[:, D:], kv_b[D:],
             a["L1_xattn_proj_w"], a["L1_xattn_proj_b"]))):
        for name, v in (("wq", paired(wq)), ("bq", paired(bq).reshape(D, 1)), ("wk", paired(wk)),
                        ("bk", paired(bk).reshape(D, 1)), ("wv", wv), ("bv", bv), ("wo", wo), ("bo", bo)):
            laid[f"a{lay}_{name}"] = v
    laid["f0_sim"], laid["f0_gates"] = a["L0_ffn_sim_matrix"], a["L0_ffn_gates"]
    laid["f0_wqk"] = np.concatenate([a["L0_ffn_q_proj"], a["L0_ffn_k_proj"]], axis=-1).transpose(1, 0, 2)
    laid["f0_wv"] = a["L0_ffn_v_proj"].transpose(1, 0, 2)
    laid["f0_wo"] = a["L0_ffn_o_proj"].reshape(-1, P, D).transpose(1, 0, 2)
    laid["f1_gamma"], laid["f1_beta"] = a["L1_ffn_ln_gamma"].reshape(D, 1), a["L1_ffn_ln_beta"].reshape(D, 1)
    laid["f1_router"], laid["f1_wgu"], laid["f1_wdn"] = (
        a["L1_ffn_router_w"], a["L1_ffn_gate_up_w"], a["L1_ffn_down_w"])
    laid["f1_sgu"], laid["f1_sdn"] = a["L1_ffn_shared_gate_up_w"], a["L1_ffn_shared_down_w"]

    nc = bacc.Bacc("TRN2", target_bir_lowering=False, num_devices=1)
    arrays, ap = {}, {}
    for name, v in laid.items():
        v = np.ascontiguousarray(v)
        arrays[f"in_{name}"] = v
        ap[name] = nc.dram_tensor(f"in_{name}", v.shape, mybir.dt.from_np(v.dtype), kind="ExternalInput").ap()
    out = nc.dram_tensor("out_0", (B, NQ, D), F32, kind="ExternalOutput").ap()
    group = lambda p: [ap[n] for n in laid if n.startswith(p)]
    build(nc, ap["x"], ap["ctxT"], ap["g_xattn"], ap["g_ffn"], [group("a0_"), group("a1_")], out,
          group("f0_"), group("f1_"))
    return run_bass_kernel_spmd(nc, [arrays], core_ids=[0]).results[0]["out_0"]
```

```python
from contextlib import ExitStack

import numpy as np

import concourse.bass as bass
from concourse import mybir

F32, BF16 = mybir.dt.float32, mybir.dt.bfloat16
ALU, ACT, AX = mybir.AluOpType, mybir.ActivationFunctionType, mybir.AxisListType

B, NQ, D = 32, 100, 128
NK, DC = 1444, 96
H = 16
HD = D // H
TOK = B * NQ
G = 4
NG, GT = B // G, G * NQ
P = 128
EPS = 1e-5

KT = -(-NK // P)
KFULL = KT - 2
KW = [P] * KFULL + [(NK - P * KFULL) // 2] * 2
KS = [sum(KW[:t]) for t in range(KT)]
assert sum(KW) == NK
PAIRS = H // 2
TERMS = [0, 0, 0, 1, 1, 2]
QTERMS = [0, 1, 2, 0, 1, 0]
ROWS = len(TERMS) * 2 * HD
SH = 3
QUADS = H // 4
QW = 4 * NQ
UNITS = KT * QUADS
CUT = [0, 482, 963, NK]
NTH = len(CUT) - 1
VS = KT // 2
LAG = 3
NE, NP_ = 3, 6


class Semaphores:

    def __init__(self, nc, suffix):
        self.nc, self.suffix, self.held = nc, suffix, []

    def __call__(self, name):
        self.held.append(self.nc.alloc_semaphore(name=f"{name}_{self.suffix}"))
        return self.held[-1]

    def clear(self):
        self.nc.clear_and_free_semaphores(self.held)
        self.nc.all_engine_barrier()


class Step:

    def __init__(self, place, reg=None):
        self.place, self.reg = place, reg

    def lin(self, mult, off=0):
        if self.reg is None:
            return mult * self.place + off
        return self.reg * (3 * mult) + (mult * (1 + self.place) + off)

    def mod3(self, off=0):
        return (self.place + off + (0 if self.reg is None else 1)) % 3

    def has_prep(self):
        return self.reg is not None or -2 <= self.place <= B - 3

    def has_max(self):
        return self.reg is not None or -1 <= self.place <= B - 2

    def has_main(self):
        return self.reg is not None or 0 <= self.place <= B - 1

    def has_final(self):
        return self.reg is not None or 1 <= self.place <= B


LOOPS = 9
HEAD_STEPS = [Step(b) for b in (-2, -1, 0)]
TAIL_STEPS = [Step(b) for b in range(3 * LOOPS + 1, B + 1)]

NSLOT = 4
MAXES = NTH * H
EARLY = 10
M_END = 36


OTHERS = ((2, ("K", 0)), (5, ("K", 1)), (8, ("K", 2)), (10, ("O", 0)), (13, ("A", 0)), (17, ("W", 0)),
          (20, ("V", 0)), (24, ("V", 1)), (28, ("V", 2)), (32, ("V", 3)), (36, ("V", 4)), (40, ("V", 5)))
T_AT = M_END + 3


def _slot_users():
    late = MAXES - EARLY
    users = [(2 + n * (M_END - 2) // (late - 1), ("M", EARLY + n)) for n in range(late)]
    users += [(T_AT + 1 + n * (UNITS - 1 - T_AT) // EARLY, ("N", n)) for n in range(EARLY)]
    users = sorted([*users, *OTHERS, (T_AT, ("T", 0))], key=lambda u: u[0])
    return [(*user, at) for at, user in users]


USERS = _slot_users()
DVE_USERS = [u for u in USERS if u[0] != "K"]
for _u in (u for u in USERS if u[0] == "K"):
    DVE_USERS.insert(USERS.index(_u) + 3, _u)
SLOT = {(k, i): n % NSLOT for n, (k, i, _) in enumerate(USERS)}
PER_STEP = [sum(v == n for v in SLOT.values()) for n in range(NSLOT)]


def _present(step, kind):
    return {"K": step.has_prep, "V": step.has_prep, "N": step.has_prep, "M": step.has_max, "T": step.has_max,
            "O": step.has_final, "A": step.has_final, "W": step.has_final}[kind]()


def _uses(place, slot):
    step = Step(place)
    return sum(_present(step, k) and SLOT[k, i] == slot for k, i, _ in USERS)


def slot_count(step, kind, idx):
    slot = SLOT[kind, idx]
    rank = 0
    for k, i, _ in USERS:
        if SLOT[k, i] == slot and _present(step, k):
            rank += 1
        if (k, i) == (kind, idx):
            break
    if step.reg is None:
        return sum(_uses(p, slot) for p in range(-2, step.place)) + rank
    return step.lin(PER_STEP[slot], sum(_uses(p, slot) for p in range(-2, 1)) - PER_STEP[slot] + rank)


def attention(nc, env, lay, W, scr, x_sb):
    (ctxT, wq, bq, wk, bk, wv, bv, wo, bo) = W
    kscr, qscr, mscr = scr
    ident, tg = env["ident"], env["tg"]

    sem = Semaphores(nc, f"a{lay}")
    st = ExitStack()
    with st:
        sb = lambda name, shape, dt=F32: st.enter_context(nc.sbuf_tensor(f"{name}{lay}", shape, dt))

        wq_sb, bq_sb = sb("wq", [D, D]), sb("bq", [D, 1])
        wk_sb, bk_sb, wv_sb = sb("wk", [DC, D]), sb("bk", [D, 1]), sb("wv", [DC, D])
        bv_sb, wo_sb, bo_sb = sb("bv", [NQ, D]), sb("wo", [D, D]), sb("bo", [NQ, D])

        stat, mv = sb("stat", [NQ, B, 6]), sb("mv", [NQ, B, 2])
        rstd, nmr = sb("rstd", [NQ, B]), sb("nmr", [NQ, B])
        xn, xnT = sb("xn", [NQ, 2, G, D]), sb("xnT", [D, 2, GT])
        q32, qr = sb("q32", [D, GT]), sb("qr", [D, GT])
        qs = sb("qs", [D, 3, 2, GT], BF16)
        w_in, stats, var_ok, std_ok, rstd_ok = (sem(n) for n in ("w_in", "stats", "var_ok", "std_ok", "rstd_ok"))
        ln_ok, ln_T, ln_T_out, q_mm = (sem(n) for n in ("ln_ok", "ln_T", "ln_T_out", "q_mm"))
        q_full, q_hi, q_res, q_mid, q_split = (sem(n) for n in ("q_full", "q_hi", "q_res", "q_mid", "q_split"))
        q_out = [sem(f"q_out{u}_") for u in range(2)]

        ctx_sb = sb("ctx", [DC, 3, NK])
        k32, kr = sb("k32", [D, NK]), sb("kr", [D, NK])
        ks = sb("ks", [D, 3, NK], BF16)
        Kp, Qp, V = env["Kp"], env["Qp"], env["V"]
        probs = sb("probs", [P, NP_, QW])
        mx, mmax = sb("mx", [NQ, NTH, H]), sb("mmax", [NQ, H])
        mr = sb("mr", [H, NQ])
        mT = sb("mT", [H, 3, NQ], BF16)
        oT = sb("oT", [P, QW])
        rden, heads = sb("rden", [NQ, H]), sb("heads", [NQ, D])
        headsT, gated = sb("headsT", [D, NQ]), sb("gated", [NQ, D])

        pb = lambda name, shape: st.enter_context(nc.psum_tensor(f"{name}{lay}", shape, F32))
        slots = [pb(f"slot{n}_", [P, 512]) for n in range(NSLOT)]
        scores, o_ps = pb("scores", [P, NE, 512]), pb("o_ps", [P, 512])

        slot_full = [sem(f"slot{n}_full") for n in range(NSLOT)]
        slot_read = [sem(f"slot{n}_read") for n in range(NSLOT)]
        ctx_in = [sem(f"ctx_in{i}_") for i in range(3)]
        pack_in = [sem(f"pack_in{i}_") for i in range(3)]
        shift_in = [sem(f"shift_in{i}_") for i in range(3)]
        init, k_evac, k_res, k_split, k_out = (sem(n) for n in ("init", "k_evac", "k_res", "k_split", "k_out"))
        scored, exped, pv_done, o_evac = (sem(n) for n in ("scored", "exped", "pv_done", "o_evac"))
        m_ready, m_hi, m_res, m_mid, m_split, m_out = (
            sem(n) for n in ("m_ready", "m_hi", "m_res", "m_mid", "m_split", "m_out"))
        den_ok, heads_mul, heads_ok, headsT_ok, wo_bias, x_ok = (
            sem(n) for n in ("den_ok", "heads_mul", "heads_ok", "headsT_ok", "wo_bias", "x_ok"))

        def user_wait(eng, sems, step, kind, idx):
            eng.wait_ge(sems[SLOT[kind, idx]], slot_count(step, kind, idx))

        def users_at(step, s):
            return [(k, i) for k, i, at in USERS if at == s and _present(step, k)]

        xnT_ps = [scores[:, 0], scores[:, 1]]
        q_ps = [scores[:, 2], o_ps[:]]

        def groups(eng, ahead, behind):
            ahead(0, 0)
            with eng.Fori(0, NG // 2 - 1) as i:
                for u in range(2):
                    ahead(2 * i + (u + 1), 1 - u)
                    behind(2 * i + u, u)
            ahead(NG - 1, 1)
            behind(NG - 2, 0)
            behind(NG - 1, 1)

        def run(eng, body):
            for step in HEAD_STEPS:
                body(step)
            with eng.Fori(0, LOOPS) as i:
                for u in range(3):
                    body(Step(u, i))
            for step in TAIL_STEPS:
                body(step)

        def at_batch(step, off):
            return step.lin(1, off)

        with nc.Block() as block:
            @block.sync
            def _(sp):
                def pack_k(step):
                    nb = step.mod3(2)
                    sp.wait_ge(k_split, step.lin(NTH, 3 * NTH))
                    sp.dma_start(kscr[nb].rearrange("t p n -> p t n"), ks[:]).then_inc(k_out, 16)
                    sp.wait_ge(k_out, step.lin(16, 3 * 16))
                    for t, part in enumerate(TERMS):
                        r = 2 * t * HD
                        sp.dma_start(Kp[r:r + 2 * HD, nb, :, :],
                                     kscr[nb, part].rearrange("(r g) n -> r g n", g=PAIRS))\
                          .then_inc(pack_in[nb], 16)

                def pack_q(step, terms=range(len(QTERMS))):
                    nb = step.mod3(2)
                    for t in terms:
                        part = QTERMS[t]
                        for hh in range(2):
                            r = (2 * t + hh) * HD
                            src = qscr[part, hh * 64:(hh + 1) * 64, bass.ds(step.lin(NQ, 2 * NQ), NQ)]
                            dst = Qp[r:r + HD, nb, :].rearrange("d (g a c) -> d g a c", g=PAIRS, a=2)
                            sp.dma_start(dst[:, :, hh, :], src.rearrange("(d g) c -> d g c", g=PAIRS))\
                              .then_inc(pack_in[nb], 16)

                def write_queries(n, u):
                    sp.wait_ge(q_split, n + 1)
                    sp.dma_start(qscr[:, :, bass.ds(n * GT, GT)].rearrange("t p c -> p t c"), qs[:, :, u, :])\
                      .then_inc(q_out[u], 16)

                def body(step):
                    if step.reg is not None or -2 <= step.place <= B - 4:
                        nb = step.mod3(3)
                        if step.reg is not None or step.place >= 1:
                            sp.wait_ge(scored, step.lin(UNITS))
                        elif step.place == 0:
                            user_wait(sp, slot_full, Step(-2), "V", VS - 1)
                        sp.dma_start(ctx_sb[:, nb, :], ctxT[bass.ds(step.lin(DC, 3 * DC), DC), :])\
                          .then_inc(ctx_in[nb], 16)
                    if step.reg is None and step.place == -2:
                        pack_k(step)
                        write_queries(0, 0)
                        sp.wait_ge(q_out[0], 16)
                        for n in (1, 2, 3):
                            write_queries(n, n % 2)
                            pack_q(step, range(2 * n - 2, 2 * n))
                        with sp.Fori(2, NG // 2) as i:
                            for u in range(2):
                                write_queries(2 * i + u, u)
                    elif step.has_prep():
                        if step.reg is None and step.place == 0:
                            for u in range(2):
                                sp.wait_ge(q_out[u], 16 * (NG // 2))
                        if step.reg is not None or step.place >= 1:
                            sp.wait_ge(scored, step.lin(UNITS))
                        pack_q(step)
                        pack_k(step)
                    if step.has_max():
                        nb = step.mod3(1)
                        sp.wait_ge(m_split, step.lin(1, 2))
                        sp.dma_start(mscr[nb].rearrange("t h c -> h t c"), mT[:]).then_inc(m_out, 16)
                        sp.wait_ge(m_out, step.lin(16, 2 * 16))
                        sp.dma_start(Qp[ROWS:ROWS + SH, nb, :], mscr[nb].rearrange("t h c -> t (h c)"))\
                          .then_inc(shift_in[nb], 16)

                sp.dma_start(ctx_sb[:, 0, :], ctxT[0:DC, :]).then_inc(ctx_in[0], 16)
                for dst, src in ((wk_sb, wk), (bk_sb, bk), (wv_sb, wv), (wq_sb, wq), (bq_sb, bq), (wo_sb, wo)):
                    sp.dma_start(dst[:], src).then_inc(w_in, 16)
                sp.dma_start(bv_sb[:], bv.partition_broadcast(NQ)).then_inc(w_in, 16)
                sp.dma_start(bo_sb[:], bo.partition_broadcast(NQ)).then_inc(w_in, 16)
                run(sp, body)

            @block.gpsimd
            def _(pool):
                def body(step):
                    if step.has_prep():
                        for i in range(NTH):
                            third = slice(CUT[i], CUT[i + 1])
                            pool.wait_ge(k_evac, step.lin(NTH, 2 * NTH + i + 1))
                            nc.gpsimd.tensor_tensor(kr[:, third], k32[:, third], ks[:, 0, third],
                                                    ALU.subtract).then_inc(k_res, 1)
                            nc.gpsimd.tensor_tensor(ks[:, 1, third], k32[:, third], ks[:, 0, third],
                                                    ALU.subtract).then_inc(k_res, 1)
                            pool.wait_ge(k_res, step.lin(2 * NTH, 4 * NTH + 2 * (i + 1)))
                            nc.gpsimd.tensor_tensor(ks[:, 2, third], kr[:, third], ks[:, 1, third],
                                                    ALU.subtract).then_inc(k_split, 1)

                run(pool, body)

            @block.scalar
            def _(act):
                def evac_k(step, i):
                    if i == 0 and (step.reg is not None or step.place >= -1):
                        act.wait_ge(k_split, step.lin(NTH, 2 * NTH))
                    user_wait(act, slot_full, step, "K", i)
                    nc.scalar.activation(k32[:, CUT[i]:CUT[i + 1]], slots[SLOT["K", i]][:, 0:CUT[i + 1] - CUT[i]],
                                         ACT.Identity, bias=bk_sb[:, 0:1]).then_inc(slot_read[SLOT["K", i]], 1)

                def evac_v(step, i):
                    nb, slot = step.mod3(2), SLOT["V", i]
                    if i == 0 and (step.reg is not None or step.place >= 1):
                        act.wait_ge(pv_done, step.lin(UNITS))
                    user_wait(act, slot_full, step, "V", i)
                    w = KW[2 * i]
                    src = slots[slot][0:w, 0:2 * D].rearrange("p (t h d) -> p t h d", t=2, h=H)
                    nc.scalar.activation(V[0:w, nb, 2 * i:2 * i + 2, :, 0:HD], src, ACT.Copy)\
                      .then_inc(slot_read[slot], 1)

                def normalise(n, u):
                    act.wait_ge(ln_T, n + 1)
                    for j in range(G):
                        nc.scalar.activation(xn[:, u, j, :], x_sb[:, bass.ds(n * (G * D) + j * D, D)], ACT.Identity,
                                             bias=nmr[:, bass.ds(n * G + j, 1)],
                                             scale=rstd[:, bass.ds(n * G + j, 1)]).then_inc(ln_ok, 1)

                def evac_transposes(n, u):
                    act.wait_ge(ln_T, n + 3)
                    nc.scalar.activation(xnT[:, u, :], xnT_ps[u][:, 0:GT], ACT.Copy).then_inc(ln_T_out, 1)

                def queries():
                    act.wait_ge(var_ok, 1)
                    nc.scalar.activation(rstd[:], rstd[:], ACT.Sqrt).then_inc(std_ok, 1)
                    act.wait_ge(rstd_ok, 2)
                    groups(act, normalise, evac_transposes)

                def body(step):
                    for s in range(UNITS):
                        if step.reg is None and step.place == -2 and s == T_AT + 1:
                            queries()
                        if step.has_main():
                            w = KW[s // QUADS]
                            act.wait_ge(scored, step.lin(UNITS, s + 1))
                            if step.reg is not None or UNITS * step.place + s >= NP_:
                                act.wait_ge(pv_done, step.lin(UNITS, s - NP_ + 1))
                            nc.scalar.activation(probs[0:w, s % NP_, :], scores[0:w, s % NE, 0:QW], ACT.Exp)\
                              .then_inc(exped, 1)
                        if s == LAG - 1 and step.has_final():
                            act.wait_ge(pv_done, step.lin(UNITS))
                            nc.scalar.activation(oT[:], o_ps[:, 0:QW], ACT.Copy).then_inc(o_evac, 1)
                        for kind, i in users_at(step, s):
                            if kind == "K":
                                evac_k(step, i)
                            elif kind == "V":
                                evac_v(step, i)

                act.wait_ge(w_in, 16 * 8)
                run(act, body)

            @block.vector
            def _(dve):
                def high_part(step, i):
                    if i == 0 and (step.reg is not None or step.place >= -1):
                        dve.wait_ge(k_out, step.lin(16, 2 * 16))
                    user_wait(dve, slot_read, step, "K", i)
                    cols = slice(CUT[i], CUT[i + 1])
                    nc.vector.tensor_copy(ks[:, 0, cols], k32[:, cols]).then_inc(k_evac, 1)

                def split_queries(n, u):
                    dve.wait_ge(q_mm, n + 1)
                    nc.vector.tensor_scalar(q32[:], q_ps[u][:, 0:GT], bq_sb[:, 0:1], HD ** -0.5, ALU.add,
                                            ALU.mult).then_inc(q_full, 1)
                    dve.wait_ge(q_full, n + 3)
                    part = [qs[:, t, u, :] for t in range(3)]
                    nc.vector.tensor_copy(part[0], q32[:]).then_inc(q_hi, 1)
                    dve.wait_ge(q_hi, n + 1)
                    nc.vector.tensor_tensor(qr[:], q32[:], part[0], ALU.subtract).then_inc(q_res, 1)
                    dve.wait_ge(q_res, n + 1)
                    nc.vector.tensor_copy(part[1], qr[:]).then_inc(q_mid, 1)
                    dve.wait_ge(q_mid, n + 1)
                    nc.vector.tensor_tensor(part[2], qr[:], part[1], ALU.subtract).then_inc(q_split, 1)

                def queries():
                    for b in range(B):
                        nc.vector.bn_aggr(mv[:, b, :], stat[:, b, :]).then_inc(stats, 1)
                    dve.wait_ge(stats, 2 * B)
                    nc.vector.tensor_scalar_add(rstd[:], mv[:, :, 1], EPS).then_inc(var_ok, 1)
                    dve.wait_ge(std_ok, 1)
                    nc.vector.reciprocal(rstd[:], rstd[:]).then_inc(rstd_ok, 1)
                    dve.wait_ge(rstd_ok, 1)
                    nc.vector.scalar_tensor_tensor(nmr[:], mv[:, :, 0], -1.0, rstd[:], ALU.mult,
                                                   ALU.mult).then_inc(rstd_ok, 1)
                    dve.wait_ge(w_in, 16 * 8)
                    for u in range(2):
                        split_queries(u, u)
                    with dve.Fori(1, NG // 2) as i:
                        for u in range(2):
                            dve.wait_ge(q_out[u], i * 16)
                            split_queries(2 * i + u, u)
                    nc.vector.memset(o_ps[:], 0.0).then_inc(init, 1)

                def body(step):
                    for kind, i, _ in DVE_USERS:
                        if step.reg is None and step.place == -2 and (kind, i) == ("N", 0):
                            queries()
                        if kind == "V" or not _present(step, kind):
                            continue
                        if kind == "K":
                            high_part(step, i)
                            continue
                        slot = slots[SLOT[kind, i]]
                        user_wait(dve, slot_full, step, kind, i)
                        freed = slot_read[SLOT[kind, i]]
                        if kind in "MN":
                            nc.vector.tensor_reduce(mx[:, i % NTH, i // NTH:i // NTH + 1],
                                                    slot[0:NQ, 0:CUT[i % NTH + 1] - CUT[i % NTH]], AX.X,
                                                    ALU.max).then_inc(freed, 1)
                            if i == MAXES - 1:
                                user_wait(dve, slot_read, step, "M", i)
                                nc.vector.tensor_reduce(mmax[:], mx[:].rearrange("c t h -> c h t"), AX.X,
                                                        ALU.max).then_inc(m_ready, 1)
                        elif kind == "T":
                            mps = slot[0:H, 0:NQ]
                            if step.reg is not None or step.place >= 0:
                                dve.wait_ge(m_out, step.lin(16, 16))
                            nc.vector.tensor_scalar_mul(mT[:, 0, :], mps, -1.0).then_inc(m_hi, 1)
                            dve.wait_ge(m_hi, step.lin(1, 2))
                            nc.vector.scalar_tensor_tensor(mr[:], mps, -1.0, mT[:, 0, :], ALU.mult,
                                                           ALU.subtract).then_inc(freed, 1)
                            user_wait(dve, slot_read, step, "T", 0)
                            nc.vector.tensor_copy(mT[:, 1, :], mr[:]).then_inc(m_mid, 1)
                            dve.wait_ge(m_mid, step.lin(1, 2))
                            nc.vector.tensor_tensor(mT[:, 2, :], mr[:], mT[:, 1, :], ALU.subtract)\
                              .then_inc(m_split, 1)
                        elif kind == "O":
                            ov = slot[0:NQ, :].rearrange("c (h e) -> c h e", h=H)
                            nc.vector.reciprocal(rden[:], ov[:, :, HD]).then_inc(den_ok, 1)
                            dve.wait_ge(den_ok, at_batch(step, 0))
                            hv = heads[:].rearrange("c (h d) -> c h d", h=H)
                            nc.vector.tensor_tensor(hv, ov[:, :, 0:HD],
                                                    rden[:].unsqueeze(2).to_broadcast([NQ, H, HD]), ALU.mult)\
                              .then_inc(freed, 1)
                            user_wait(dve, slot_read, step, "O", 0)
                            nc.vector.tensor_tensor(heads[:], heads[:], bv_sb[:], ALU.add).then_inc(heads_ok, 1)
                        elif kind == "A":
                            nc.vector.tensor_copy(headsT[:], slot[:, 0:NQ]).then_inc(freed, 1)
                        elif kind == "W":
                            nc.vector.tensor_tensor(gated[:], slot[0:NQ, 0:D], bo_sb[:], ALU.add)\
                              .then_inc(freed, 1)
                            user_wait(dve, slot_read, step, "W", 0)
                            xb = x_sb[:, bass.ds(step.lin(D, -D), D)]
                            nc.vector.scalar_tensor_tensor(xb, gated[:], tg[0:NQ, lay:lay + 1], xb, ALU.mult,
                                                           ALU.add).then_inc(x_ok, 1)

                dve.wait_ge(env["x_in"], 16)
                with dve.Fori(0, B // 8) as i:
                    for j in range(8):
                        nc.vector.bn_stats(stat[:, bass.ds(i * 8 + j, 1), :].rearrange("p o s -> p (o s)"),
                                           x_sb[:, bass.ds(i * (8 * D) + j * D, D)]).then_inc(stats, 1)
                dve.wait_ge(stats, B)
                run(dve, body)

            @block.tensor
            def _(pe):
                def project_k(step, i):
                    nb = step.mod3(2)
                    if i == 0:
                        pe.wait_ge(ctx_in[nb], third(step, 2, 16))
                    return nc.tensor.matmul(slots[SLOT["K", i]][:, 0:CUT[i + 1] - CUT[i]], wk_sb[:],
                                            ctx_sb[:, nb, CUT[i]:CUT[i + 1]], start=True, stop=True)

                def project_v(step, i):
                    nb, slot = step.mod3(2), slots[SLOT["V", i]]
                    for n in range(2 * i, 2 * i + 2):
                        c = (n % 2) * D
                        last = nc.tensor.matmul(slot[0:KW[n], c:c + D], ctx_sb[:, nb, KS[n]:KS[n] + KW[n]],
                                                wv_sb[:], start=True, stop=True)
                    return last

                def third(step, off, mult):
                    if step.reg is None:
                        return mult * ((step.place + off) // 3 + 1)
                    return step.reg * mult + mult * ((1 + step.place + off) // 3 + 1)

                def max_unit(step, kind, i):
                    ahead = 2 if kind == "N" else 1
                    nb, h, part = step.mod3(ahead), i // NTH, i % NTH
                    if i == 0:
                        pe.wait_ge(pack_in[nb], third(step, ahead, 16 * (2 * len(QTERMS) + len(TERMS))))
                    return nc.tensor.matmul(slots[SLOT[kind, i]][0:NQ, 0:CUT[part + 1] - CUT[part]],
                                            Qp[0:ROWS, nb, h * NQ:(h + 1) * NQ],
                                            Kp[0:ROWS, nb, h // 2, CUT[part]:CUT[part + 1]],
                                            start=True, stop=True)

                def use_slot(step, kind, i):
                    count = slot_count(step, kind, i)
                    if step.reg is not None or count > 1:
                        pe.wait_ge(slot_read[SLOT[kind, i]], count - 1)
                    slot = slots[SLOT[kind, i]]
                    if kind == "K":
                        last = project_k(step, i)
                    elif kind == "V":
                        last = project_v(step, i)
                    elif kind in "MN":
                        last = max_unit(step, kind, i)
                    elif kind == "T":
                        pe.wait_ge(m_ready, at_batch(step, 2))
                        last = nc.tensor.transpose(slot[0:H, 0:NQ], mmax[:], ident[0:NQ, 0:NQ])
                    elif kind == "O":
                        pe.wait_ge(o_evac, at_batch(step, 0))
                        for q in range(QUADS):
                            last = nc.tensor.transpose(slot[0:NQ, q * P:(q + 1) * P], oT[:, q * NQ:(q + 1) * NQ],
                                                       ident[:])
                    elif kind == "A":
                        pe.wait_ge(heads_ok, at_batch(step, 0))
                        last = nc.tensor.transpose(slot[:, 0:NQ], heads[:], ident[0:NQ, 0:NQ])
                    elif kind == "W":
                        user_wait(pe, slot_read, step, "A", 0)
                        last = nc.tensor.matmul(slot[0:NQ, 0:D], headsT[:], wo_sb[:], start=True, stop=True)
                    last.then_inc(slot_full[SLOT[kind, i]], 1)

                def score_unit(step, s):
                    nb, n, q = step.mod3(), s // QUADS, s % QUADS
                    if s == 0:
                        pe.wait_ge(shift_in[nb], third(step, 0, 16))
                    if step.reg is not None or UNITS * step.place + s >= NE:
                        pe.wait_ge(exped, step.lin(UNITS, s - NE + 1))
                    for a in range(2):
                        g = 2 * q + a
                        last = nc.tensor.matmul(scores[0:KW[n], s % NE, a * 2 * NQ:(a + 1) * 2 * NQ],
                                                Kp[0:ROWS + SH, nb, g, KS[n]:KS[n] + KW[n]],
                                                Qp[0:ROWS + SH, nb, g * 2 * NQ:(g + 1) * 2 * NQ],
                                                start=True, stop=True)
                    last.then_inc(scored, 1)

                def pv_unit(step, s, back):
                    nb, n, q = step.mod3(-back), s // QUADS, s % QUADS
                    if s == 0:
                        if step.reg is not None or step.place >= 1:
                            pe.wait_ge(o_evac, at_batch(step, 0))
                    pe.wait_ge(exped, step.lin(UNITS, s + 1 - back * UNITS))
                    for j in range(4):
                        last = nc.tensor.matmul(o_ps[32 * j:32 * j + HD + 1, q * NQ:(q + 1) * NQ],
                                                V[0:KW[n], nb, n, 4 * q + j, :],
                                                probs[0:KW[n], s % NP_, j * NQ:(j + 1) * NQ],
                                                start=(n == 0 and q == 0), stop=(n == KT - 1),
                                                skip_group_check=True)
                    last.then_inc(pv_done, 1)

                def transpose_group(n, u):
                    pe.wait_ge(ln_ok, n * G + G)
                    for j in range(G):
                        last = nc.tensor.transpose(xnT_ps[u][:, j * NQ:(j + 1) * NQ], xn[:, u, j, :],
                                                   ident[0:NQ, 0:NQ])
                    last.then_inc(ln_T, 1)

                def project_queries(n, u):
                    pe.wait_ge(ln_T_out, n + 1)
                    pe.wait_ge(q_full, n + 1)
                    nc.tensor.matmul(q_ps[u][:, 0:GT], wq_sb[:], xnT[:, u, :], start=True, stop=True)\
                      .then_inc(q_mm, 1)

                def queries():
                    pe.sem_inc(ln_T, 2)
                    pe.sem_inc(q_full, 2)
                    groups(pe, transpose_group, project_queries)
                    pe.wait_ge(init, 1)

                def body(step):
                    for s in range(UNITS):
                        if step.reg is None and step.place == -2 and s == T_AT + 1:
                            queries()
                        if step.reg is None and step.place == 0 and s == 0:
                            pe.wait_ge(env["ones_in"], 16)
                        if step.has_main():
                            score_unit(step, s)
                        if s < LAG:
                            if step.has_final():
                                pv_unit(step, UNITS - LAG + s, 1)
                        elif step.has_main():
                            pv_unit(step, s - LAG, 0)
                        for kind, i in users_at(step, s):
                            use_slot(step, kind, i)

                pe.wait_ge(w_in, 16 * 8)
                run(pe, body)
    sem.clear()


def layer_norm_stats(nc, dve, act_io, x_of, stat, mv, rstd, nmr, sems):
    stats, var_ok, std_ok, rstd_ok = sems
    with dve.Fori(0, B // 4) as i:
        for j in range(4):
            nc.vector.bn_stats(stat[:, bass.ds(i * 4 + j, 1), :].rearrange("p o s -> p (o s)"),
                               x_of(i * (4 * D) + j * D)).then_inc(stats, 1)
    dve.wait_ge(stats, B)
    for b in range(B):
        nc.vector.bn_aggr(mv[:, b, :], stat[:, b, :]).then_inc(stats, 1)
    dve.wait_ge(stats, 2 * B)
    nc.vector.tensor_scalar_add(rstd[:], mv[:, :, 1], EPS).then_inc(var_ok, 1)
    dve.wait_ge(std_ok, 1)
    nc.vector.reciprocal(rstd[:], rstd[:]).then_inc(rstd_ok, 1)
    dve.wait_ge(rstd_ok, 1)
    nc.vector.scalar_tensor_tensor(nmr[:], mv[:, :, 0], -1.0, rstd[:], ALU.mult,
                                   ALU.mult).then_inc(rstd_ok, 1)


def bc(ap, n):
    return ap.unsqueeze(2).to_broadcast([ap.shape[0], ap.shape[1], n])


def bm(ap, n):
    return ap.unsqueeze(1).to_broadcast([ap.shape[0], n, ap.shape[1]])


def top_two(nc, link, L, L2, desc, cand, f1, f2, mx, E):
    for n, (src, f) in enumerate(((L, f1), (L2, f2))):
        link(nc.vector.tensor_tensor(cand, src, bc(mx, E), ALU.is_ge))
        link(nc.vector.tensor_tensor(cand, cand, desc, ALU.mult))
        link(nc.vector.tensor_reduce(mx, cand, AX.X, ALU.max))
        link(nc.vector.tensor_tensor(f, cand, bc(mx, E), ALU.is_equal))
        if n == 0:
            link(nc.vector.scalar_tensor_tensor(L2, f, -1e30, L, ALU.mult, ALU.add))
            link(nc.vector.tensor_reduce(mx, L2, AX.X, ALU.max))
    link(nc.vector.tensor_tensor(f1, f1, f2, ALU.add))


def expert_attention(nc, env, W, x_sb):
    sim, gates, wqk, wv, wo = W
    E, HE = 16, 64
    EP = E // 2
    ident, tg = env["ident"], env["tg"]
    sem = Semaphores(nc, "f")
    st = ExitStack()
    with st:
        sb = lambda name, shape, dt=F32: st.enter_context(nc.sbuf_tensor(f"{name}_f", shape, dt))
        wqk_sb, wv_sb, wo_sb = sb("wqk", [D, E, 2 * HE]), sb("wve", [D, E, HE]), sb("woe", [P, EP, D])
        causal = sb("causal", [NQ, NQ])
        rstd, nmr, rw = sb("rstd", [NQ, B]), sb("nmr", [NQ, B]), sb("rw", [NQ, B, E])

        with ExitStack() as s1:
            sg_ = lambda name, shape, dt=F32: s1.enter_context(nc.sbuf_tensor(f"{name}_g", shape, dt))
            sim_sb, ssq, snorm, ones = sg_("sim", [D, E]), sg_("ssq", [D, E]), sg_("snorm", [D, E]), sg_("ones", [D, D])
            gs = sg_("gs", [NQ, E])
            stat, mv = sg_("stat", [NQ, B, 6]), sg_("mv", [NQ, B, 2])
            xn, sq, xnT = sg_("xn", [NQ, 2, G, D]), sg_("sq", [NQ, 2, G, D]), sg_("xnT", [D, 2, GT])
            ss = sg_("ss", [NQ, B])
            L, L2, cand = sg_("L", [NQ, B, E]), sg_("L2", [NQ, B, E]), sg_("cand", [NQ, B, E])
            f1, f2, mask = sg_("f1", [NQ, B, E]), sg_("f2", [NQ, B, E]), sg_("mask", [NQ, B, E])
            gated = sg_("gated", [NQ, B, E])
            mx, top, idle = sg_("mx", [NQ, B]), sg_("top", [NQ, B]), sg_("idle", [NQ, B])
            desc_i, desc = sg_("desc_i", [NQ, E], mybir.dt.int32), sg_("desc", [NQ, E])
            xnT_ps = s1.enter_context(nc.psum_tensor("xnT_ps_g", [P, 2, 512], F32))
            log_ps = s1.enter_context(nc.psum_tensor("log_ps_g", [P, 2, 512], F32))
            sim_ps = s1.enter_context(nc.psum_tensor("sim_ps_g", [P, 512], F32))
            sim_in, w_in, stats, var_ok, std_ok, rstd_ok = (
                sem(n) for n in ("sim_in", "w_in", "stats", "var_ok", "std_ok", "rstd_ok"))
            sim_sq, sim_sum, sim_root, sim_n, sig_exp = (
                sem(n) for n in ("sim_sq", "sim_sum", "sim_root", "sim_n", "sig_exp"))
            ln_ok, sq_ok, ln_T, ln_T_out, logit_mm, logit_ok = (
                sem(n) for n in ("ln_ok", "sq_ok", "ln_T", "ln_T_out", "logit_mm", "logit_ok"))
            norm_root, pre_exp, gate_exp, chain, iota_ok = (
                sem(n) for n in ("norm_root", "pre_exp", "gate_exp", "chain", "iota_ok"))

            with nc.Block() as block:
                @block.sync
                def _(sp):
                    sp.dma_start(sim_sb[:], sim).then_inc(sim_in, 16)
                    sp.dma_start(gs[:], gates.partition_broadcast(NQ)).then_inc(sim_in, 16)
                    sp.dma_start(wqk_sb[:], wqk).then_inc(w_in, 16)
                    sp.dma_start(wv_sb[:], wv).then_inc(w_in, 16)
                    sp.dma_start(wo_sb[:], wo).then_inc(w_in, 16)
                    sp.wait_ge(w_in, 48)

                @block.gpsimd
                def _(pool):
                    nc.gpsimd.iota(desc_i[:], [[-1, E]], base=E, channel_multiplier=0).then_inc(iota_ok, 1)
                    nc.gpsimd.memset(causal[:], 0.0).then_inc(iota_ok, 1)
                    pool.wait_ge(iota_ok, 2)
                    nc.gpsimd.affine_select(out=causal[:], in_=causal[:], compare_op=ALU.is_ge, fill=-1e30, base=0,
                                            pattern=[[-1, NQ]], channel_multiplier=1).then_inc(iota_ok, 1)

                @block.scalar
                def _(act):
                    act.wait_ge(sim_in, 32)
                    nc.scalar.activation(gs[:], gs[:], ACT.Exp, scale=-1.0).then_inc(sig_exp, 1)
                    act.wait_ge(sim_sum, 1)
                    nc.scalar.activation(snorm[:], sim_ps[:, 0:E], ACT.Sqrt).then_inc(sim_root, 1)
                    act.wait_ge(var_ok, 1)
                    nc.scalar.activation(rstd[:], rstd[:], ACT.Sqrt).then_inc(std_ok, 1)
                    act.wait_ge(rstd_ok, 2)
                    with act.Fori(0, NG // 2) as i:
                        for u in range(2):
                            n = 2 * i + u
                            act.wait_ge(ln_T, n + 1)
                            act.wait_ge(logit_ok, n + 1)
                            for j in range(G):
                                off = i * (2 * G) + (u * G + j)
                                nc.scalar.activation(
                                    xn[:, u, j, :], x_sb[:, bass.ds(i * (2 * G * D) + (u * G + j) * D, D)],
                                    ACT.Identity, bias=nmr[:, bass.ds(off, 1)],
                                    scale=rstd[:, bass.ds(off, 1)]).then_inc(ln_ok, 1)
                            act.wait_ge(ln_ok, i * (2 * G) + (u + 1) * G)
                            nc.scalar.activation(sq[:, u], xn[:, u], ACT.Square).then_inc(sq_ok, 1)
                    act.wait_ge(logit_ok, NG + 2)
                    nc.scalar.activation(ss[:], ss[:], ACT.Sqrt).then_inc(norm_root, 1)
                    act.wait_ge(pre_exp, 1)
                    nc.scalar.activation(L[:], gated[:], ACT.Exp).then_inc(gate_exp, 1)

                @block.tensor
                def _(pe):
                    pe.sem_inc(ln_T, 2)
                    pe.wait_ge(sim_sq, 2)
                    nc.tensor.matmul(sim_ps[:, 0:E], ones[:], ssq[:], start=True, stop=True).then_inc(sim_sum, 1)
                    pe.wait_ge(sim_n, 3)
                    with pe.Fori(0, NG // 2) as i:
                        for u in range(2):
                            n = 2 * i + u
                            pe.wait_ge(ln_ok, i * (2 * G) + G * (u + 1))
                            for j in range(G):
                                last = nc.tensor.transpose(xnT_ps[:, u, j * NQ:(j + 1) * NQ], xn[:, u, j, :],
                                                           ident[0:NQ, 0:NQ])
                            last.then_inc(ln_T, 1)
                            pe.wait_ge(ln_T_out, n + 1)
                            for j in range(G):
                                last = nc.tensor.matmul(log_ps[0:NQ, u, j * E:(j + 1) * E],
                                                        xnT[:, u, j * NQ:(j + 1) * NQ], sim_sb[:],
                                                        start=True, stop=True)
                            last.then_inc(logit_mm, 1)

                @block.vector
                def _(dve):
                    done = [0]

                    def link(ins):
                        done[0] += 1
                        ins.then_inc(chain, 1)
                        dve.wait_ge(chain, done[0])

                    dve.sem_inc(logit_ok, 2)
                    nc.vector.memset(ones[:], 1.0).then_inc(sim_sq, 1)
                    dve.wait_ge(sim_in, 32)
                    nc.vector.tensor_tensor(ssq[:], sim_sb[:], sim_sb[:], ALU.mult).then_inc(sim_sq, 1)
                    dve.wait_ge(sig_exp, 1)
                    link(nc.vector.tensor_scalar_add(gs[:], gs[:], 1.0))
                    link(nc.vector.reciprocal(gs[:], gs[:]))
                    dve.wait_ge(iota_ok, 1)
                    link(nc.vector.tensor_copy(desc[:], desc_i[:]))
                    dve.wait_ge(sim_root, 1)
                    nc.vector.tensor_scalar_max(snorm[:], snorm[:], 1e-12).then_inc(sim_n, 1)
                    dve.wait_ge(sim_n, 1)
                    nc.vector.reciprocal(snorm[:], snorm[:]).then_inc(sim_n, 1)
                    dve.wait_ge(sim_n, 2)
                    nc.vector.tensor_tensor(sim_sb[:], sim_sb[:], snorm[:], ALU.mult).then_inc(sim_n, 1)
                    layer_norm_stats(nc, dve, None, lambda off: x_sb[:, bass.ds(off, D)], stat, mv, rstd, nmr,
                                     (stats, var_ok, std_ok, rstd_ok))
                    Lf = L[:].rearrange("p b e -> p (b e)")
                    with dve.Fori(0, NG // 2) as i:
                        for u in range(2):
                            n = 2 * i + u
                            dve.wait_ge(ln_T, n + 3)
                            nc.vector.tensor_copy(xnT[:, u, :], xnT_ps[:, u, 0:GT]).then_inc(ln_T_out, 1)
                            dve.wait_ge(sq_ok, n + 1)
                            nc.vector.tensor_reduce(ss[:, bass.ds(n * G, G)], sq[:, u], AX.X, ALU.add)
                            dve.wait_ge(logit_mm, n + 1)
                            nc.vector.tensor_copy(Lf[:, bass.ds(n * (G * E), G * E)],
                                                  log_ps[0:NQ, u, 0:G * E]).then_inc(logit_ok, 1)
                    dve.wait_ge(norm_root, 1)
                    link(nc.vector.tensor_scalar_max(ss[:], ss[:], 1e-12))
                    link(nc.vector.reciprocal(ss[:], ss[:]))
                    link(nc.vector.tensor_tensor(L[:], L[:], bc(ss[:], E), ALU.mult))
                    link(nc.vector.tensor_tensor(L[:], L[:], bm(gs[:], B), ALU.subtract))
                    link(nc.vector.tensor_reduce(top[:], L[:], AX.X, ALU.max))
                    nc.vector.tensor_scalar_max(gated[:], L[:], 0.0)
                    nc.vector.tensor_single_scalar(mask[:], L[:], 0.0, ALU.is_gt)
                    nc.vector.tensor_single_scalar(idle[:], top[:], 0.0, ALU.is_le)
                    link(nc.vector.tensor_copy(mx[:], top[:]))
                    top_two(nc, link, L[:], L2[:], bm(desc[:], B), cand[:], f1[:], f2[:], mx[:], E)
                    link(nc.vector.tensor_tensor(f1[:], f1[:], bc(idle[:], E), ALU.mult))
                    nc.vector.tensor_tensor(mask[:], mask[:], f1[:], ALU.add)
                    link(nc.vector.tensor_scalar_max(top[:], top[:], 0.0))
                    nc.vector.tensor_tensor(gated[:], gated[:], bc(top[:], E), ALU.subtract).then_inc(pre_exp, 1)
                    dve.wait_ge(gate_exp, 1)
                    link(nc.vector.tensor_tensor(L[:], L[:], mask[:], ALU.mult))
                    link(nc.vector.tensor_reduce(mx[:], L[:], AX.X, ALU.add))
                    link(nc.vector.reciprocal(mx[:], mx[:]))
                    link(nc.vector.tensor_tensor(rw[:], L[:], bc(mx[:], E), ALU.mult))

        xn, xs = sb("xnb", [NQ, D]), sb("xs", [NQ, E, D])
        xsT = sb("xsT", [D, E * NQ])
        qT, kT, v = sb("qT", [HE, NQ]), sb("kT", [HE, NQ]), sb("v", [NQ, HE])
        masked, nmax, den, rden = sb("masked", [NQ, NQ]), sb("nmax", [NQ, 1]), sb("den", [NQ, 1]), sb("rden", [NQ, 1])
        pr, prT, rwd = sb("pr", [NQ, NQ]), sb("prT", [NQ, NQ]), sb("rwd", [NQ, E])
        mixed, mixT = sb("mixed", [NQ, E, HE]), sb("mixT", [P, EP * NQ])
        pb = lambda name: st.enter_context(nc.psum_tensor(f"{name}_f", [P, 512], F32))
        T_ps = [pb("T_a"), pb("T_b")]
        qk_ps, v_ps, sc_ps, prT_ps, att_ps, out_ps = (
            pb(n) for n in ("qk_ps", "v_ps", "sc_ps", "prT_ps", "att_ps", "out_ps"))
        T_full, T_read, xn_ok, xs_ok, qk_mm, qk_out, v_mm, v_out = (
            sem(n) for n in ("T_full", "T_read", "xn_ok", "xs_ok", "qk_mm", "qk_out", "v_mm", "v_out"))
        sc_mm, masked_ok, nmax_ok, pr_ok, prT_full, prT_out, att_mm = (
            sem(n) for n in ("sc_mm", "masked_ok", "nmax_ok", "pr_ok", "prT_full", "prT_out", "att_mm"))
        rden_ok, rwd_ok, mixed_ok, out_mm, x_ok = (
            sem(n) for n in ("rden_ok", "rwd_ok", "mixed_ok", "out_mm", "x_ok"))

        class Two:

            def __init__(self, place, reg=None):
                self.place, self.reg = place, reg

            def lin(self, mult, off=0):
                if self.reg is None:
                    return mult * self.place + off
                return self.reg * (2 * mult) + (mult * (2 + self.place) + off)

            def on(self, lag):
                return self.reg is not None or 0 <= self.place - lag < B

        def T_use(step, k):
            if step.reg is not None:
                return step.lin(6, k - 4)
            first = sum(4 * Two(p).on(0) + 2 * Two(p).on(2) for p in range(step.place))
            return first + (k if step.on(0) else k - 4)

        def run(eng, body):
            for p in (-1, 0, 1):
                body(Two(p))
            with eng.Fori(0, (B - 4) // 2) as i:
                for u in range(2):
                    body(Two(u, i))
            for p in (B - 2, B - 1, B, B + 1):
                body(Two(p))

        with nc.Block() as block:
            @block.tensor
            def _(pe):
                def transposes(step, k, src, w):
                    n = T_use(step, k)
                    if step.reg is not None or n >= 2:
                        pe.wait_ge(T_read, n - 1)
                    for j in range(4):
                        last = nc.tensor.transpose(T_ps[k % 2][:, j * NQ:(j + 1) * NQ], src[:, 4 * (k % 4) + j, :],
                                                   ident[0:NQ, 0:NQ])
                    last.then_inc(T_full, 1)

                def body(step):
                    if step.on(0):
                        pe.wait_ge(xs_ok, step.lin(1, 1))
                        for k in range(4):
                            transposes(step, k, xs, D)
                    if step.on(1):
                        pe.wait_ge(qk_out, step.lin(1))
                        nc.tensor.matmul(sc_ps[0:NQ, 0:NQ], qT[:], kT[:], start=True, stop=True).then_inc(sc_mm, 1)
                    if step.on(2):
                        pe.wait_ge(mixed_ok, step.lin(1, -1))
                        mv_ = mixed[:].rearrange("p (j a) d -> p j (a d)", a=2)
                        for k in range(4, 6):
                            transposes(step, k, mv_, P)
                    if step.on(0):
                        pe.wait_ge(T_read, T_use(step, 3) + 1)
                        for e in range(E):
                            last = nc.tensor.matmul(qk_ps[:, 0:NQ], wqk_sb[:, e, :], xsT[:, e * NQ:(e + 1) * NQ],
                                                    start=(e == 0), stop=(e == E - 1))
                        last.then_inc(qk_mm, 1)
                    if step.on(2):
                        pe.wait_ge(T_read, T_use(step, 5) + 1)
                        for j in range(EP):
                            last = nc.tensor.matmul(out_ps[0:NQ, 0:D], mixT[:, j * NQ:(j + 1) * NQ], wo_sb[:, j, :],
                                                    start=(j == 0), stop=(j == EP - 1))
                        last.then_inc(out_mm, 1)
                    if step.on(1):
                        pe.wait_ge(pr_ok, step.lin(1))
                        nc.tensor.transpose(prT_ps[0:NQ, 0:NQ], pr[:], ident[0:NQ, 0:NQ]).then_inc(prT_full, 1)
                    if step.on(0):
                        if step.reg is not None or step.place >= 1:
                            pe.wait_ge(v_out, step.lin(1))
                        for e in range(E):
                            last = nc.tensor.matmul(v_ps[0:NQ, 0:HE], xsT[:, e * NQ:(e + 1) * NQ], wv_sb[:, e, :],
                                                    start=(e == 0), stop=(e == E - 1))
                        last.then_inc(v_mm, 1)
                    if step.on(1):
                        pe.wait_ge(prT_out, step.lin(1))
                        pe.wait_ge(v_out, step.lin(1))
                        nc.tensor.matmul(att_ps[0:NQ, 0:HE], prT[:], v[:], start=True, stop=True)\
                          .then_inc(att_mm, 1)

                run(pe, body)

            @block.scalar
            def _(act):
                def evac(step, k, dst):
                    act.wait_ge(T_full, T_use(step, k) + 1)
                    nc.scalar.activation(dst[:, (k % 4) * GT:(k % 4 + 1) * GT], T_ps[k % 2][:, 0:GT], ACT.Copy)\
                      .then_inc(T_read, 1)

                def body(step):
                    if step.on(0):
                        for k in range(4):
                            evac(step, k, xsT)
                    if step.on(-1):
                        if step.reg is not None or step.place >= 0:
                            act.wait_ge(xs_ok, step.lin(1, 1))
                        nc.scalar.activation(xn[:], x_sb[:, bass.ds(step.lin(D, D), D)], ACT.Identity,
                                             bias=nmr[:, bass.ds(step.lin(1, 1), 1)],
                                             scale=rstd[:, bass.ds(step.lin(1, 1), 1)]).then_inc(xn_ok, 1)
                    if step.on(2):
                        for k in range(4, 6):
                            evac(step, k, mixT)
                    if step.on(1):
                        act.wait_ge(nmax_ok, step.lin(1))
                        if step.reg is not None or step.place >= 2:
                            act.wait_ge(rden_ok, step.lin(1, -1))
                        nc.scalar.activation(pr[:], masked[:], ACT.Exp, bias=nmax[:, 0:1],
                                             accum_out=den[:, 0:1]).then_inc(pr_ok, 1)
                        act.wait_ge(prT_full, step.lin(1))
                        nc.scalar.activation(prT[:], prT_ps[0:NQ, 0:NQ], ACT.Copy).then_inc(prT_out, 1)
                    if step.on(0):
                        act.wait_ge(v_mm, step.lin(1, 1))
                        if step.reg is not None or step.place >= 1:
                            act.wait_ge(att_mm, step.lin(1))
                        nc.scalar.activation(v[:], v_ps[0:NQ, 0:HE], ACT.Copy).then_inc(v_out, 1)

                run(act, body)

            @block.vector
            def _(dve):
                def body(step):
                    if step.on(1):
                        dve.wait_ge(sc_mm, step.lin(1))
                        nc.vector.scalar_tensor_tensor(masked[:], sc_ps[0:NQ, 0:NQ], HE ** -0.5, causal[:],
                                                       ALU.mult, ALU.add).then_inc(masked_ok, 1)
                        dve.wait_ge(masked_ok, step.lin(1))
                        nc.vector.tensor_reduce(nmax[:], masked[:], AX.X, ALU.max, negate=True)\
                          .then_inc(nmax_ok, 1)
                    if step.on(-1):
                        dve.wait_ge(xn_ok, step.lin(1, 2))
                        if step.reg is not None or step.place >= 0:
                            dve.wait_ge(T_full, T_use(step, 3) + 1)
                        nc.vector.tensor_tensor(
                            xs[:], xn[:].unsqueeze(1).to_broadcast([NQ, E, D]),
                            bc(rw[:, bass.ds(step.lin(1, 1), 1), :].rearrange("p o e -> p (o e)"), D), ALU.mult)\
                          .then_inc(xs_ok, 1)
                    if step.on(0):
                        dve.wait_ge(qk_mm, step.lin(1, 1))
                        nc.vector.tensor_copy(qT[:], qk_ps[0:HE, 0:NQ])
                        nc.vector.tensor_copy(kT[:], qk_ps[HE:2 * HE, 0:NQ]).then_inc(qk_out, 1)
                    if step.on(1):
                        dve.wait_ge(pr_ok, step.lin(1))
                        nc.vector.reciprocal(rden[:], den[:]).then_inc(rden_ok, 1)
                        dve.wait_ge(rden_ok, step.lin(1))
                        nc.vector.tensor_scalar(
                            rwd[:], rw[:, bass.ds(step.lin(1, -1), 1), :].rearrange("p o e -> p (o e)"),
                            rden[:, 0:1], None, ALU.mult).then_inc(rwd_ok, 1)
                    if step.on(2):
                        dve.wait_ge(out_mm, step.lin(1, -1))
                        xb = x_sb[:, bass.ds(step.lin(D, -2 * D), D)]
                        nc.vector.scalar_tensor_tensor(xb, out_ps[0:NQ, 0:D], tg[0:NQ, 2:3], xb, ALU.mult,
                                                       ALU.add).then_inc(x_ok, 1)
                    if step.on(1):
                        dve.wait_ge(rwd_ok, step.lin(1))
                        dve.wait_ge(att_mm, step.lin(1))
                        nc.vector.tensor_tensor(mixed[:], att_ps[0:NQ, 0:HE].unsqueeze(1).to_broadcast([NQ, E, HE]),
                                                bc(rwd[:], HE), ALU.mult).then_inc(mixed_ok, 1)

                run(dve, body)
    sem.clear()


def mixture_of_experts(nc, env, W, x_sb):
    gamma, beta, router, wgu, wdn, sgu, sdn = W
    E, F = 8, 512
    FC = F // P
    CHUNKS = [(E, 0)] + [(e, c) for e in range(E) for c in range(FC)]
    NC = len(CHUNKS)
    NB = 3
    BACK = 2
    assert NC % NB == 0
    ident, tg = env["ident"], env["tg"]
    sem = Semaphores(nc, "m")
    st = ExitStack()
    with st:
        sb = lambda name, shape, dt=F32: st.enter_context(nc.sbuf_tensor(f"{name}_m", shape, dt))
        wgu_sb, wdn_sb = sb("wgu", [D, E, 2 * F]), sb("wdn", [P, E, FC, D])
        sgu_sb, sdn_sb = sb("sgu", [D, 2 * P]), sb("sdn", [P, D])
        xT, comb = sb("xT", [D, TOK]), sb("comb", [NQ, B, E])
        w_in = sem("w_in")

        with ExitStack() as s1:
            sg_ = lambda name, shape, dt=F32: s1.enter_context(nc.sbuf_tensor(f"{name}_r", shape, dt))
            gb, rt = sg_("gb", [D, 2]), sg_("rt", [D, E])
            h = sg_("h", [NQ, B * D])
            stat, mv, rstd, nmr = sg_("stat", [NQ, B, 6]), sg_("mv", [NQ, B, 2]), sg_("rstd", [NQ, B]), sg_("nmr", [NQ, B])
            stat2, mv2, rstd2, nmr2 = (sg_("stat2", [NQ, B, 6]), sg_("mv2", [NQ, B, 2]), sg_("rstd2", [NQ, B]),
                                       sg_("nmr2", [NQ, B]))
            xn, xg = sg_("xn", [NQ, 2, G, D]), sg_("xg", [D, 2, GT])
            L, L2, cand, f1, f2 = (sg_(n, [NQ, B, E]) for n in ("L", "L2", "cand", "f1", "f2"))
            mx = sg_("mx", [NQ, B])
            desc_i, desc = sg_("desc_i", [NQ, E], mybir.dt.int32), sg_("desc", [NQ, E])
            xnT_ps = s1.enter_context(nc.psum_tensor("xnT_ps_r", [P, 2, 512], F32))
            log_ps = s1.enter_context(nc.psum_tensor("log_ps_r", [P, 2, 512], F32))
            small_in, iota_ok = sem("small_in"), sem("iota_ok")
            ln1 = [sem(n) for n in ("stats", "var_ok", "std_ok", "rstd_ok")]
            ln2 = [sem(n) for n in ("stats2", "var_ok2", "std_ok2", "rstd_ok2")]
            h_ok, ln_ok, ln_T, ln_T_out, xT_ok, logit_mm, logit_ok, pre_exp, gate_exp, chain = (
                sem(n) for n in ("h_ok", "ln_ok", "ln_T", "ln_T_out", "xT_ok", "logit_mm", "logit_ok", "pre_exp",
                                 "gate_exp", "chain"))

            with nc.Block() as block:
                @block.sync
                def _(sp):
                    for dst, src in ((gb[:, 0:1], gamma), (gb[:, 1:2], beta), (rt[:], router)):
                        sp.dma_start(dst, src).then_inc(small_in, 16)
                    sp.dma_start(sgu_sb[:], sgu).then_inc(w_in, 16)
                    sp.dma_start(sdn_sb[:], sdn).then_inc(w_in, 16)
                    sp.dma_start(wgu_sb[:], wgu.rearrange("e c f -> c e f")).then_inc(w_in, 16)
                    sp.dma_start(wdn_sb[:], wdn.rearrange("e (a f) c -> f e a c", a=FC)).then_inc(w_in, 16)
                    sp.wait_ge(w_in, 64)

                @block.gpsimd
                def _(pool):
                    nc.gpsimd.iota(desc_i[:], [[-1, E]], base=E, channel_multiplier=0).then_inc(iota_ok, 1)

                @block.scalar
                def _(act):
                    act.wait_ge(ln1[1], 1)
                    nc.scalar.activation(rstd[:], rstd[:], ACT.Sqrt).then_inc(ln1[2], 1)
                    act.wait_ge(ln1[3], 2)
                    with act.Fori(0, B // 4) as i:
                        for j in range(4):
                            at = bass.ds(i * (4 * D) + j * D, D)
                            nc.scalar.activation(h[:, at], x_sb[:, at], ACT.Identity,
                                                 bias=nmr[:, bass.ds(i * 4 + j, 1)],
                                                 scale=rstd[:, bass.ds(i * 4 + j, 1)]).then_inc(h_ok, 1)
                    act.wait_ge(ln2[1], 1)
                    nc.scalar.activation(rstd2[:], rstd2[:], ACT.Sqrt).then_inc(ln2[2], 1)
                    act.wait_ge(ln2[3], 2)
                    with act.Fori(0, NG // 2) as i:
                        for u in range(2):
                            n = 2 * i + u
                            act.wait_ge(ln_T, n + 1)
                            for j in range(G):
                                off = i * (2 * G) + (u * G + j)
                                nc.scalar.activation(
                                    xn[:, u, j, :], h[:, bass.ds(i * (2 * G * D) + (u * G + j) * D, D)],
                                    ACT.Identity, bias=nmr2[:, bass.ds(off, 1)],
                                    scale=rstd2[:, bass.ds(off, 1)]).then_inc(ln_ok, 1)
                            act.wait_ge(ln_T_out, n + 1)
                            nc.scalar.activation(xT[:, bass.ds(n * GT, GT)], xg[:, u, :], ACT.Copy)\
                              .then_inc(xT_ok, 1)
                    act.wait_ge(pre_exp, 1)
                    nc.scalar.activation(L[:], L[:], ACT.Exp).then_inc(gate_exp, 1)

                @block.tensor
                def _(pe):
                    pe.sem_inc(ln_T, 2)
                    pe.wait_ge(small_in, 48)
                    with pe.Fori(0, NG // 2) as i:
                        for u in range(2):
                            n = 2 * i + u
                            pe.wait_ge(ln_ok, i * (2 * G) + G * (u + 1))
                            for j in range(G):
                                last = nc.tensor.transpose(xnT_ps[:, u, j * NQ:(j + 1) * NQ], xn[:, u, j, :],
                                                           ident[0:NQ, 0:NQ])
                            last.then_inc(ln_T, 1)
                            pe.wait_ge(ln_T_out, n + 1)
                            for j in range(G):
                                last = nc.tensor.matmul(log_ps[0:NQ, u, j * E:(j + 1) * E],
                                                        xg[:, u, j * NQ:(j + 1) * NQ], rt[:], start=True, stop=True)
                            last.then_inc(logit_mm, 1)

                @block.vector
                def _(dve):
                    done = [0]

                    def link(ins):
                        done[0] += 1
                        ins.then_inc(chain, 1)
                        dve.wait_ge(chain, done[0])

                    dve.sem_inc(xT_ok, 2)
                    dve.wait_ge(iota_ok, 1)
                    link(nc.vector.tensor_copy(desc[:], desc_i[:]))
                    layer_norm_stats(nc, dve, None, lambda off: x_sb[:, bass.ds(off, D)], stat, mv, rstd, nmr, ln1)
                    dve.wait_ge(h_ok, B)
                    layer_norm_stats(nc, dve, None, lambda off: h[:, bass.ds(off, D)], stat2, mv2, rstd2, nmr2, ln2)
                    dve.wait_ge(small_in, 48)
                    Lf = L[:].rearrange("p b e -> p (b e)")
                    with dve.Fori(0, NG // 2) as i:
                        for u in range(2):
                            n = 2 * i + u
                            dve.wait_ge(ln_T, n + 3)
                            dve.wait_ge(xT_ok, n + 1)
                            nc.vector.tensor_scalar(xg[:, u, :], xnT_ps[:, u, 0:GT], gb[:, 0:1], gb[:, 1:2],
                                                    ALU.mult, ALU.add).then_inc(ln_T_out, 1)
                            dve.wait_ge(logit_mm, n + 1)
                            nc.vector.tensor_copy(Lf[:, bass.ds(n * (G * E), G * E)],
                                                  log_ps[0:NQ, u, 0:G * E]).then_inc(logit_ok, 1)
                    dve.wait_ge(logit_ok, NG)
                    link(nc.vector.tensor_reduce(mx[:], L[:], AX.X, ALU.max))
                    nc.vector.tensor_tensor(L[:], L[:], bc(mx[:], E), ALU.subtract).then_inc(pre_exp, 1)
                    dve.wait_ge(gate_exp, 1)
                    link(nc.vector.tensor_reduce(mx[:], L[:], AX.X, ALU.add))
                    link(nc.vector.reciprocal(mx[:], mx[:]))
                    link(nc.vector.tensor_tensor(L[:], L[:], bc(mx[:], E), ALU.mult))
                    link(nc.vector.tensor_reduce(mx[:], L[:], AX.X, ALU.max))
                    top_two(nc, link, L[:], L2[:], bm(desc[:], B), cand[:], f1[:], f2[:], mx[:], E)
                    link(nc.vector.tensor_tensor(L[:], L[:], f1[:], ALU.mult))
                    link(nc.vector.tensor_reduce(mx[:], L[:], AX.X, ALU.add))
                    link(nc.vector.reciprocal(mx[:], mx[:]))
                    link(nc.vector.tensor_tensor(comb[:], L[:], bc(mx[:], E), ALU.mult))

        xg, clip, silu, hT = (sb("xgm", [D, 2, GT]), sb("clip", [P, NB, GT]), sb("silu", [P, NB, GT]),
                              sb("hT", [P, NB, GT]))
        acc = sb("acc", [NQ, 2, G, D])
        gate_ps = st.enter_context(nc.psum_tensor("gate_ps", [P, NB, 512], F32))
        up_ps = st.enter_context(nc.psum_tensor("up_ps", [P, NB, 512], F32))
        down_ps = st.enter_context(nc.psum_tensor("down_ps", [P, 2, 512], F32))
        xg_ok, gate_mm, clip_ok, silu_ok, h_ok2, down_mm, acc_ok, group_ok, x_ok = (
            sem(n) for n in ("xg_ok", "gate_mm", "clip_ok", "silu_ok", "h_ok2", "down_mm", "acc_ok", "group_ok",
                             "x_ok"))
        EX = E + 1
        with nc.Block() as block:
            @block.tensor
            def _(pe):
                pe.sem_inc(h_ok2, NB)
                pe.sem_inc(acc_ok, 2)
                with pe.Fori(0, NG // 2) as i:
                    def gate_up(k):
                        u, (e, c) = k // NC, CHUNKS[k % NC]
                        pe.wait_ge(h_ok2, i * (2 * NC) + (k + 1))
                        w = sgu_sb if e == E else wgu_sb[:, e, :]
                        f = P if e == E else F
                        nc.tensor.matmul(gate_ps[:, k % NB, 0:GT], w[:, c * P:(c + 1) * P], xg[:, u, :],
                                         start=True, stop=True).then_inc(gate_mm, 1)
                        nc.tensor.matmul(up_ps[:, k % NB, 0:GT], w[:, f + c * P:f + (c + 1) * P], xg[:, u, :],
                                         start=True, stop=True).then_inc(gate_mm, 1)

                    def down(k):
                        u, (e, c) = k // NC, CHUNKS[k % NC]
                        x = u * EX + (0 if e == E else e + 1)
                        last_c = 0 if e == E else FC - 1
                        if c == 0:
                            pe.wait_ge(acc_ok, i * (2 * EX) + (x + 1))
                        pe.wait_ge(h_ok2, i * (2 * NC) + (k + 1 + NB))
                        for j in range(G):
                            last = nc.tensor.matmul(down_ps[0:NQ, x % 2, j * D:(j + 1) * D],
                                                    hT[:, k % NB, j * NQ:(j + 1) * NQ],
                                                    sdn_sb[:] if e == E else wdn_sb[:, e, c, :],
                                                    start=(c == 0 and j == 0), stop=(c == last_c),
                                                    skip_group_check=True)
                        if c == last_c:
                            last.then_inc(down_mm, 1)

                    for k in range(2 * NC + BACK):
                        if k < 2 * NC:
                            if k % NC == 0:
                                pe.wait_ge(xg_ok, 2 * i + (k // NC + 1))
                            gate_up(k)
                        if k >= BACK:
                            down(k - BACK)

            @block.scalar
            def _(act):
                with act.Fori(0, NG // 2) as i:
                    for u in range(2):
                        nc.scalar.activation(xg[:, u, :], xT[:, bass.ds(i * (2 * GT) + u * GT, GT)], ACT.Copy)\
                          .then_inc(xg_ok, 1)
                    for k in range(2 * NC):
                        act.wait_ge(clip_ok, i * (2 * NC) + (k + 1))
                        nc.scalar.activation(silu[:, k % NB, :], clip[:, k % NB, :], ACT.Silu).then_inc(silu_ok, 1)
                    act.wait_ge(gate_mm, i * (4 * NC) + 4 * NC)

            @block.vector
            def _(dve):
                with dve.Fori(0, NG // 2) as i:
                    def clipped(k):
                        dve.wait_ge(gate_mm, i * (4 * NC) + (2 * k + 1))
                        nc.vector.tensor_scalar(clip[:, k % NB, :], gate_ps[:, k % NB, 0:GT], -10.0, 10.0, ALU.max,
                                                ALU.min).then_inc(clip_ok, 1)

                    def hidden(k):
                        dve.wait_ge(gate_mm, i * (4 * NC) + (2 * k + 2))
                        dve.wait_ge(silu_ok, i * (2 * NC) + (k + 1))
                        nc.vector.tensor_tensor(hT[:, k % NB, :], silu[:, k % NB, :], up_ps[:, k % NB, 0:GT],
                                                ALU.mult).then_inc(h_ok2, 1)

                    def accumulate(x):
                        u, e = x // EX, x % EX - 1
                        dve.wait_ge(down_mm, i * (2 * EX) + (x + 1))
                        if e < 0:
                            nc.vector.tensor_copy(acc[:, u].rearrange("p j d -> p (j d)"), down_ps[0:NQ, x % 2, :])\
                              .then_inc(acc_ok, 1)
                        else:
                            dve.wait_ge(acc_ok, i * (2 * EX) + (x + 2))
                            for j in range(G):
                                w = comb[:, bass.ds(i * (2 * G) + (u * G + j), 1), e]
                                last = nc.vector.scalar_tensor_tensor(
                                    acc[:, u, j, :], down_ps[0:NQ, x % 2, j * D:(j + 1) * D], w, acc[:, u, j, :],
                                    ALU.mult, ALU.add)
                            last.then_inc(acc_ok, 1)
                        if e == E - 1:
                            dve.wait_ge(acc_ok, i * (2 * EX) + (x + 3))
                            xb = x_sb[:, bass.ds(i * (2 * G * D) + u * (G * D), G * D)]
                            nc.vector.scalar_tensor_tensor(xb, acc[:, u].rearrange("p j d -> p (j d)"),
                                                           tg[0:NQ, 3:4], xb, ALU.mult, ALU.add).then_inc(x_ok, 1)

                    ends = {}
                    for x in range(2 * EX):
                        u, e = x // EX, x % EX - 1
                        ends[u * NC + (0 if e < 0 else 1 + e * FC + FC - 1)] = x
                    for k in range(2 * NC + BACK + 1):
                        if k < 2 * NC:
                            clipped(k)
                        if 1 <= k <= 2 * NC:
                            hidden(k - 1)
                        if k - BACK - 1 in ends:
                            accumulate(ends[k - BACK - 1])
    sem.clear()


def build(nc, x, ctxT, g_xattn, g_ffn, layers, out, ffn0=None, ffn1=None):
    ctx = ExitStack()
    with ctx:
        sb = lambda name, shape, dt=F32: ctx.enter_context(nc.sbuf_tensor(name, shape, dt))
        sem = lambda name: ctx.enter_context(nc.semaphore(name))
        env = {"ctx": ctx}
        x_sb = sb("x_sb", [NQ, B * D])
        ident = env["ident"] = sb("ident", [P, P])
        gates = sb("gates", [P, 4])
        tg = env["tg"] = sb("tg", [P, 4])
        x_in, g_in, ident_ok, tanh_ok, packs_ok, ones_ok, ones_in = (
            sem(n) for n in ("x_in", "g_in", "ident_ok", "tanh_ok", "packs_ok", "ones_ok", "ones_in"))
        env["x_in"], env["ones_in"] = x_in, ones_in
        ones = sb("ones", [P, NK], BF16)
        kscr = nc.dram_tensor("kscr", (3, 3, P, NK), BF16).ap()
        qscr = nc.dram_tensor("qscr", (3, P, TOK), BF16).ap()
        mscr = nc.dram_tensor("mscr", (3, SH, H, NQ), BF16).ap()

        with ExitStack() as packs:
            env["Kp"] = packs.enter_context(nc.sbuf_tensor("Kp", [P, 3, PAIRS, NK], BF16))
            env["Qp"] = packs.enter_context(nc.sbuf_tensor("Qp", [P, 3, H * NQ], BF16))
            env["V"] = packs.enter_context(nc.sbuf_tensor("V", [P, 3, KT, H, HD + 1], F32))

            with nc.Block() as block:
                @block.sync
                def _(sp):
                    sp.dma_start(x_sb[:].rearrange("q (b d) -> q b d", b=B), x.rearrange("b q d -> q b d"))\
                      .then_inc(x_in, 16)
                    for i, g in enumerate((g_xattn, g_ffn)):
                        sp.dma_start(gates[:, 2 * i:2 * i + 2], g.partition_broadcast(P)).then_inc(g_in, 16)
                    sp.wait_ge(ones_ok, 1)
                    sp.dma_start(env["Kp"][ROWS:ROWS + SH].rearrange("p b g n -> p (b g) n"),
                                 ones[0:SH].unsqueeze(1).to_broadcast([SH, 3 * PAIRS, NK])).then_inc(ones_in, 16)

                @block.scalar
                def _(act):
                    act.wait_ge(g_in, 32)
                    nc.scalar.activation(tg[:], gates[:], ACT.Tanh).then_inc(tanh_ok, 1)

                @block.gpsimd
                def _(pool):
                    nc.gpsimd.memset(ident[:], 0.0).then_inc(ident_ok, 1)
                    pool.wait_ge(ident_ok, 1)
                    nc.gpsimd.affine_select(out=ident[:], in_=ident[:], compare_op=ALU.not_equal, fill=1.0, base=0,
                                            pattern=[[-1, P]], channel_multiplier=1).then_inc(ident_ok, 1)
                    nc.gpsimd.memset(env["V"][:, :, :, :, HD:HD + 1].rearrange("p b t h o -> p (b t h o)"), 1.0)\
                      .then_inc(packs_ok, 1)

                @block.vector
                def _(dve):
                    nc.vector.memset(ones[0:SH], 1.0).then_inc(ones_ok, 1)
                    nc.vector.memset(env["Qp"][:], 0.0).then_inc(packs_ok, 1)

            scr = (kscr, qscr, mscr)
            attention(nc, env, 0, (ctxT, *layers[0]), scr, x_sb)
            if ffn0:
                expert_attention(nc, env, ffn0, x_sb)
            if len(layers) > 1:
                attention(nc, env, 1, (ctxT, *layers[1]), scr, x_sb)

        if ffn1:
            mixture_of_experts(nc, env, ffn1, x_sb)
        out_done = sem("out_done")
        with nc.Block() as block:
            @block.sync
            def _(sp):
                sp.dma_start(out.rearrange("b q d -> q b d"), x_sb[:].rearrange("q (b d) -> q b d", b=B))\
                  .then_inc(out_done, 16)
                sp.wait_ge(out_done, 16)


def kernel(**inputs):
    import concourse.bacc as bacc
    from concourse.bass_utils import run_bass_kernel_spmd

    def paired(w):
        w = w.reshape(-1, PAIRS, 2, HD)
        return w.transpose(0, 2, 3, 1).reshape(w.shape[0], D)

    a = {name: np.asarray(v) for name, v in inputs.items()}
    kv_w, kv_b = a["L1_xattn_kv_w"], a["L1_xattn_kv_b"]
    laid = {
        "x": a["x"],
        "ctxT": a["ctx_768"].transpose(0, 2, 1).reshape(B * DC, NK),
        "g_xattn": a["g_xattn"], "g_ffn": a["g_ffn"],
    }
    for lay, (wq, bq, wk, bk, wv, bv, wo, bo) in enumerate((
            tuple(a[f"L0_xattn_{n}"] for n in ("Wq", "bq", "Wk", "bk", "Wv", "bv", "Wo", "bo")),
            (a["L1_xattn_q_w"], a["L1_xattn_q_b"], kv_w[:, :D], kv_b[:D], kv_w[:, D:], kv_b[D:],
             a["L1_xattn_proj_w"], a["L1_xattn_proj_b"]))):
        for name, v in (("wq", paired(wq)), ("bq", paired(bq).reshape(D, 1)), ("wk", paired(wk)),
                        ("bk", paired(bk).reshape(D, 1)), ("wv", wv), ("bv", bv), ("wo", wo), ("bo", bo)):
            laid[f"a{lay}_{name}"] = v
    laid["f0_sim"], laid["f0_gates"] = a["L0_ffn_sim_matrix"], a["L0_ffn_gates"]
    laid["f0_wqk"] = np.concatenate([a["L0_ffn_q_proj"], a["L0_ffn_k_proj"]], axis=-1).transpose(1, 0, 2)
    laid["f0_wv"] = a["L0_ffn_v_proj"].transpose(1, 0, 2)
    laid["f0_wo"] = a["L0_ffn_o_proj"].reshape(-1, P, D).transpose(1, 0, 2)
    laid["f1_gamma"], laid["f1_beta"] = a["L1_ffn_ln_gamma"].reshape(D, 1), a["L1_ffn_ln_beta"].reshape(D, 1)
    laid["f1_router"], laid["f1_wgu"], laid["f1_wdn"] = (
        a["L1_ffn_router_w"], a["L1_ffn_gate_up_w"], a["L1_ffn_down_w"])
    laid["f1_sgu"], laid["f1_sdn"] = a["L1_ffn_shared_gate_up_w"], a["L1_ffn_shared_down_w"]

    nc = bacc.Bacc("TRN2", target_bir_lowering=False, num_devices=1)
    arrays, ap = {}, {}
    for name, v in laid.items():
        v = np.ascontiguousarray(v)
        arrays[f"in_{name}"] = v
        ap[name] = nc.dram_tensor(f"in_{name}", v.shape, mybir.dt.from_np(v.dtype), kind="ExternalInput").ap()
    out = nc.dram_tensor("out_0", (B, NQ, D), F32, kind="ExternalOutput").ap()
    group = lambda p: [ap[n] for n in laid if n.startswith(p)]
    build(nc, ap["x"], ap["ctxT"], ap["g_xattn"], ap["g_ffn"], [group("a0_"), group("a1_")], out,
          group("f0_"), group("f1_"))
    return run_bass_kernel_spmd(nc, [arrays], core_ids=[0]).results[0]["out_0"]
```

```python
from contextlib import ExitStack

import numpy as np

import concourse.bass as bass
from concourse import mybir

F32, BF16, F32R = mybir.dt.float32, mybir.dt.bfloat16, mybir.dt.float32r
ALU, ACT, AX = mybir.AluOpType, mybir.ActivationFunctionType, mybir.AxisListType

B, NQ, D = 32, 100, 128
NK, DC = 1444, 96
H = 16
HD = D // H
TOK = B * NQ
G = 4
NG, GT = B // G, G * NQ
P = 128
EPS = 1e-5

KT = -(-NK // P)
KFULL = KT - 2
KW = [P] * KFULL + [(NK - P * KFULL) // 2] * 2
KS = [sum(KW[:t]) for t in range(KT)]
assert sum(KW) == NK
PAIRS = H // 2
TERMS = [0, 0, 0, 1, 1, 2]
QTERMS = [0, 1, 2, 0, 1, 0]
ROWS = len(TERMS) * 2 * HD
SH = 3
QUADS = H // 4
QW = 4 * NQ
UNITS = KT * QUADS
CUT = [0, 482, 963, NK]
NTH = len(CUT) - 1
VS = KT // 2
LAG = 3
NE, NP_ = 3, 6


class Semaphores:

    def __init__(self, nc, suffix):
        self.nc, self.suffix, self.held = nc, suffix, []

    def __call__(self, name):
        self.held.append(self.nc.alloc_semaphore(name=f"{name}_{self.suffix}"))
        return self.held[-1]

    def clear(self):
        self.nc.clear_and_free_semaphores(self.held)
        self.nc.all_engine_barrier()


class Step:

    def __init__(self, place, reg=None):
        self.place, self.reg = place, reg

    def lin(self, mult, off=0):
        if self.reg is None:
            return mult * self.place + off
        return self.reg * (3 * mult) + (mult * (1 + self.place) + off)

    def mod3(self, off=0):
        return (self.place + off + (0 if self.reg is None else 1)) % 3

    def has_prep(self):
        return self.reg is not None or -2 <= self.place <= B - 3

    def has_max(self):
        return self.reg is not None or -1 <= self.place <= B - 2

    def has_main(self):
        return self.reg is not None or 0 <= self.place <= B - 1

    def has_final(self):
        return self.reg is not None or 1 <= self.place <= B


LOOPS = 9
HEAD_STEPS = [Step(b) for b in (-2, -1, 0)]
TAIL_STEPS = [Step(b) for b in range(3 * LOOPS + 1, B + 1)]

NSLOT = 4
MAXES = NTH * H
EARLY = 10
M_START, M_END = 2, 36
T_AT = M_END + 3
OTHERS = ((2, ("K", 0)), (5, ("K", 1)), (8, ("K", 2)), (10, ("O", 0)), (13, ("A", 0)), (17, ("W", 0)),
          (20, ("V", 0)), (24, ("V", 1)), (28, ("V", 2)), (32, ("V", 3)), (36, ("V", 4)), (42, ("V", 5)))


def _slot_users():
    late = MAXES - EARLY
    users = [(M_START + n * (M_END - M_START) // (late - 1), ("M", EARLY + n)) for n in range(late)]
    users += [(T_AT + 1 + n * (UNITS - 1 - T_AT) // EARLY, ("N", n)) for n in range(EARLY)]
    users = sorted([*users, *OTHERS, (T_AT, ("T", 0))], key=lambda u: u[0])
    return [(*user, at) for at, user in users]


USERS = _slot_users()
DVE_USERS = [u for u in USERS if u[0] != "K"]
for _u in (u for u in USERS if u[0] == "K"):
    DVE_USERS.insert(USERS.index(_u) + 3, _u)
SLOT = {(k, i): n % NSLOT for n, (k, i, _) in enumerate(USERS)}
PER_STEP = [sum(v == n for v in SLOT.values()) for n in range(NSLOT)]


def _present(step, kind):
    return {"K": step.has_prep, "V": step.has_prep, "N": step.has_prep, "M": step.has_max, "T": step.has_max,
            "O": step.has_final, "A": step.has_final, "W": step.has_final}[kind]()


def _uses(place, slot):
    step = Step(place)
    return sum(_present(step, k) and SLOT[k, i] == slot for k, i, _ in USERS)


def slot_count(step, kind, idx):
    slot = SLOT[kind, idx]
    rank = 0
    for k, i, _ in USERS:
        if SLOT[k, i] == slot and _present(step, k):
            rank += 1
        if (k, i) == (kind, idx):
            break
    if step.reg is None:
        return sum(_uses(p, slot) for p in range(-2, step.place)) + rank
    return step.lin(PER_STEP[slot], sum(_uses(p, slot) for p in range(-2, 1)) - PER_STEP[slot] + rank)


def groups(eng, ahead, behind):
    ahead(0, 0)
    with eng.Fori(0, NG // 2 - 1) as i:
        for u in range(2):
            ahead(2 * i + (u + 1), 1 - u)
            behind(2 * i + u, u)
    ahead(NG - 1, 1)
    behind(NG - 2, 0)
    behind(NG - 1, 1)


def attention(nc, env, lay, W, scr, x_sb):
    (ctxT, wq, bq, wk, bk, wv, bv, wo, bo) = W
    kscr, qscr, mscr = scr
    ident, tg = env["ident"], env["tg"]

    sem = Semaphores(nc, f"a{lay}")
    st = ExitStack()
    with st:
        sb = lambda name, shape, dt=F32: st.enter_context(nc.sbuf_tensor(f"{name}{lay}", shape, dt))

        wq_sb, bq_sb = sb("wq", [D, D]), sb("bq", [D, 1])
        wk_sb, bk_sb, wv_sb = sb("wk", [DC, D]), sb("bk", [D, 1]), sb("wv", [DC, D])
        bv_sb, wo_sb, bo_sb = sb("bv", [NQ, D]), sb("wo", [D, D]), sb("bo", [NQ, D])

        stat, mv = env["stat"], sb("mv", [NQ, B, 2])
        rstd, nmr = sb("rstd", [NQ, B]), sb("nmr", [NQ, B])
        xn, xnT = sb("xn", [NQ, 2, G, D]), sb("xnT", [D, 2, GT])
        q32, qr = sb("q32", [D, GT]), sb("qr", [D, 2, GT])
        qs = sb("qs", [D, 3, 4, GT], BF16)
        w_in, stats, var_ok, std_ok, rstd_ok = (sem(n) for n in ("w_in", "stats", "var_ok", "std_ok", "rstd_ok"))
        ln_ok, ln_T, ln_T_out, q_mm = (sem(n) for n in ("ln_ok", "ln_T", "ln_T_out", "q_mm"))
        q_full, q_hi, q_res, q_mid, q_split = (sem(n) for n in ("q_full", "q_hi", "q_res", "q_mid", "q_split"))
        q_out = [sem(f"q_out{u}_") for u in range(4)]

        ctx_sb = sb("ctx", [DC, 3, NK])
        k32, kr = sb("k32", [D, NK]), sb("kr", [D, NK])
        ks = sb("ks", [D, 3, NK], BF16)
        Kp, Qp, V = env["Kp"], env["Qp"], env["V"]
        probs = sb("probs", [P, NP_, QW])
        mx, mmax = sb("mx", [NQ, NTH, H]), sb("mmax", [NQ, H])
        mr = sb("mr", [H, NQ])
        mT = sb("mT", [H, 3, NQ], BF16)
        oT = sb("oT", [P, QW])
        rden, heads = sb("rden", [NQ, H]), sb("heads", [NQ, D])
        headsT, gated = sb("headsT", [D, NQ]), sb("gated", [NQ, D])

        pb = lambda name, shape: st.enter_context(nc.psum_tensor(f"{name}{lay}", shape, F32))
        slots = [pb(f"slot{n}_", [P, 512]) for n in range(NSLOT)]
        scores, o_ps = pb("scores", [P, NE, 512]), pb("o_ps", [P, 512])

        slot_full = [sem(f"slot{n}_full") for n in range(NSLOT)]
        slot_read = [sem(f"slot{n}_read") for n in range(NSLOT)]
        ctx_in = [sem(f"ctx_in{i}_") for i in range(3)]
        pack_in = [sem(f"pack_in{i}_") for i in range(3)]
        shift_in = [sem(f"shift_in{i}_") for i in range(3)]
        init, k_evac, k_res, k_split, k_out = (sem(n) for n in ("init", "k_evac", "k_res", "k_split", "k_out"))
        scored, exped, pv_done, o_evac = (sem(n) for n in ("scored", "exped", "pv_done", "o_evac"))
        m_ready, m_hi, m_mid, m_split, m_out = (
            sem(n) for n in ("m_ready", "m_hi", "m_mid", "m_split", "m_out"))
        den_ok, heads_ok, x_ok = (sem(n) for n in ("den_ok", "heads_ok", "x_ok"))

        def user_wait(eng, sems, step, kind, idx):
            eng.wait_ge(sems[SLOT[kind, idx]], slot_count(step, kind, idx))

        def users_at(step, s):
            return [(k, i) for k, i, at in USERS if at == s and _present(step, k)]

        xnT_ps = [scores[:, 0], scores[:, 1]]
        q_ps = [scores[:, 2], o_ps[:]]

        def run(eng, body):
            for step in HEAD_STEPS:
                body(step)
            with eng.Fori(0, LOOPS) as i:
                for u in range(3):
                    body(Step(u, i))
            for step in TAIL_STEPS:
                body(step)

        def at_batch(step, off):
            return step.lin(1, off)

        with nc.Block() as block:
            @block.sync
            def _(sp):
                def write_k(step):
                    sp.wait_ge(k_split, step.lin(NTH, 3 * NTH))
                    sp.dma_start(kscr[step.mod3(2)].rearrange("t p n -> p t n"), ks[:]).then_inc(k_out, 16)

                def pack_k(step):
                    nb = step.mod3(2)
                    sp.wait_ge(k_out, step.lin(16, 3 * 16))
                    for t, part in enumerate(TERMS):
                        r = 2 * t * HD
                        sp.dma_start(Kp[r:r + 2 * HD, nb, :, :],
                                     kscr[nb, part].rearrange("(r g) n -> r g n", g=PAIRS))\
                          .then_inc(pack_in[nb], 16)

                def pack_q(step, terms=range(len(QTERMS))):
                    nb = step.mod3(2)
                    for t in terms:
                        part = QTERMS[t]
                        for hh in range(2):
                            r = (2 * t + hh) * HD
                            src = qscr[part, hh * 64:(hh + 1) * 64, bass.ds(step.lin(NQ, 2 * NQ), NQ)]
                            dst = Qp[r:r + HD, nb, :].rearrange("d (g a c) -> d g a c", g=PAIRS, a=2)
                            sp.dma_start(dst[:, :, hh, :], src.rearrange("(d g) c -> d g c", g=PAIRS))\
                              .then_inc(pack_in[nb], 16)

                def write_queries(n, u):
                    sp.wait_ge(q_split, n + 1)
                    sp.dma_start(qscr[:, :, bass.ds(n * GT, GT)].rearrange("t p c -> p t c"), qs[:, :, u, :])\
                      .then_inc(q_out[u], 16)

                def body(step):
                    if step.reg is not None or -2 <= step.place <= B - 4:
                        nb = step.mod3(3)
                        if step.reg is not None or step.place >= 1:
                            sp.wait_ge(scored, step.lin(UNITS))
                        elif step.place == 0:
                            user_wait(sp, slot_full, Step(-2), "V", VS - 1)
                        sp.dma_start(ctx_sb[:, nb, :], ctxT[bass.ds(step.lin(DC, 3 * DC), DC), :])\
                          .then_inc(ctx_in[nb], 16)
                    if step.reg is None and step.place == -2:
                        write_k(step)
                        for n in range(NG):
                            write_queries(n, n % 4)
                            if n == 1:
                                pack_k(step)
                                sp.wait_ge(q_out[0], 16)
                            if 1 <= n <= 3:
                                pack_q(step, range(2 * n - 2, 2 * n))
                    elif step.has_prep():
                        if step.reg is None and step.place == 0:
                            for u in range(4):
                                sp.wait_ge(q_out[u], 16 * (NG // 4))
                        if step.reg is not None or step.place >= 1:
                            sp.wait_ge(scored, step.lin(UNITS))
                        pack_q(step)
                        write_k(step)
                        pack_k(step)
                    if step.has_max():
                        nb = step.mod3(1)
                        sp.wait_ge(m_split, step.lin(1, 2))
                        sp.dma_start(mscr[nb].rearrange("t h c -> h t c"), mT[:]).then_inc(m_out, 16)
                        sp.wait_ge(m_out, step.lin(16, 2 * 16))
                        sp.dma_start(Qp[ROWS:ROWS + SH, nb, :], mscr[nb].rearrange("t h c -> t (h c)"))\
                          .then_inc(shift_in[nb], 16)

                sp.dma_start(ctx_sb[:, 0, :], ctxT[0:DC, :]).then_inc(ctx_in[0], 16)
                for dst, src in ((wk_sb, wk), (bk_sb, bk), (wv_sb, wv), (wq_sb, wq), (bq_sb, bq), (wo_sb, wo)):
                    sp.dma_start(dst[:], src).then_inc(w_in, 16)
                sp.dma_start(bv_sb[:], bv.partition_broadcast(NQ)).then_inc(w_in, 16)
                sp.dma_start(bo_sb[:], bo.partition_broadcast(NQ)).then_inc(w_in, 16)
                run(sp, body)

            @block.gpsimd
            def _(pool):
                def body(step):
                    if step.has_prep():
                        for i in range(NTH):
                            third = slice(CUT[i], CUT[i + 1])
                            pool.wait_ge(k_evac, step.lin(NTH, 2 * NTH + i + 1))
                            nc.gpsimd.tensor_tensor(kr[:, third], k32[:, third], ks[:, 0, third],
                                                    ALU.subtract).then_inc(k_res, 1)
                            nc.gpsimd.tensor_tensor(ks[:, 1, third], k32[:, third], ks[:, 0, third],
                                                    ALU.subtract).then_inc(k_res, 1)
                            pool.wait_ge(k_res, step.lin(2 * NTH, 4 * NTH + 2 * (i + 1)))
                            nc.gpsimd.tensor_tensor(ks[:, 2, third], kr[:, third], ks[:, 1, third],
                                                    ALU.subtract).then_inc(k_split, 1)
                    if step.reg is None and step.place == -2:
                        for n in range(NG):
                            pool.wait_ge(q_mid, n + 1)
                            nc.gpsimd.tensor_tensor(qs[:, 2, n % 4, :], qr[:, n % 2, :], qs[:, 1, n % 4, :], ALU.subtract)\
                              .then_inc(q_split, 1)

                run(pool, body)

            @block.scalar
            def _(act):
                def evac_k(step, i):
                    if i == 0 and (step.reg is not None or step.place >= -1):
                        act.wait_ge(k_split, step.lin(NTH, 2 * NTH))
                    user_wait(act, slot_full, step, "K", i)
                    nc.scalar.activation(k32[:, CUT[i]:CUT[i + 1]], slots[SLOT["K", i]][:, 0:CUT[i + 1] - CUT[i]],
                                         ACT.Identity, bias=bk_sb[:, 0:1]).then_inc(slot_read[SLOT["K", i]], 1)

                def evac_v(step, i):
                    nb, slot = step.mod3(2), SLOT["V", i]
                    if i == 0 and (step.reg is not None or step.place >= 1):
                        act.wait_ge(pv_done, step.lin(UNITS))
                    user_wait(act, slot_full, step, "V", i)
                    w = KW[2 * i]
                    src = slots[slot][0:w, 0:2 * D].rearrange("p (t h d) -> p t h d", t=2, h=H)
                    nc.scalar.activation(V[0:w, nb, 2 * i:2 * i + 2, :, 0:HD], src, ACT.Copy)\
                      .then_inc(slot_read[slot], 1)

                def normalise(n, u):
                    act.wait_ge(ln_T, n + 1)
                    for j in range(G):
                        nc.scalar.activation(xn[:, u, j, :], x_sb[:, bass.ds(n * (G * D) + j * D, D)], ACT.Identity,
                                             bias=nmr[:, bass.ds(n * G + j, 1)],
                                             scale=rstd[:, bass.ds(n * G + j, 1)]).then_inc(ln_ok, 1)

                def evac_transposes(n, u):
                    act.wait_ge(ln_T, n + 3)
                    nc.scalar.activation(xnT[:, u, :], xnT_ps[u][:, 0:GT], ACT.Copy).then_inc(ln_T_out, 1)

                def queries():
                    act.wait_ge(var_ok, 1)
                    nc.scalar.activation(rstd[:], rstd[:], ACT.Sqrt).then_inc(std_ok, 1)
                    act.wait_ge(rstd_ok, 2)
                    groups(act, normalise, evac_transposes)

                def body(step):
                    for s in range(UNITS):
                        if step.reg is None and step.place == -2 and s == T_AT + 1:
                            queries()
                        if step.has_main():
                            w = KW[s // QUADS]
                            act.wait_ge(scored, step.lin(UNITS, s + 1))
                            if step.reg is not None or UNITS * step.place + s >= NP_:
                                act.wait_ge(pv_done, step.lin(UNITS, s - NP_ + 1))
                            nc.scalar.activation(probs[0:w, s % NP_, :], scores[0:w, s % NE, 0:QW], ACT.Exp)\
                              .then_inc(exped, 1)
                        if s == LAG - 1 and step.has_final():
                            act.wait_ge(pv_done, step.lin(UNITS))
                            nc.scalar.activation(oT[:], o_ps[:, 0:QW], ACT.Copy).then_inc(o_evac, 1)
                        for kind, i in users_at(step, s):
                            if kind == "K":
                                evac_k(step, i)
                            elif kind == "V":
                                evac_v(step, i)

                act.wait_ge(w_in, 16 * 8)
                run(act, body)

            @block.vector
            def _(dve):
                def high_part(step, i):
                    if i == 0 and (step.reg is not None or step.place >= -1):
                        dve.wait_ge(k_out, step.lin(16, 2 * 16))
                    user_wait(dve, slot_read, step, "K", i)
                    cols = slice(CUT[i], CUT[i + 1])
                    nc.vector.tensor_copy(ks[:, 0, cols], k32[:, cols]).then_inc(k_evac, 1)

                def split_queries(n, u):
                    dve.wait_ge(q_mm, n + 1)
                    nc.vector.tensor_scalar(q32[:], q_ps[u][:, 0:GT], bq_sb[:, 0:1], HD ** -0.5, ALU.add,
                                            ALU.mult).then_inc(q_full, 1)
                    dve.wait_ge(q_full, n + 3)
                    if n >= 2:
                        dve.wait_ge(q_split, n - 1)
                    part = [qs[:, t, n % 4, :] for t in range(2)]
                    nc.vector.tensor_copy(part[0], q32[:]).then_inc(q_hi, 1)
                    dve.wait_ge(q_hi, n + 1)
                    nc.vector.tensor_tensor(qr[:, u, :], q32[:], part[0], ALU.subtract).then_inc(q_res, 1)
                    dve.wait_ge(q_res, n + 1)
                    nc.vector.tensor_copy(part[1], qr[:, u, :]).then_inc(q_mid, 1)

                def queries():
                    layer_norm_scale(nc, dve, stat, mv, rstd, nmr, (stats, var_ok, std_ok, rstd_ok),
                                     B if lay == 0 else 0)
                    dve.wait_ge(w_in, 16 * 8)
                    for n in range(NG):
                        if n >= 4:
                            dve.wait_ge(q_out[n % 4], 16 * (n // 4))
                        split_queries(n, n % 2)
                    nc.vector.memset(o_ps[:], 0.0).then_inc(init, 1)

                def body(step):
                    for kind, i, _ in DVE_USERS:
                        if step.reg is None and step.place == -2 and (kind, i) == ("N", 0):
                            queries()
                        if kind == "V" or not _present(step, kind):
                            continue
                        if kind == "K":
                            high_part(step, i)
                            continue
                        slot = slots[SLOT[kind, i]]
                        user_wait(dve, slot_full, step, kind, i)
                        freed = slot_read[SLOT[kind, i]]
                        if kind in "MN":
                            nc.vector.tensor_reduce(mx[:, i % NTH, i // NTH:i // NTH + 1],
                                                    slot[0:NQ, 0:CUT[i % NTH + 1] - CUT[i % NTH]], AX.X,
                                                    ALU.max).then_inc(freed, 1)
                            if i == MAXES - 1:
                                user_wait(dve, slot_read, step, "M", i)
                                nc.vector.tensor_reduce(mmax[:], mx[:].rearrange("c t h -> c h t"), AX.X,
                                                        ALU.max).then_inc(m_ready, 1)
                        elif kind == "T":
                            mps = slot[0:H, 0:NQ]
                            if step.reg is not None or step.place >= 0:
                                dve.wait_ge(m_out, step.lin(16, 16))
                            nc.vector.tensor_scalar_mul(mT[:, 0, :], mps, -1.0).then_inc(m_hi, 1)
                            dve.wait_ge(m_hi, step.lin(1, 2))
                            nc.vector.scalar_tensor_tensor(mr[:], mps, -1.0, mT[:, 0, :], ALU.mult,
                                                           ALU.subtract).then_inc(freed, 1)
                            user_wait(dve, slot_read, step, "T", 0)
                            nc.vector.tensor_copy(mT[:, 1, :], mr[:]).then_inc(m_mid, 1)
                            dve.wait_ge(m_mid, step.lin(1, 2))
                            nc.vector.tensor_tensor(mT[:, 2, :], mr[:], mT[:, 1, :], ALU.subtract)\
                              .then_inc(m_split, 1)
                        elif kind == "O":
                            ov = slot[0:NQ, :].rearrange("c (h e) -> c h e", h=H)
                            nc.vector.reciprocal(rden[:], ov[:, :, HD]).then_inc(den_ok, 1)
                            dve.wait_ge(den_ok, at_batch(step, 0))
                            hv = heads[:].rearrange("c (h d) -> c h d", h=H)
                            nc.vector.tensor_tensor(hv, ov[:, :, 0:HD],
                                                    rden[:].unsqueeze(2).to_broadcast([NQ, H, HD]), ALU.mult)\
                              .then_inc(freed, 1)
                            user_wait(dve, slot_read, step, "O", 0)
                            nc.vector.tensor_tensor(heads[:], heads[:], bv_sb[:], ALU.add).then_inc(heads_ok, 1)
                        elif kind == "A":
                            nc.vector.tensor_copy(headsT[:], slot[:, 0:NQ]).then_inc(freed, 1)
                        elif kind == "W":
                            nc.vector.tensor_tensor(gated[:], slot[0:NQ, 0:D], bo_sb[:], ALU.add)\
                              .then_inc(freed, 1)
                            user_wait(dve, slot_read, step, "W", 0)
                            xb = x_sb[:, bass.ds(step.lin(D, -D), D)]
                            nc.vector.scalar_tensor_tensor(xb, gated[:], tg[0:NQ, lay:lay + 1], xb, ALU.mult,
                                                           ALU.add).then_inc(x_ok, 1)
                            dve.wait_ge(x_ok, at_batch(step, 0))
                            nc.vector.bn_stats(stat[:, bass.ds(step.lin(1, -1), 1), :].rearrange("p o s -> p (o s)"),
                                               xb)

                if lay == 0:
                    dve.wait_ge(env["x_in"], 16)
                    batch_stats(nc, dve, lambda off: x_sb[:, bass.ds(off, D)], stat, stats)
                run(dve, body)

            @block.tensor
            def _(pe):
                def project_k(step, i):
                    nb = step.mod3(2)
                    if i == 0:
                        pe.wait_ge(ctx_in[nb], third(step, 2, 16))
                    return nc.tensor.matmul(slots[SLOT["K", i]][:, 0:CUT[i + 1] - CUT[i]], wk_sb[:],
                                            ctx_sb[:, nb, CUT[i]:CUT[i + 1]], start=True, stop=True)

                def project_v(step, i):
                    nb, slot = step.mod3(2), slots[SLOT["V", i]]
                    for n in range(2 * i, 2 * i + 2):
                        c = (n % 2) * D
                        last = nc.tensor.matmul(slot[0:KW[n], c:c + D], ctx_sb[:, nb, KS[n]:KS[n] + KW[n]],
                                                wv_sb[:], start=True, stop=True)
                    return last

                def third(step, off, mult):
                    if step.reg is None:
                        return mult * ((step.place + off) // 3 + 1)
                    return step.reg * mult + mult * ((1 + step.place + off) // 3 + 1)

                def max_unit(step, kind, i):
                    ahead = 2 if kind == "N" else 1
                    nb, h, part = step.mod3(ahead), i // NTH, i % NTH
                    if i == 0:
                        pe.wait_ge(pack_in[nb], third(step, ahead, 16 * (2 * len(QTERMS) + len(TERMS))))
                    return nc.tensor.matmul(slots[SLOT[kind, i]][0:NQ, 0:CUT[part + 1] - CUT[part]],
                                            Qp[0:ROWS, nb, h * NQ:(h + 1) * NQ],
                                            Kp[0:ROWS, nb, h // 2, CUT[part]:CUT[part + 1]],
                                            start=True, stop=True)

                def use_slot(step, kind, i):
                    count = slot_count(step, kind, i)
                    if step.reg is not None or count > 1:
                        pe.wait_ge(slot_read[SLOT[kind, i]], count - 1)
                    slot = slots[SLOT[kind, i]]
                    if kind == "K":
                        last = project_k(step, i)
                    elif kind == "V":
                        last = project_v(step, i)
                    elif kind in "MN":
                        last = max_unit(step, kind, i)
                    elif kind == "T":
                        pe.wait_ge(m_ready, at_batch(step, 2))
                        last = nc.tensor.transpose(slot[0:H, 0:NQ], mmax[:], ident[0:NQ, 0:NQ])
                    elif kind == "O":
                        pe.wait_ge(o_evac, at_batch(step, 0))
                        for q in range(QUADS):
                            last = nc.tensor.transpose(slot[0:NQ, q * P:(q + 1) * P], oT[:, q * NQ:(q + 1) * NQ],
                                                       ident[:])
                    elif kind == "A":
                        pe.wait_ge(heads_ok, at_batch(step, 0))
                        last = nc.tensor.transpose(slot[:, 0:NQ], heads[:], ident[0:NQ, 0:NQ])
                    elif kind == "W":
                        user_wait(pe, slot_read, step, "A", 0)
                        last = nc.tensor.matmul(slot[0:NQ, 0:D], headsT[:], wo_sb[:], start=True, stop=True)
                    last.then_inc(slot_full[SLOT[kind, i]], 1)

                def score_unit(step, s):
                    nb, n, q = step.mod3(), s // QUADS, s % QUADS
                    if s == 0:
                        pe.wait_ge(shift_in[nb], third(step, 0, 16))
                    if step.reg is not None or UNITS * step.place + s >= NE:
                        pe.wait_ge(exped, step.lin(UNITS, s - NE + 1))
                    for a in range(2):
                        g = 2 * q + a
                        last = nc.tensor.matmul(scores[0:KW[n], s % NE, a * 2 * NQ:(a + 1) * 2 * NQ],
                                                Kp[0:ROWS + SH, nb, g, KS[n]:KS[n] + KW[n]],
                                                Qp[0:ROWS + SH, nb, g * 2 * NQ:(g + 1) * 2 * NQ],
                                                start=True, stop=True)
                    last.then_inc(scored, 1)

                def pv_unit(step, s, back):
                    nb, n, q = step.mod3(-back), s // QUADS, s % QUADS
                    if s == 0:
                        if step.reg is not None or step.place >= 1:
                            pe.wait_ge(o_evac, at_batch(step, 0))
                    pe.wait_ge(exped, step.lin(UNITS, s + 1 - back * UNITS))
                    for j in range(4):
                        last = nc.tensor.matmul(o_ps[32 * j:32 * j + HD + 1, q * NQ:(q + 1) * NQ],
                                                V[0:KW[n], nb, n, 4 * q + j, :],
                                                probs[0:KW[n], s % NP_, j * NQ:(j + 1) * NQ],
                                                start=(n == 0 and q == 0), stop=(n == KT - 1),
                                                skip_group_check=True)
                    last.then_inc(pv_done, 1)

                def transpose_group(n, u):
                    pe.wait_ge(ln_ok, n * G + G)
                    for j in range(G):
                        last = nc.tensor.transpose(xnT_ps[u][:, j * NQ:(j + 1) * NQ], xn[:, u, j, :],
                                                   ident[0:NQ, 0:NQ])
                    last.then_inc(ln_T, 1)

                def project_queries(n, u):
                    pe.wait_ge(ln_T_out, n + 1)
                    pe.wait_ge(q_full, n + 1)
                    nc.tensor.matmul(q_ps[u][:, 0:GT], wq_sb[:], xnT[:, u, :], start=True, stop=True)\
                      .then_inc(q_mm, 1)

                def queries():
                    pe.sem_inc(ln_T, 2)
                    pe.sem_inc(q_full, 2)
                    groups(pe, transpose_group, project_queries)
                    pe.wait_ge(init, 1)

                def body(step):
                    for s in range(UNITS):
                        if step.reg is None and step.place == -2 and s == T_AT + 1:
                            queries()
                        if step.reg is None and step.place == 0 and s == 0:
                            pe.wait_ge(env["ones_in"], 16)
                        if step.has_main():
                            score_unit(step, s)
                        if s < LAG:
                            if step.has_final():
                                pv_unit(step, UNITS - LAG + s, 1)
                        elif step.has_main():
                            pv_unit(step, s - LAG, 0)
                        for kind, i in users_at(step, s):
                            use_slot(step, kind, i)

                pe.wait_ge(w_in, 16 * 8)
                run(pe, body)
    sem.clear()


def batch_stats(nc, dve, x_of, stat, stats, ready=None):
    with dve.Fori(0, B // 8) as i:
        for j in range(8):
            if ready is not None:
                dve.wait_ge(ready, i * 8 + (j + 1))
            nc.vector.bn_stats(stat[:, bass.ds(i * 8 + j, 1), :].rearrange("p o s -> p (o s)"),
                               x_of(i * (8 * D) + j * D)).then_inc(stats, 1)
    dve.wait_ge(stats, B)


def layer_norm_scale(nc, dve, stat, mv, rstd, nmr, sems, before):
    stats, var_ok, std_ok, rstd_ok = sems
    for b in range(B):
        nc.vector.bn_aggr(mv[:, b, :], stat[:, b, :]).then_inc(stats, 1)
    dve.wait_ge(stats, before + B)
    nc.vector.tensor_scalar_add(rstd[:], mv[:, :, 1], EPS).then_inc(var_ok, 1)
    dve.wait_ge(std_ok, 1)
    nc.vector.reciprocal(rstd[:], rstd[:]).then_inc(rstd_ok, 1)
    dve.wait_ge(rstd_ok, 1)
    nc.vector.scalar_tensor_tensor(nmr[:], mv[:, :, 0], -1.0, rstd[:], ALU.mult,
                                   ALU.mult).then_inc(rstd_ok, 1)


def bc(ap, n):
    return ap.unsqueeze(2).to_broadcast([ap.shape[0], ap.shape[1], n])


def bm(ap, n):
    return ap.unsqueeze(1).to_broadcast([ap.shape[0], n, ap.shape[1]])


def top_two(nc, link, L, L2, desc, cand, f1, f2, mx, E):
    for n, (src, f) in enumerate(((L, f1), (L2, f2))):
        link(nc.vector.tensor_tensor(cand, src, bc(mx, E), ALU.is_ge))
        link(nc.vector.tensor_tensor(cand, cand, desc, ALU.mult))
        link(nc.vector.tensor_reduce(mx, cand, AX.X, ALU.max))
        link(nc.vector.tensor_tensor(f, cand, bc(mx, E), ALU.is_equal))
        if n == 0:
            link(nc.vector.scalar_tensor_tensor(L2, f, -1e30, L, ALU.mult, ALU.add))
            link(nc.vector.tensor_reduce(mx, L2, AX.X, ALU.max))
    link(nc.vector.tensor_tensor(f1, f1, f2, ALU.add))


def expert_attention(nc, env, W, x_sb):
    sim, gates, wqk, wv, wo = W
    E, HE = 16, 64
    EP = E // 2
    ident, tg = env["ident"], env["tg"]
    sem = Semaphores(nc, "f")
    st = ExitStack()
    with st:
        sb = lambda name, shape, dt=F32: st.enter_context(nc.sbuf_tensor(f"{name}_f", shape, dt))
        wqk_sb, wv_sb, wo_sb = sb("wqk", [D, E, 2 * HE]), sb("wve", [D, E, HE]), sb("woe", [P, EP, D])
        causal = sb("causal", [NQ, NQ])
        rstd, nmr, rw = sb("rstd", [NQ, B]), sb("nmr", [NQ, B]), sb("rw", [NQ, B, E])

        with ExitStack() as s1:
            sg_ = lambda name, shape, dt=F32: s1.enter_context(nc.sbuf_tensor(f"{name}_g", shape, dt))
            sim_sb, ssq, snorm, ones = sg_("sim", [D, E]), sg_("ssq", [D, E]), sg_("snorm", [D, E]), sg_("ones", [D, D])
            gs = sg_("gs", [NQ, E])
            stat, mv = env["stat"], sg_("mv", [NQ, B, 2])
            xn, sq, xnT = sg_("xn", [NQ, 2, G, D]), sg_("sq", [NQ, 2, G, D]), sg_("xnT", [D, 2, GT])
            ss = sg_("ss", [NQ, B])
            L, L2, cand = sg_("L", [NQ, B, E]), sg_("L2", [NQ, B, E]), sg_("cand", [NQ, B, E])
            f1, f2, mask = sg_("f1", [NQ, B, E]), sg_("f2", [NQ, B, E]), sg_("mask", [NQ, B, E])
            gated = sg_("gated", [NQ, B, E])
            mx, top, idle = sg_("mx", [NQ, B]), sg_("top", [NQ, B]), sg_("idle", [NQ, B])
            desc_i, desc = sg_("desc_i", [NQ, E], mybir.dt.int32), sg_("desc", [NQ, E])
            xnT_ps = s1.enter_context(nc.psum_tensor("xnT_ps_g", [P, 2, 512], F32))
            log_ps = s1.enter_context(nc.psum_tensor("log_ps_g", [P, 2, 512], F32))
            sim_ps = s1.enter_context(nc.psum_tensor("sim_ps_g", [P, 512], F32))
            sim_in, w_in, stats, var_ok, std_ok, rstd_ok = (
                sem(n) for n in ("sim_in", "w_in", "stats", "var_ok", "std_ok", "rstd_ok"))
            sim_sq, sim_sum, sim_root, sim_n, sig_exp = (
                sem(n) for n in ("sim_sq", "sim_sum", "sim_root", "sim_n", "sig_exp"))
            ln_ok, sq_ok, sq_read, ln_T, ln_T_out, logit_mm, logit_ok = (
                sem(n) for n in ("ln_ok", "sq_ok", "sq_read", "ln_T", "ln_T_out", "logit_mm", "logit_ok"))
            norm_root, pre_exp, gate_exp, chain, iota_ok = (
                sem(n) for n in ("norm_root", "pre_exp", "gate_exp", "chain", "iota_ok"))

            with nc.Block() as block:
                @block.sync
                def _(sp):
                    sp.dma_start(sim_sb[:], sim).then_inc(sim_in, 16)
                    sp.dma_start(gs[:], gates.partition_broadcast(NQ)).then_inc(sim_in, 16)
                    sp.dma_start(wqk_sb[:], wqk).then_inc(w_in, 16)
                    sp.dma_start(wv_sb[:], wv).then_inc(w_in, 16)
                    sp.dma_start(wo_sb[:], wo).then_inc(w_in, 16)
                    sp.wait_ge(w_in, 48)

                @block.gpsimd
                def _(pool):
                    nc.gpsimd.iota(desc_i[:], [[-1, E]], base=E, channel_multiplier=0).then_inc(iota_ok, 1)
                    nc.gpsimd.memset(causal[:], 0.0).then_inc(iota_ok, 1)
                    pool.wait_ge(iota_ok, 2)
                    nc.gpsimd.affine_select(out=causal[:], in_=causal[:], compare_op=ALU.is_ge, fill=-1e30, base=0,
                                            pattern=[[-1, NQ]], channel_multiplier=1).then_inc(iota_ok, 1)
                    with pool.Fori(0, NG // 2) as i:
                        for u in range(2):
                            pool.wait_ge(ln_ok, i * (2 * G) + (u + 1) * G)
                            pool.wait_ge(sq_read, 2 * i + (u + 1))
                            nc.gpsimd.tensor_tensor(sq[:, u], xn[:, u], xn[:, u], ALU.mult).then_inc(sq_ok, 1)

                @block.scalar
                def _(act):
                    act.wait_ge(sim_in, 32)
                    nc.scalar.activation(gs[:], gs[:], ACT.Exp, scale=-1.0).then_inc(sig_exp, 1)
                    act.wait_ge(var_ok, 1)
                    nc.scalar.activation(rstd[:], rstd[:], ACT.Sqrt).then_inc(std_ok, 1)
                    act.wait_ge(sim_sum, 1)
                    nc.scalar.activation(snorm[:], sim_ps[:, 0:E], ACT.Sqrt).then_inc(sim_root, 1)
                    act.wait_ge(rstd_ok, 2)
                    with act.Fori(0, NG // 2) as i:
                        for u in range(2):
                            n = 2 * i + u
                            act.wait_ge(ln_T, n + 1)
                            act.wait_ge(sq_read, n + 1)
                            for j in range(G):
                                off = i * (2 * G) + (u * G + j)
                                nc.scalar.activation(
                                    xn[:, u, j, :], x_sb[:, bass.ds(i * (2 * G * D) + (u * G + j) * D, D)],
                                    ACT.Identity, bias=nmr[:, bass.ds(off, 1)],
                                    scale=rstd[:, bass.ds(off, 1)]).then_inc(ln_ok, 1)
                    act.wait_ge(sq_read, NG + 2)
                    nc.scalar.activation(ss[:], ss[:], ACT.Sqrt).then_inc(norm_root, 1)
                    act.wait_ge(pre_exp, 1)
                    nc.scalar.activation(L[:], gated[:], ACT.Exp).then_inc(gate_exp, 1)

                @block.tensor
                def _(pe):
                    pe.sem_inc(ln_T, 2)
                    pe.wait_ge(sim_sq, 2)
                    nc.tensor.matmul(sim_ps[:, 0:E], ones[:], ssq[:], start=True, stop=True).then_inc(sim_sum, 1)

                    def transpose_group(n, u):
                        pe.wait_ge(ln_ok, n * G + G)
                        for j in range(G):
                            last = nc.tensor.transpose(xnT_ps[:, u, j * NQ:(j + 1) * NQ], xn[:, u, j, :],
                                                       ident[0:NQ, 0:NQ])
                        last.then_inc(ln_T, 1)

                    def logits(n, u):
                        pe.wait_ge(sim_n, 3)
                        pe.wait_ge(ln_T_out, n + 1)
                        for j in range(G):
                            last = nc.tensor.matmul(log_ps[0:NQ, u, j * E:(j + 1) * E],
                                                    xnT[:, u, j * NQ:(j + 1) * NQ], sim_sb[:],
                                                    start=True, stop=True)
                        last.then_inc(logit_mm, 1)

                    groups(pe, transpose_group, logits)

                @block.vector
                def _(dve):
                    done = [0]

                    def link(ins):
                        done[0] += 1
                        ins.then_inc(chain, 1)
                        dve.wait_ge(chain, done[0])

                    dve.sem_inc(sq_read, 2)
                    nc.vector.memset(ones[:], 1.0).then_inc(sim_sq, 1)
                    dve.wait_ge(sim_in, 32)
                    nc.vector.tensor_tensor(ssq[:], sim_sb[:], sim_sb[:], ALU.mult).then_inc(sim_sq, 1)
                    layer_norm_scale(nc, dve, stat, mv, rstd, nmr, (stats, var_ok, std_ok, rstd_ok), 0)
                    dve.wait_ge(sim_root, 1)
                    nc.vector.tensor_scalar_max(snorm[:], snorm[:], 1e-12).then_inc(sim_n, 1)
                    dve.wait_ge(sim_n, 1)
                    nc.vector.reciprocal(snorm[:], snorm[:]).then_inc(sim_n, 1)
                    dve.wait_ge(sim_n, 2)
                    nc.vector.tensor_tensor(sim_sb[:], sim_sb[:], snorm[:], ALU.mult).then_inc(sim_n, 1)
                    dve.wait_ge(sig_exp, 1)
                    link(nc.vector.tensor_scalar_add(gs[:], gs[:], 1.0))
                    link(nc.vector.reciprocal(gs[:], gs[:]))
                    dve.wait_ge(iota_ok, 1)
                    link(nc.vector.tensor_copy(desc[:], desc_i[:]))
                    Lf = L[:].rearrange("p b e -> p (b e)")

                    def evac_transposes(n, u):
                        dve.wait_ge(ln_T, n + 3)
                        nc.vector.tensor_copy(xnT[:, u, :], xnT_ps[:, u, 0:GT]).then_inc(ln_T_out, 1)
                        dve.wait_ge(sq_ok, n + 1)
                        nc.vector.tensor_reduce(ss[:, bass.ds(n * G, G)], sq[:, u], AX.X, ALU.add)\
                          .then_inc(sq_read, 1)

                    def evac_logits(n, u):
                        dve.wait_ge(logit_mm, n + 1)
                        nc.vector.tensor_copy(Lf[:, bass.ds(n * (G * E), G * E)],
                                              log_ps[0:NQ, u, 0:G * E]).then_inc(logit_ok, 1)

                    groups(dve, evac_transposes, evac_logits)
                    dve.wait_ge(logit_ok, NG)
                    dve.wait_ge(norm_root, 1)
                    link(nc.vector.tensor_scalar_max(ss[:], ss[:], 1e-12))
                    link(nc.vector.reciprocal(ss[:], ss[:]))
                    link(nc.vector.tensor_tensor(L[:], L[:], bc(ss[:], E), ALU.mult))
                    link(nc.vector.tensor_tensor(L[:], L[:], bm(gs[:], B), ALU.subtract))
                    link(nc.vector.tensor_reduce(top[:], L[:], AX.X, ALU.max))
                    nc.vector.tensor_scalar_max(gated[:], L[:], 0.0)
                    nc.vector.tensor_single_scalar(mask[:], L[:], 0.0, ALU.is_gt)
                    nc.vector.tensor_single_scalar(idle[:], top[:], 0.0, ALU.is_le)
                    link(nc.vector.tensor_copy(mx[:], top[:]))
                    top_two(nc, link, L[:], L2[:], bm(desc[:], B), cand[:], f1[:], f2[:], mx[:], E)
                    link(nc.vector.tensor_tensor(f1[:], f1[:], bc(idle[:], E), ALU.mult))
                    nc.vector.tensor_tensor(mask[:], mask[:], f1[:], ALU.add)
                    link(nc.vector.tensor_scalar_max(top[:], top[:], 0.0))
                    nc.vector.tensor_tensor(gated[:], gated[:], bc(top[:], E), ALU.subtract).then_inc(pre_exp, 1)
                    dve.wait_ge(gate_exp, 1)
                    link(nc.vector.tensor_tensor(L[:], L[:], mask[:], ALU.mult))
                    link(nc.vector.tensor_reduce(mx[:], L[:], AX.X, ALU.add))
                    link(nc.vector.reciprocal(mx[:], mx[:]))
                    link(nc.vector.tensor_tensor(rw[:], L[:], bc(mx[:], E), ALU.mult))

        xn, xs = sb("xnb", [NQ, D]), sb("xs", [NQ, E, D])
        xsT = sb("xsT", [D, E * NQ])
        qT, kT, v = sb("qT", [HE, NQ]), sb("kT", [HE, NQ]), sb("v", [NQ, HE])
        masked, nmax, den, rden = sb("masked", [NQ, NQ]), sb("nmax", [NQ, 1]), sb("den", [NQ, 1]), sb("rden", [NQ, 1])
        pr, prT, rwd = sb("pr", [NQ, NQ]), sb("prT", [NQ, NQ]), sb("rwd", [NQ, E])
        mixed, mixT = sb("mixed", [NQ, E, HE]), sb("mixT", [P, EP * NQ])
        pb = lambda name: st.enter_context(nc.psum_tensor(f"{name}_f", [P, 512], F32))
        T_ps = [pb("T_a"), pb("T_b")]
        qk_ps, v_ps, sc_ps, prT_ps, att_ps, out_ps = (
            pb(n) for n in ("qk_ps", "v_ps", "sc_ps", "prT_ps", "att_ps", "out_ps"))
        T_full, T_read, xn_ok, xs_ok, qk_mm, qk_out, v_mm, v_out = (
            sem(n) for n in ("T_full", "T_read", "xn_ok", "xs_ok", "qk_mm", "qk_out", "v_mm", "v_out"))
        sc_mm, masked_ok, nmax_ok, pr_ok, prT_full, prT_out, att_mm = (
            sem(n) for n in ("sc_mm", "masked_ok", "nmax_ok", "pr_ok", "prT_full", "prT_out", "att_mm"))
        rden_ok, rwd_ok, mixed_ok, out_mm, x_ok = (
            sem(n) for n in ("rden_ok", "rwd_ok", "mixed_ok", "out_mm", "x_ok"))

        class Two:

            def __init__(self, place, reg=None):
                self.place, self.reg = place, reg

            def lin(self, mult, off=0):
                if self.reg is None:
                    return mult * self.place + off
                return self.reg * (2 * mult) + (mult * (2 + self.place) + off)

            def on(self, lag):
                return self.reg is not None or 0 <= self.place - lag < B

        def T_use(step, k):
            if step.reg is not None:
                return step.lin(6, k - 4)
            first = sum(4 * Two(p).on(0) + 2 * Two(p).on(2) for p in range(step.place))
            return first + (k if step.on(0) else k - 4)

        def run(eng, body):
            for p in (-1, 0, 1):
                body(Two(p))
            with eng.Fori(0, (B - 4) // 2) as i:
                for u in range(2):
                    body(Two(u, i))
            for p in (B - 2, B - 1, B, B + 1):
                body(Two(p))

        with nc.Block() as block:
            @block.tensor
            def _(pe):
                def transposes(step, k, src, w):
                    n = T_use(step, k)
                    if step.reg is not None or n >= 2:
                        pe.wait_ge(T_read, n - 1)
                    for j in range(4):
                        last = nc.tensor.transpose(T_ps[k % 2][:, j * NQ:(j + 1) * NQ], src[:, 4 * (k % 4) + j, :],
                                                   ident[0:NQ, 0:NQ])
                    last.then_inc(T_full, 1)

                def body(step):
                    if step.on(0):
                        pe.wait_ge(xs_ok, step.lin(1, 1))
                        for k in range(2):
                            transposes(step, k, xs, D)
                    if step.on(1):
                        pe.wait_ge(qk_out, step.lin(1))
                        nc.tensor.matmul(sc_ps[0:NQ, 0:NQ], qT[:], kT[:], start=True, stop=True).then_inc(sc_mm, 1)
                    if step.on(0):
                        for k in range(2, 4):
                            transposes(step, k, xs, D)
                        for e in range(E):
                            if e % 4 == 0:
                                pe.wait_ge(T_read, T_use(step, e // 4) + 1)
                            last = nc.tensor.matmul(qk_ps[:, 0:NQ], wqk_sb[:, e, :], xsT[:, e * NQ:(e + 1) * NQ],
                                                    start=(e == 0), stop=(e == E - 1))
                        last.then_inc(qk_mm, 1)
                    if step.on(1):
                        pe.wait_ge(pr_ok, step.lin(1))
                        nc.tensor.transpose(prT_ps[0:NQ, 0:NQ], pr[:], ident[0:NQ, 0:NQ]).then_inc(prT_full, 1)
                    if step.on(2):
                        pe.wait_ge(mixed_ok, step.lin(1, -1))
                        mv_ = mixed[:].rearrange("p (j a) d -> p j (a d)", a=2)
                        for k in range(4, 6):
                            transposes(step, k, mv_, P)
                    if step.on(1):
                        pe.wait_ge(prT_out, step.lin(1))
                        pe.wait_ge(v_out, step.lin(1))
                        nc.tensor.matmul(att_ps[0:NQ, 0:HE], prT[:], v[:], start=True, stop=True)\
                          .then_inc(att_mm, 1)
                    if step.on(0):
                        if step.reg is not None or step.place >= 1:
                            pe.wait_ge(v_out, step.lin(1))
                        for e in range(E):
                            last = nc.tensor.matmul(v_ps[0:NQ, 0:HE], xsT[:, e * NQ:(e + 1) * NQ], wv_sb[:, e, :],
                                                    start=(e == 0), stop=(e == E - 1))
                        last.then_inc(v_mm, 1)
                    if step.on(2):
                        pe.wait_ge(x_ok, step.lin(1, -1))
                        for j in range(EP):
                            if j % 4 == 0:
                                pe.wait_ge(T_read, T_use(step, 4 + j // 4) + 1)
                            last = nc.tensor.matmul(out_ps[0:NQ, 0:D], mixT[:, j * NQ:(j + 1) * NQ], wo_sb[:, j, :],
                                                    start=(j == 0), stop=(j == EP - 1))
                        last.then_inc(out_mm, 1)

                pe.sem_inc(x_ok, 1)
                run(pe, body)

            @block.scalar
            def _(act):
                def evac(step, k, dst):
                    act.wait_ge(T_full, T_use(step, k) + 1)
                    nc.scalar.activation(dst[:, (k % 4) * GT:(k % 4 + 1) * GT], T_ps[k % 2][:, 0:GT], ACT.Copy)\
                      .then_inc(T_read, 1)

                def body(step):
                    if step.on(0):
                        for k in range(4):
                            evac(step, k, xsT)
                    if step.on(-1):
                        if step.reg is not None or step.place >= 0:
                            act.wait_ge(xs_ok, step.lin(1, 1))
                        nc.scalar.activation(xn[:], x_sb[:, bass.ds(step.lin(D, D), D)], ACT.Identity,
                                             bias=nmr[:, bass.ds(step.lin(1, 1), 1)],
                                             scale=rstd[:, bass.ds(step.lin(1, 1), 1)]).then_inc(xn_ok, 1)
                    if step.on(1):
                        act.wait_ge(nmax_ok, step.lin(1))
                        if step.reg is not None or step.place >= 2:
                            act.wait_ge(rden_ok, step.lin(1, -1))
                        nc.scalar.activation(pr[:], masked[:], ACT.Exp, bias=nmax[:, 0:1],
                                             accum_out=den[:, 0:1]).then_inc(pr_ok, 1)
                        act.wait_ge(prT_full, step.lin(1))
                        nc.scalar.activation(prT[:], prT_ps[0:NQ, 0:NQ], ACT.Copy).then_inc(prT_out, 1)
                    if step.on(2):
                        for k in range(4, 6):
                            evac(step, k, mixT)
                    if step.on(0):
                        act.wait_ge(v_mm, step.lin(1, 1))
                        if step.reg is not None or step.place >= 1:
                            act.wait_ge(att_mm, step.lin(1))
                        nc.scalar.activation(v[:], v_ps[0:NQ, 0:HE], ACT.Copy).then_inc(v_out, 1)

                run(act, body)

            @block.vector
            def _(dve):
                def body(step):
                    if step.on(1):
                        dve.wait_ge(sc_mm, step.lin(1))
                        nc.vector.scalar_tensor_tensor(masked[:], sc_ps[0:NQ, 0:NQ], HE ** -0.5, causal[:],
                                                       ALU.mult, ALU.add).then_inc(masked_ok, 1)
                        dve.wait_ge(masked_ok, step.lin(1))
                        nc.vector.tensor_reduce(nmax[:], masked[:], AX.X, ALU.max, negate=True)\
                          .then_inc(nmax_ok, 1)
                    if step.on(-1):
                        dve.wait_ge(xn_ok, step.lin(1, 2))
                        if step.reg is not None or step.place >= 0:
                            dve.wait_ge(T_full, T_use(step, 3) + 1)
                        nc.vector.tensor_tensor(
                            xs[:], xn[:].unsqueeze(1).to_broadcast([NQ, E, D]),
                            bc(rw[:, bass.ds(step.lin(1, 1), 1), :].rearrange("p o e -> p (o e)"), D), ALU.mult)\
                          .then_inc(xs_ok, 1)
                    if step.on(0):
                        dve.wait_ge(qk_mm, step.lin(1, 1))
                        nc.vector.tensor_copy(qT[:], qk_ps[0:HE, 0:NQ])
                        nc.vector.tensor_copy(kT[:], qk_ps[HE:2 * HE, 0:NQ]).then_inc(qk_out, 1)
                    if step.on(1):
                        dve.wait_ge(pr_ok, step.lin(1))
                        nc.vector.reciprocal(rden[:], den[:]).then_inc(rden_ok, 1)
                        dve.wait_ge(rden_ok, step.lin(1))
                        nc.vector.tensor_scalar(
                            rwd[:], rw[:, bass.ds(step.lin(1, -1), 1), :].rearrange("p o e -> p (o e)"),
                            rden[:, 0:1], None, ALU.mult).then_inc(rwd_ok, 1)
                    if step.on(1):
                        dve.wait_ge(rwd_ok, step.lin(1))
                        dve.wait_ge(att_mm, step.lin(1))
                        nc.vector.tensor_tensor(mixed[:], att_ps[0:NQ, 0:HE].unsqueeze(1).to_broadcast([NQ, E, HE]),
                                                bc(rwd[:], HE), ALU.mult).then_inc(mixed_ok, 1)
                    if step.on(2):
                        dve.wait_ge(out_mm, step.lin(1, -1))
                        xb = x_sb[:, bass.ds(step.lin(D, -2 * D), D)]
                        nc.vector.scalar_tensor_tensor(xb, out_ps[0:NQ, 0:D], tg[0:NQ, 2:3], xb, ALU.mult,
                                                       ALU.add).then_inc(x_ok, 1)
                        dve.wait_ge(x_ok, step.lin(1))
                        nc.vector.bn_stats(env["stat"][:, bass.ds(step.lin(1, -2), 1), :]
                                           .rearrange("p o s -> p (o s)"), xb)

                run(dve, body)
    sem.clear()


def rounded(ap):
    return ap.bitcast(F32R)


def products(nc, out, stationary, moving):
    terms = ((0, 1), (1, 0), (0, 0))
    for n, (a, b) in enumerate(terms):
        ins = nc.tensor.matmul(out, rounded(stationary[a]), rounded(moving[b]), start=(n == 0),
                               stop=(n == len(terms) - 1))
    return ins


def mixture_of_experts(nc, env, W, x_sb):
    gamma, beta, router, wgu, wdn, sgu, sdn = W
    E, F = 8, 512
    FC = F // P
    CHUNKS = [(E, 0)] + [(e, c) for e in range(E) for c in range(FC)]
    NC = len(CHUNKS)
    NB = 3
    BACK = 2
    assert NC % NB == 0
    ident, tg = env["ident"], env["tg"]
    NS = 4
    sem = Semaphores(nc, "m")
    st = ExitStack()
    with st:
        sb = lambda name, shape, dt=F32: st.enter_context(nc.sbuf_tensor(f"{name}_m", shape, dt))
        wdn_sb, sdn_sb = sb("wdn", [P, E, FC, D]), sb("sdn", [P, D])
        wgu_hi, wgu_lo = sb("wgu_hi", [D, E, 2 * F]), sb("wgu_lo", [D, E, 2 * F])
        sgu_hi, sgu_lo = sb("sgu_hi", [D, 2 * P]), sb("sgu_lo", [D, 2 * P])
        xT_hi, xT_lo, comb = sb("xT_hi", [D, TOK]), sb("xT_lo", [D, TOK]), sb("comb", [NQ, B, E])
        w_in, w_high, w_low = sem("w_in"), sem("w_high"), sem("w_low")
        stage_in = [sem(f"stage_in{n}_") for n in range(NS)]

        with ExitStack() as s1:
            sg_ = lambda name, shape, dt=F32: s1.enter_context(nc.sbuf_tensor(f"{name}_r", shape, dt))
            gb, rt = sg_("gb", [D, 2]), sg_("rt", [D, E])
            sgu_sb, stage = sg_("sgu", [D, 2 * P]), sg_("stage", [D, NS, 2 * F])
            SPLITS = [(sgu_sb[:], sgu_hi[:], sgu_lo[:])] + [
                (stage[:, e % NS, :], wgu_hi[:, e, :], wgu_lo[:, e, :]) for e in range(E)]
            h = sg_("h", [NQ, B * D])
            stat, mv, rstd, nmr = env["stat"], sg_("mv", [NQ, B, 2]), sg_("rstd", [NQ, B]), sg_("nmr", [NQ, B])
            stat2, mv2, rstd2, nmr2 = (sg_("stat2", [NQ, B, 6]), sg_("mv2", [NQ, B, 2]), sg_("rstd2", [NQ, B]),
                                       sg_("nmr2", [NQ, B]))
            xn, xg = sg_("xn", [NQ, 2, G, D]), sg_("xg", [D, 2, GT])
            L, L2, cand, f1, f2 = (sg_(n, [NQ, B, E]) for n in ("L", "L2", "cand", "f1", "f2"))
            mx = sg_("mx", [NQ, B])
            desc_i, desc = sg_("desc_i", [NQ, E], mybir.dt.int32), sg_("desc", [NQ, E])
            xnT_ps = s1.enter_context(nc.psum_tensor("xnT_ps_r", [P, 2, 512], F32))
            log_ps = s1.enter_context(nc.psum_tensor("log_ps_r", [P, 2, 512], F32))
            small_in, iota_ok = sem("small_in"), sem("iota_ok")
            ln1 = [sem(n) for n in ("stats", "var_ok", "std_ok", "rstd_ok")]
            ln2 = [sem(n) for n in ("stats2", "var_ok2", "std_ok2", "rstd_ok2")]
            h_ok, ln_ok, ln_T, ln_T_out, xT_ok, xT_low, logit_mm, logit_ok, pre_exp, gate_exp, chain = (
                sem(n) for n in ("h_ok", "ln_ok", "ln_T", "ln_T_out", "xT_ok", "xT_low", "logit_mm", "logit_ok",
                                 "pre_exp", "gate_exp", "chain"))

            with nc.Block() as block:
                @block.sync
                def _(sp):
                    for dst, src in ((gb[:, 0:1], gamma), (gb[:, 1:2], beta), (rt[:], router)):
                        sp.dma_start(dst, src).then_inc(small_in, 16)
                    sp.dma_start(sgu_sb[:], sgu).then_inc(small_in, 16)
                    for e in range(NS):
                        sp.dma_start(stage[:, e, :], wgu[e]).then_inc(stage_in[e], 16)
                    sp.dma_start(sdn_sb[:], sdn).then_inc(w_in, 16)
                    sp.dma_start(wdn_sb[:], wdn.rearrange("e (a f) c -> f e a c", a=FC)).then_inc(w_in, 16)
                    for e in range(NS, E):
                        sp.wait_ge(w_low, e - NS + 2)
                        sp.dma_start(stage[:, e % NS, :], wgu[e]).then_inc(stage_in[e % NS], 16)
                    sp.wait_ge(w_in, 32)

                @block.gpsimd
                def _(pool):
                    nc.gpsimd.iota(desc_i[:], [[-1, E]], base=E, channel_multiplier=0).then_inc(iota_ok, 1)
                    for n, (w, high, low) in enumerate(SPLITS):
                        pool.wait_ge(w_high, n + 1)
                        nc.gpsimd.tensor_tensor(rounded(low), w, high, ALU.subtract).then_inc(w_low, 1)

                @block.scalar
                def _(act):
                    def high_parts(first, last):
                        for n in range(first, last):
                            w, high, _ = SPLITS[n]
                            if n >= 1:
                                e = n - 1
                                act.wait_ge(stage_in[e % NS], 16 * (e // NS + 1))
                            nc.scalar.activation(rounded(high), w, ACT.Copy).then_inc(w_high, 1)

                    act.wait_ge(ln1[1], 1)
                    nc.scalar.activation(rstd[:], rstd[:], ACT.Sqrt).then_inc(ln1[2], 1)
                    act.wait_ge(ln1[3], 2)
                    with act.Fori(0, B // 4) as i:
                        for j in range(4):
                            at = bass.ds(i * (4 * D) + j * D, D)
                            nc.scalar.activation(h[:, at], x_sb[:, at], ACT.Identity,
                                                 bias=nmr[:, bass.ds(i * 4 + j, 1)],
                                                 scale=rstd[:, bass.ds(i * 4 + j, 1)]).then_inc(h_ok, 1)
                    act.wait_ge(small_in, 64)
                    high_parts(0, NS + 1)
                    act.wait_ge(ln2[1], 1)
                    nc.scalar.activation(rstd2[:], rstd2[:], ACT.Sqrt).then_inc(ln2[2], 1)
                    act.wait_ge(ln2[3], 2)

                    def normalise(n, u):
                        act.wait_ge(ln_T, n + 1)
                        for j in range(G):
                            nc.scalar.activation(xn[:, u, j, :], h[:, bass.ds(n * (G * D) + j * D, D)], ACT.Identity,
                                                 bias=nmr2[:, bass.ds(n * G + j, 1)],
                                                 scale=rstd2[:, bass.ds(n * G + j, 1)]).then_inc(ln_ok, 1)

                    def keep(n, u):
                        act.wait_ge(ln_T_out, n + 1)
                        nc.scalar.activation(rounded(xT_hi[:, bass.ds(n * GT, GT)]), xg[:, u, :], ACT.Copy)\
                          .then_inc(xT_ok, 1)

                    groups(act, normalise, keep)
                    high_parts(NS + 1, E + 1)
                    act.wait_ge(pre_exp, 1)
                    nc.scalar.activation(L[:], L[:], ACT.Exp).then_inc(gate_exp, 1)

                @block.tensor
                def _(pe):
                    pe.sem_inc(ln_T, 2)
                    pe.sem_inc(xT_low, 2)
                    pe.wait_ge(small_in, 64)

                    def transpose_group(n, u):
                        pe.wait_ge(ln_ok, n * G + G)
                        for j in range(G):
                            last = nc.tensor.transpose(xnT_ps[:, u, j * NQ:(j + 1) * NQ], xn[:, u, j, :],
                                                       ident[0:NQ, 0:NQ])
                        last.then_inc(ln_T, 1)

                    def logits(n, u):
                        pe.wait_ge(ln_T_out, n + 1)
                        for j in range(G):
                            last = nc.tensor.matmul(log_ps[0:NQ, u, j * E:(j + 1) * E],
                                                    xg[:, u, j * NQ:(j + 1) * NQ], rt[:], start=True, stop=True)
                        last.then_inc(logit_mm, 1)

                    groups(pe, transpose_group, logits)

                @block.vector
                def _(dve):
                    done = [0]

                    def link(ins):
                        done[0] += 1
                        ins.then_inc(chain, 1)
                        dve.wait_ge(chain, done[0])

                    dve.wait_ge(iota_ok, 1)
                    link(nc.vector.tensor_copy(desc[:], desc_i[:]))
                    layer_norm_scale(nc, dve, stat, mv, rstd, nmr, ln1, 0)
                    batch_stats(nc, dve, lambda off: h[:, bass.ds(off, D)], stat2, ln2[0], ready=h_ok)
                    layer_norm_scale(nc, dve, stat2, mv2, rstd2, nmr2, ln2, B)
                    dve.wait_ge(small_in, 64)
                    Lf = L[:].rearrange("p b e -> p (b e)")

                    def evac_transposes(n, u):
                        dve.wait_ge(ln_T, n + 3)
                        dve.wait_ge(xT_low, n + 1)
                        nc.vector.tensor_scalar(xg[:, u, :], xnT_ps[:, u, 0:GT], gb[:, 0:1], gb[:, 1:2],
                                                ALU.mult, ALU.add).then_inc(ln_T_out, 1)

                    def evac_logits(n, u):
                        dve.wait_ge(logit_mm, n + 1)
                        nc.vector.tensor_copy(Lf[:, bass.ds(n * (G * E), G * E)],
                                              log_ps[0:NQ, u, 0:G * E]).then_inc(logit_ok, 1)
                        dve.wait_ge(xT_ok, n + 1)
                        at = bass.ds(n * GT, GT)
                        nc.vector.tensor_tensor(rounded(xT_lo[:, at]), xg[:, u, :], xT_hi[:, at], ALU.subtract)\
                          .then_inc(xT_low, 1)

                    groups(dve, evac_transposes, evac_logits)
                    dve.wait_ge(logit_ok, NG)
                    link(nc.vector.tensor_reduce(mx[:], L[:], AX.X, ALU.max))
                    nc.vector.tensor_tensor(L[:], L[:], bc(mx[:], E), ALU.subtract).then_inc(pre_exp, 1)
                    dve.wait_ge(gate_exp, 1)
                    link(nc.vector.tensor_reduce(mx[:], L[:], AX.X, ALU.add))
                    link(nc.vector.reciprocal(mx[:], mx[:]))
                    link(nc.vector.tensor_tensor(L[:], L[:], bc(mx[:], E), ALU.mult))
                    link(nc.vector.tensor_reduce(mx[:], L[:], AX.X, ALU.max))
                    top_two(nc, link, L[:], L2[:], bm(desc[:], B), cand[:], f1[:], f2[:], mx[:], E)
                    link(nc.vector.tensor_tensor(L[:], L[:], f1[:], ALU.mult))
                    link(nc.vector.tensor_reduce(mx[:], L[:], AX.X, ALU.add))
                    link(nc.vector.reciprocal(mx[:], mx[:]))
                    link(nc.vector.tensor_tensor(comb[:], L[:], bc(mx[:], E), ALU.mult))

        clip, silu, hT = (sb(n, [P, NB, GT]) for n in ("clip", "silu", "hT"))
        acc = sb("acc", [NQ, 2, G, D])
        gate_ps = st.enter_context(nc.psum_tensor("gate_ps", [P, NB, 512], F32))
        up_ps = st.enter_context(nc.psum_tensor("up_ps", [P, NB, 512], F32))
        down_ps = st.enter_context(nc.psum_tensor("down_ps", [P, 2, 512], F32))
        gate_mm, clip_ok, silu_ok, h_ok2, down_mm, acc_ok, x_ok = (
            sem(n) for n in ("gate_mm", "clip_ok", "silu_ok", "h_ok2", "down_mm", "acc_ok", "x_ok"))
        EX = E + 1
        with nc.Block() as block:
            @block.tensor
            def _(pe):
                pe.sem_inc(h_ok2, NB)
                pe.sem_inc(acc_ok, 2)
                with pe.Fori(0, NG // 2) as i:
                    def gate_up(k):
                        u, (e, c) = k // NC, CHUNKS[k % NC]
                        pe.wait_ge(h_ok2, i * (2 * NC) + (k + 1))
                        hi, lo = (sgu_hi, sgu_lo) if e == E else (wgu_hi[:, e, :], wgu_lo[:, e, :])
                        f = P if e == E else F
                        at = bass.ds(i * (2 * GT) + u * GT, GT)
                        for ps, c0 in ((gate_ps, c * P), (up_ps, f + c * P)):
                            products(nc, ps[:, k % NB, 0:GT], (hi[:, c0:c0 + P], lo[:, c0:c0 + P]),
                                     (xT_hi[:, at], xT_lo[:, at])).then_inc(gate_mm, 1)

                    def down(k):
                        u, (e, c) = k // NC, CHUNKS[k % NC]
                        x = u * EX + (0 if e == E else e + 1)
                        last_c = 0 if e == E else FC - 1
                        if c == 0:
                            pe.wait_ge(acc_ok, i * (2 * EX) + (x + 1))
                        pe.wait_ge(h_ok2, i * (2 * NC) + (k + 1 + NB))
                        for j in range(G):
                            last = nc.tensor.matmul(down_ps[0:NQ, x % 2, j * D:(j + 1) * D],
                                                    hT[:, k % NB, j * NQ:(j + 1) * NQ],
                                                    sdn_sb[:] if e == E else wdn_sb[:, e, c, :],
                                                    start=(c == 0 and j == 0), stop=(c == last_c),
                                                    skip_group_check=True)
                        if c == last_c:
                            last.then_inc(down_mm, 1)

                    for k in range(2 * NC + BACK):
                        if k < 2 * NC:
                            gate_up(k)
                        if k >= BACK:
                            down(k - BACK)

            @block.scalar
            def _(act):
                with act.Fori(0, NG // 2) as i:
                    for k in range(2 * NC):
                        act.wait_ge(clip_ok, i * (2 * NC) + (k + 1))
                        nc.scalar.activation(silu[:, k % NB, :], clip[:, k % NB, :], ACT.Silu).then_inc(silu_ok, 1)

            @block.vector
            def _(dve):
                with dve.Fori(0, NG // 2) as i:
                    def clipped(k):
                        dve.wait_ge(gate_mm, i * (4 * NC) + (2 * k + 1))
                        nc.vector.tensor_scalar(clip[:, k % NB, :], gate_ps[:, k % NB, 0:GT], -10.0, 10.0, ALU.max,
                                                ALU.min).then_inc(clip_ok, 1)

                    def hidden(k):
                        dve.wait_ge(gate_mm, i * (4 * NC) + (2 * k + 2))
                        dve.wait_ge(silu_ok, i * (2 * NC) + (k + 1))
                        nc.vector.tensor_tensor(hT[:, k % NB, :], silu[:, k % NB, :], up_ps[:, k % NB, 0:GT],
                                                ALU.mult).then_inc(h_ok2, 1)

                    def accumulate(x):
                        u, e = x // EX, x % EX - 1
                        dve.wait_ge(down_mm, i * (2 * EX) + (x + 1))
                        if e < 0:
                            nc.vector.tensor_copy(acc[:, u].rearrange("p j d -> p (j d)"), down_ps[0:NQ, x % 2, :])\
                              .then_inc(acc_ok, 1)
                        else:
                            dve.wait_ge(acc_ok, i * (2 * EX) + (x + 2))
                            for j in range(G):
                                w = comb[:, bass.ds(i * (2 * G) + (u * G + j), 1), e]
                                last = nc.vector.scalar_tensor_tensor(
                                    acc[:, u, j, :], down_ps[0:NQ, x % 2, j * D:(j + 1) * D], w, acc[:, u, j, :],
                                    ALU.mult, ALU.add)
                            last.then_inc(acc_ok, 1)
                        if e == E - 1:
                            dve.wait_ge(acc_ok, i * (2 * EX) + (x + 3))
                            xb = x_sb[:, bass.ds(i * (2 * G * D) + u * (G * D), G * D)]
                            nc.vector.scalar_tensor_tensor(xb, acc[:, u].rearrange("p j d -> p (j d)"),
                                                           tg[0:NQ, 3:4], xb, ALU.mult, ALU.add).then_inc(x_ok, 1)

                    ends = {}
                    for x in range(2 * EX):
                        u, e = x // EX, x % EX - 1
                        ends[u * NC + (0 if e < 0 else 1 + e * FC + FC - 1)] = x
                    for k in range(2 * NC + BACK + 1):
                        if k < 2 * NC:
                            clipped(k)
                        if 1 <= k <= 2 * NC:
                            hidden(k - 1)
                        if k - BACK - 1 in ends:
                            accumulate(ends[k - BACK - 1])
    sem.clear()


def build(nc, x, ctxT, g_xattn, g_ffn, layers, out, ffn0=None, ffn1=None):
    ctx = ExitStack()
    with ctx:
        sb = lambda name, shape, dt=F32: ctx.enter_context(nc.sbuf_tensor(name, shape, dt))
        sem = lambda name: ctx.enter_context(nc.semaphore(name))
        env = {}
        x_sb = sb("x_sb", [NQ, B * D])
        env["stat"] = sb("stat", [NQ, B, 6])
        ident = env["ident"] = sb("ident", [P, P])
        gates = sb("gates", [P, 4])
        tg = env["tg"] = sb("tg", [P, 4])
        x_in, g_in, ident_ok, tanh_ok, packs_ok, ones_ok, ones_in = (
            sem(n) for n in ("x_in", "g_in", "ident_ok", "tanh_ok", "packs_ok", "ones_ok", "ones_in"))
        env["x_in"], env["ones_in"] = x_in, ones_in
        ones = sb("ones", [P, NK], BF16)
        kscr = nc.dram_tensor("kscr", (3, 3, P, NK), BF16).ap()
        qscr = nc.dram_tensor("qscr", (3, P, TOK), BF16).ap()
        mscr = nc.dram_tensor("mscr", (3, SH, H, NQ), BF16).ap()

        with ExitStack() as packs:
            env["Kp"] = packs.enter_context(nc.sbuf_tensor("Kp", [P, 3, PAIRS, NK], BF16))
            env["Qp"] = packs.enter_context(nc.sbuf_tensor("Qp", [P, 3, H * NQ], BF16))
            env["V"] = packs.enter_context(nc.sbuf_tensor("V", [P, 3, KT, H, HD + 1], F32))

            with nc.Block() as block:
                @block.sync
                def _(sp):
                    sp.dma_start(x_sb[:].rearrange("q (b d) -> q b d", b=B), x.rearrange("b q d -> q b d"))\
                      .then_inc(x_in, 16)
                    for i, g in enumerate((g_xattn, g_ffn)):
                        sp.dma_start(gates[:, 2 * i:2 * i + 2], g.partition_broadcast(P)).then_inc(g_in, 16)
                    sp.wait_ge(ones_ok, 1)
                    sp.dma_start(env["Kp"][ROWS:ROWS + SH].rearrange("p b g n -> p (b g) n"),
                                 ones[0:SH].unsqueeze(1).to_broadcast([SH, 3 * PAIRS, NK])).then_inc(ones_in, 16)

                @block.scalar
                def _(act):
                    act.wait_ge(g_in, 32)
                    nc.scalar.activation(tg[:], gates[:], ACT.Tanh).then_inc(tanh_ok, 1)

                @block.gpsimd
                def _(pool):
                    nc.gpsimd.memset(ident[:], 0.0).then_inc(ident_ok, 1)
                    pool.wait_ge(ident_ok, 1)
                    nc.gpsimd.affine_select(out=ident[:], in_=ident[:], compare_op=ALU.not_equal, fill=1.0, base=0,
                                            pattern=[[-1, P]], channel_multiplier=1).then_inc(ident_ok, 1)
                    nc.gpsimd.memset(env["V"][:, :, :, :, HD:HD + 1].rearrange("p b t h o -> p (b t h o)"), 1.0)\
                      .then_inc(packs_ok, 1)

                @block.vector
                def _(dve):
                    nc.vector.memset(ones[0:SH], 1.0).then_inc(ones_ok, 1)
                    nc.vector.memset(env["Qp"][:], 0.0).then_inc(packs_ok, 1)

            scr = (kscr, qscr, mscr)
            attention(nc, env, 0, (ctxT, *layers[0]), scr, x_sb)
            if ffn0:
                expert_attention(nc, env, ffn0, x_sb)
            if len(layers) > 1:
                attention(nc, env, 1, (ctxT, *layers[1]), scr, x_sb)

        if ffn1:
            mixture_of_experts(nc, env, ffn1, x_sb)
        out_done = sem("out_done")
        with nc.Block() as block:
            @block.sync
            def _(sp):
                sp.dma_start(out.rearrange("b q d -> q b d"), x_sb[:].rearrange("q (b d) -> q b d", b=B))\
                  .then_inc(out_done, 16)
                sp.wait_ge(out_done, 16)


def kernel(**inputs):
    import concourse.bacc as bacc
    from concourse.bass_utils import run_bass_kernel_spmd

    def paired(w):
        w = w.reshape(-1, PAIRS, 2, HD)
        return w.transpose(0, 2, 3, 1).reshape(w.shape[0], D)

    a = {name: np.asarray(v) for name, v in inputs.items()}
    kv_w, kv_b = a["L1_xattn_kv_w"], a["L1_xattn_kv_b"]
    laid = {
        "x": a["x"],
        "ctxT": a["ctx_768"].transpose(0, 2, 1).reshape(B * DC, NK),
        "g_xattn": a["g_xattn"], "g_ffn": a["g_ffn"],
    }
    for lay, (wq, bq, wk, bk, wv, bv, wo, bo) in enumerate((
            tuple(a[f"L0_xattn_{n}"] for n in ("Wq", "bq", "Wk", "bk", "Wv", "bv", "Wo", "bo")),
            (a["L1_xattn_q_w"], a["L1_xattn_q_b"], kv_w[:, :D], kv_b[:D], kv_w[:, D:], kv_b[D:],
             a["L1_xattn_proj_w"], a["L1_xattn_proj_b"]))):
        for name, v in (("wq", paired(wq)), ("bq", paired(bq).reshape(D, 1)), ("wk", paired(wk)),
                        ("bk", paired(bk).reshape(D, 1)), ("wv", wv), ("bv", bv), ("wo", wo), ("bo", bo)):
            laid[f"a{lay}_{name}"] = v
    laid["f0_sim"], laid["f0_gates"] = a["L0_ffn_sim_matrix"], a["L0_ffn_gates"]
    laid["f0_wqk"] = np.concatenate([a["L0_ffn_q_proj"], a["L0_ffn_k_proj"]], axis=-1).transpose(1, 0, 2)
    laid["f0_wv"] = a["L0_ffn_v_proj"].transpose(1, 0, 2)
    laid["f0_wo"] = a["L0_ffn_o_proj"].reshape(-1, P, D).transpose(1, 0, 2)
    laid["f1_gamma"], laid["f1_beta"] = a["L1_ffn_ln_gamma"].reshape(D, 1), a["L1_ffn_ln_beta"].reshape(D, 1)
    laid["f1_router"], laid["f1_wgu"], laid["f1_wdn"] = (
        a["L1_ffn_router_w"], a["L1_ffn_gate_up_w"], a["L1_ffn_down_w"])
    laid["f1_sgu"], laid["f1_sdn"] = a["L1_ffn_shared_gate_up_w"], a["L1_ffn_shared_down_w"]

    nc = bacc.Bacc("TRN2", target_bir_lowering=False, num_devices=1)
    arrays, ap = {}, {}
    for name, v in laid.items():
        v = np.ascontiguousarray(v)
        arrays[f"in_{name}"] = v
        ap[name] = nc.dram_tensor(f"in_{name}", v.shape, mybir.dt.from_np(v.dtype), kind="ExternalInput").ap()
    out = nc.dram_tensor("out_0", (B, NQ, D), F32, kind="ExternalOutput").ap()
    group = lambda p: [ap[n] for n in laid if n.startswith(p)]
    build(nc, ap["x"], ap["ctxT"], ap["g_xattn"], ap["g_ffn"], [group("a0_"), group("a1_")], out,
          group("f0_"), group("f1_"))
    return run_bass_kernel_spmd(nc, [arrays], core_ids=[0]).results[0]["out_0"]
```
